# Optimizing a Trainium2 kernel written in Bass

```python
import numpy as np
import jax
import jax.numpy as jnp

def _softmax(x, axis=-1):
    return jax.nn.softmax(x, axis=axis)

def _gelu(x):
    return jax.nn.gelu(x, approximate=True)

def _silu(x):
    return jax.nn.silu(x)

def _sigmoid(x):
    return jax.nn.sigmoid(x)

def _layernorm(x, axis=-1, eps=1e-05):
    m = jnp.mean(x, axis=axis, keepdims=True)
    v = jnp.var(x, axis=axis, keepdims=True)
    return (x - m) / jnp.sqrt(v + eps)

def _scatter_add(tgt, idx, src, axis=0):
    return tgt.at[idx].add(src)

def _segment_sum(src, seg, n):
    return jax.ops.segment_sum(src, seg, n)
kernel_name = 'mk_gnn_ffn_d2_gnn_r16_51acbf'

def setup_inputs(seed: int=0):
    np.random.seed(seed)
    _w = jnp.asarray

    def _rec_inputs():
        import jax
        import jax.numpy as jnp
        _gk = jax.random.key(seed)
        x = -0.0002117 + 1 * jax.random.normal(jax.random.fold_in(_gk, 1), (6250, 256), jnp.float32)
        src = jax.random.randint(jax.random.fold_in(_gk, 2), (100000,), 0, 6250, jnp.int32)
        dst = jax.random.randint(jax.random.fold_in(_gk, 3), (100000,), 0, 6250, jnp.int32)
        _o = jnp.argsort(dst, stable=True)
        src = src[_o]
        dst = dst[_o]
        edge_attr_8 = -0.00019784 + 0.999804 * jax.random.normal(jax.random.fold_in(_gk, 12), (100000, 8), jnp.float32)
        edge_type_8 = jax.random.randint(jax.random.fold_in(_gk, 14), (100000,), 0, 8, jnp.int32)
        return (x, src, dst, edge_attr_8, edge_type_8)
    x, src, dst, edge_attr_8, edge_type_8 = _rec_inputs()

    def _L0_gnn_setup():
        import jax, jax.numpy as jnp
        import numpy as np
        N = 6250
        E = 50000
        FEAT = 256
        HEADS = 8
        HEAD_DIM = FEAT // HEADS
        SCALING = HEAD_DIM ** (-0.5)
        key = jax.random.key(seed)
        ks = jax.random.split(key, 8)
        w_scale = (2.0 / (FEAT + FEAT)) ** 0.5
        return {'nfeat': jax.random.normal(ks[0], (N, FEAT), dtype=jnp.float32), 'attn_bias': jax.random.normal(ks[1], (E, HEADS), dtype=jnp.float32), 'Wq': jax.random.normal(ks[2], (FEAT, FEAT), dtype=jnp.float32) * w_scale, 'Wk': jax.random.normal(ks[3], (FEAT, FEAT), dtype=jnp.float32) * w_scale, 'Wv': jax.random.normal(ks[4], (FEAT, FEAT), dtype=jnp.float32) * w_scale, 'Wo': jax.random.normal(ks[5], (FEAT, FEAT), dtype=jnp.float32) * w_scale, 'src': jax.random.randint(ks[6], (E,), 0, N, dtype=jnp.int32), 'dst': jax.random.randint(ks[7], (E,), 0, N, dtype=jnp.int32)}
    _L0_gnn_all = _L0_gnn_setup()
    _L0_gnn_in = {k: v for k, v in _L0_gnn_all.items() if k in ('Wq', 'Wk', 'Wv', 'Wo')}
    del _L0_gnn_all

    def _L0_ffn_setup():
        import jax, jax.numpy as jnp
        import numpy as np
        C = 256
        HID = 1024
        E = 8
        TEMP = 1.0
        key = jax.random.key(seed)
        ks = jax.random.split(key, 7)
        x = jax.random.normal(ks[0], (8, 1024, C), dtype=jnp.float32)
        W1 = jax.random.normal(ks[1], (C, HID), dtype=jnp.float32) * 0.02
        b1 = jnp.zeros((HID,), dtype=jnp.float32)
        Wg = jax.random.normal(ks[2], (HID, E), dtype=jnp.float32) * 0.02
        bg = jnp.zeros((E,), dtype=jnp.float32)
        Wd = jax.random.normal(ks[3], (E, HID, C), dtype=jnp.float32) * 0.02
        bd = jnp.zeros((E, C), dtype=jnp.float32)
        return {'x': x, 'W1': W1, 'b1': b1, 'Wg': Wg, 'bg': bg, 'Wd': Wd, 'bd': bd}
    _L0_ffn_all = _L0_ffn_setup()
    _L0_ffn_in = {k: v for k, v in _L0_ffn_all.items() if k in ('W1', 'b1', 'Wg', 'bg', 'Wd', 'bd')}
    del _L0_ffn_all

    def _L1_gnn_setup():
        import jax, jax.numpy as jnp
        import numpy as np
        N, E, R, H, D = (1875, 18750, 8, 8, 32)
        IN_F = 256
        NEG_SLOPE = 0.2
        key = jax.random.key(seed)
        k = jax.random.split(key, 6)
        x = jax.random.normal(k[0], (N, IN_F), dtype=jnp.float32)
        W = jax.random.normal(k[1], (R, H * D, IN_F), dtype=jnp.float32) * 0.05
        attn_src = jax.random.normal(k[2], (H, D), dtype=jnp.float32) * 0.1
        attn_dst = jax.random.normal(k[3], (H, D), dtype=jnp.float32) * 0.1
        edge_index = jax.random.randint(k[4], (2, E), 0, N, dtype=jnp.int64) if jax.config.read('jax_enable_x64') else jax.random.randint(k[4], (2, E), 0, N, dtype=jnp.int32)
        edge_type = jax.random.randint(k[5], (E,), 0, R, dtype=edge_index.dtype)
        return dict(x=x, W=W, attn_src=attn_src, attn_dst=attn_dst, edge_index=edge_index, edge_type=edge_type)
    _L1_gnn_all = _L1_gnn_setup()
    _L1_gnn_in = {k: v for k, v in _L1_gnn_all.items() if k in ('W', 'attn_src', 'attn_dst')}
    del _L1_gnn_all

    def _L1_ffn_setup():
        import jax, jax.numpy as jnp
        import numpy as np
        NUM_EXPERTS = 8
        TOP_K = 2
        B, S, D = (8, 512, 256)

        def _moe(tokens, router_w, w1, b1, w2, b2):
            N = tokens.shape[0]
            E = router_w.shape[0]
            logits = tokens.astype(jnp.float32) @ router_w.astype(jnp.float32).T
            probs = jax.nn.softmax(logits, axis=-1)
            rw, re = jax.lax.top_k(probs, TOP_K)
            if TOP_K > 1:
                rw = rw / jnp.maximum(rw.sum(-1, keepdims=True), 1e-12)
            rw = rw.astype(tokens.dtype)
            combine = jnp.zeros((N, E), tokens.dtype).at[jnp.arange(N)[:, None], re].set(rw)
            out = tokens
            for e in range(E):
                h = jax.nn.gelu(tokens @ w1[e] + b1[e], approximate=False)
                y = h @ w2[e] + b2[e]
                out = out + combine[:, e:e + 1] * y
            return out
        key = jax.random.key(seed)
        ks = jax.random.split(key, 4)
        scale = 1.0 / np.sqrt(D).astype(np.float32)
        return {'input_embeddings': jax.random.normal(ks[0], (B, S, D), jnp.float32), 'router_w': jax.random.normal(ks[1], (NUM_EXPERTS, D), jnp.float32) * scale, 'w1': jax.random.normal(ks[2], (NUM_EXPERTS, D, D), jnp.float32) * scale, 'b1': jnp.zeros((NUM_EXPERTS, D), jnp.float32), 'w2': jax.random.normal(ks[3], (NUM_EXPERTS, D, D), jnp.float32) * scale, 'b2': jnp.zeros((NUM_EXPERTS, D), jnp.float32)}
    _L1_ffn_all = _L1_ffn_setup()
    _L1_ffn_in = {k: v for k, v in _L1_ffn_all.items() if k in ('router_w', 'w1', 'b1', 'w2', 'b2')}
    del _L1_ffn_all
    return {'x': x, 'src': src, 'dst': dst, 'edge_attr_8': edge_attr_8, 'edge_type_8': edge_type_8, 'L0_gnn_Wq': _L0_gnn_in['Wq'], 'L0_gnn_Wk': _L0_gnn_in['Wk'], 'L0_gnn_Wv': _L0_gnn_in['Wv'], 'L0_gnn_Wo': _L0_gnn_in['Wo'], 'L0_ffn_W1': _L0_ffn_in['W1'], 'L0_ffn_b1': _L0_ffn_in['b1'], 'L0_ffn_Wg': _L0_ffn_in['Wg'], 'L0_ffn_bg': _L0_ffn_in['bg'], 'L0_ffn_Wd': _L0_ffn_in['Wd'], 'L0_ffn_bd': _L0_ffn_in['bd'], 'L1_gnn_W': _L1_gnn_in['W'], 'L1_gnn_attn_src': _L1_gnn_in['attn_src'], 'L1_gnn_attn_dst': _L1_gnn_in['attn_dst'], 'L1_ffn_router_w': _L1_ffn_in['router_w'], 'L1_ffn_w1': _L1_ffn_in['w1'], 'L1_ffn_b1': _L1_ffn_in['b1'], 'L1_ffn_w2': _L1_ffn_in['w2'], 'L1_ffn_b2': _L1_ffn_in['b2']}

def reference(x, src, dst, edge_attr_8, edge_type_8, L0_gnn_Wq, L0_gnn_Wk, L0_gnn_Wv, L0_gnn_Wo, L0_ffn_W1, L0_ffn_b1, L0_ffn_Wg, L0_ffn_bg, L0_ffn_Wd, L0_ffn_bd, L1_gnn_W, L1_gnn_attn_src, L1_gnn_attn_dst, L1_ffn_router_w, L1_ffn_w1, L1_ffn_b1, L1_ffn_w2, L1_ffn_b2):
    import jax
    import jax.numpy as jnp

    def _L0_gnn_ref(nfeat, attn_bias, Wq, Wk, Wv, Wo, src, dst):
        import jax, jax.numpy as jnp
        import numpy as np
        N = 6250
        E = 50000
        FEAT = 256
        HEADS = 8
        HEAD_DIM = FEAT // HEADS
        SCALING = HEAD_DIM ** (-0.5)
        n = nfeat.shape[0]
        q = (nfeat @ Wq.T).reshape(n, HEADS, HEAD_DIM) / SCALING
        k = (nfeat @ Wk.T).reshape(n, HEADS, HEAD_DIM)
        v = (nfeat @ Wv.T).reshape(n, HEADS, HEAD_DIM)
        attn = jnp.einsum('ehd,ehd->eh', k[src], q[dst])
        attn = attn + attn_bias
        m = jax.ops.segment_max(attn, dst, num_segments=n)
        a = jnp.exp(attn - m[dst])
        s = jax.ops.segment_sum(a, dst, num_segments=n)
        a = a / s[dst]
        out = jax.ops.segment_sum(v[src] * a[:, :, None], dst, num_segments=n)
        return out.reshape(n, FEAT) @ Wo.T

    def _L0_ffn_ref(x, W1, b1, Wg, bg, Wd, bd):
        import jax, jax.numpy as jnp
        import numpy as np
        C = 256
        HID = 1024
        E = 8
        TEMP = 1.0
        orig_shape = x.shape
        xf = x.reshape(-1, orig_shape[-1])
        H = jax.nn.gelu(xf @ W1 + b1, approximate=False)
        probs = jax.nn.softmax((H @ Wg + bg) / TEMP, axis=-1)
        assign = jnp.argmax(probs, axis=-1)
        out = jnp.zeros_like(xf)
        for e in range(Wd.shape[0]):
            y = H @ Wd[e] + bd[e]
            sel = (assign == e)[:, None]
            out = out + jnp.where(sel, probs[:, e:e + 1] * y, 0.0)
        return out.reshape(orig_shape)

    def _L1_gnn_ref(x, W, attn_src, attn_dst, edge_index, edge_type):
        import jax, jax.numpy as jnp
        import numpy as np
        N, E, R, H, D = (1875, 18750, 8, 8, 32)
        IN_F = 256
        NEG_SLOPE = 0.2
        n = x.shape[0]
        r = W.shape[0]
        h, d = attn_src.shape
        h_all = jnp.einsum('nf,rof->rno', x, W).reshape(r, n, h, d)
        src, dst = (edge_index[0], edge_index[1])
        h_src = h_all[edge_type, src]
        h_dst = h_all[edge_type, dst]
        scores = jnp.einsum('ehd,hd->eh', h_src, attn_src) + jnp.einsum('ehd,hd->eh', h_dst, attn_dst)
        scores = jnp.where(scores > 0, scores, NEG_SLOPE * scores)
        amax = jnp.maximum(jax.ops.segment_max(scores, dst, num_segments=n), 0.0)
        w = jnp.exp(scores - amax[dst])
        denom = jax.ops.segment_sum(w, dst, num_segments=n) + 1e-12
        w = w / denom[dst]
        msg = h_src * w[..., None]
        out = jax.ops.segment_sum(msg, dst, num_segments=n)
        return out.reshape(n, h * d)

    def _L1_ffn_ref(input_embeddings, router_w, w1, b1, w2, b2):
        import jax, jax.numpy as jnp
        import numpy as np
        NUM_EXPERTS = 8
        TOP_K = 2
        B, S, D = (8, 512, 256)

        def _moe(tokens, router_w, w1, b1, w2, b2):
            N = tokens.shape[0]
            E = router_w.shape[0]
            logits = tokens.astype(jnp.float32) @ router_w.astype(jnp.float32).T
            probs = jax.nn.softmax(logits, axis=-1)
            rw, re = jax.lax.top_k(probs, TOP_K)
            if TOP_K > 1:
                rw = rw / jnp.maximum(rw.sum(-1, keepdims=True), 1e-12)
            rw = rw.astype(tokens.dtype)
            combine = jnp.zeros((N, E), tokens.dtype).at[jnp.arange(N)[:, None], re].set(rw)
            out = tokens
            for e in range(E):
                h = jax.nn.gelu(tokens @ w1[e] + b1[e], approximate=False)
                y = h @ w2[e] + b2[e]
                out = out + combine[:, e:e + 1] * y
            return out
        b, s, d = input_embeddings.shape
        tokens = input_embeddings.reshape(b * s, d)
        return _moe(tokens, router_w, w1, b1, w2, b2).reshape(b, s, d)
    edge_index = jnp.stack([src, dst])
    x = x + _L0_gnn_ref(_layernorm(x, axis=-1), edge_attr_8, L0_gnn_Wq, L0_gnn_Wk, L0_gnn_Wv, L0_gnn_Wo, src, dst)
    x = x + _L0_ffn_ref(_layernorm(x, axis=-1)[None], L0_ffn_W1, L0_ffn_b1, L0_ffn_Wg, L0_ffn_bg, L0_ffn_Wd, L0_ffn_bd)[0]
    x = x + _L1_gnn_ref(_layernorm(x, axis=-1), L1_gnn_W, L1_gnn_attn_src, L1_gnn_attn_dst, edge_index, edge_type_8)
    x = x + _L1_ffn_ref(_layernorm(x, axis=-1)[None], L1_ffn_router_w, L1_ffn_w1, L1_ffn_b1, L1_ffn_w2, L1_ffn_b2)[0]
    return x

_drawn_inputs = setup_inputs


def setup_inputs(seed=0):
    import zlib

    import numpy as np

    out = dict(_drawn_inputs(seed))
    spreads = {'L0_ffn_b1': (0.0, 0.457),
     'L0_ffn_bg': (0.0, 0.376),
     'L0_ffn_bd': (0.0, 0.426),
     'L1_ffn_b1': (0.0, 0.376),
     'L1_ffn_b2': (0.0, 0.1)}
    factors = {'L0_ffn_Wg': 2.697, 'L0_ffn_Wd': 2.888}
    for name, (base, spread) in spreads.items():
        noise = np.random.default_rng([zlib.crc32(name.encode()), seed]).standard_normal(out[name].shape)
        drawn = base * np.exp(spread * noise) if base else spread * noise
        out[name] = jnp.asarray(drawn.astype(out[name].dtype))
    for name, factor in factors.items():
        out[name] = (out[name] * factor).astype(out[name].dtype)
    return out
```

```python
from contextlib import ExitStack

import concourse.bass as bass
from concourse import mybir

ALU = mybir.AluOpType
ACT = mybir.ActivationFunctionType
AX = mybir.AxisListType
F32 = mybir.dt.float32
BF16 = mybir.dt.bfloat16
I32 = mybir.dt.int32
U32 = mybir.dt.uint32

P = 128
N, FEAT, HEADS = 6250, 256, 8
DH = FEAT // HEADS
E = 100000
RELS = 8
EXPERTS = 8
HID = 1024
BLOCKS = 50
NPAD = BLOCKS * P
LAST_BLOCK = (N - 1) // P
PAD_NODE = LAST_BLOCK * P + P - 1
TILES = -(-E // P)
TROWS = TILES + 1
IT = 16
CHUNKS = 16
STEPS = -(-(TILES + LAST_BLOCK) // IT) * IT
ITS = STEPS // IT
SPAD = STEPS + IT
CS = SPAD // CHUNKS
SGROUPS = -(-SPAD // P)
CLEN = CS * P
assert CS * CHUNKS == SPAD
BIG = 1e30
SORTED = (NPAD + EXPERTS * (P - 1)) // P
SORTED += SORTED % 2
QSCALE = float(DH) ** 0.5
LN_EPS = 1e-5
NUMC = FEAT + HEADS


class Shared:
    pass


def new_sem(nc, m, name):
    m.phase_sems.append(nc.alloc_semaphore(name=name))
    return m.phase_sems[-1]


def end_phase(nc, m):
    nc.clear_and_free_semaphores(m.phase_sems)
    m.phase_sems = []
    nc.all_engine_barrier()


def sems(nc, m, prefix, names):
    return {n: new_sem(nc, m, f"{prefix}_{n}") for n in names.split()}


def hold(eng, m):
    eng.sem_inc(m.passed, 1)


class Link:

    def __init__(self, eng, sem):
        self.eng, self.sem, self.n = eng, sem, 0

    def __call__(self, ins):
        self.n += 1
        ins.then_inc(self.sem, 1)
        self.eng.wait_ge(self.sem, self.n)


def constants(nc, m):
    with ExitStack() as ctx:
        s = sems(nc, m, "const", "raw pool link")
        tmp = ctx.enter_context(nc.sbuf_tensor("const_i", [P, 128], I32))
        hm = ctx.enter_context(nc.sbuf_tensor("const_h", [P, 16], I32))
        hf = ctx.enter_context(nc.sbuf_tensor("const_hf", [P, 16], F32))
        block = ctx.enter_context(nc.Block())

        @block.gpsimd
        def _(pool):
            link = Link(pool, s["pool"])
            link(pool.memset(m.ident[:, :], 0.0))
            link(pool.affine_select(out=m.ident[:, :], in_=m.ident[:, :], compare_op=ALU.not_equal, fill=1.0,
                                    base=0, pattern=[[-1, 128]], channel_multiplier=1))
            pool.iota(tmp[:, :], pattern=[[1, 128]], base=0, channel_multiplier=0).then_inc(s["raw"], 1)
            pool.iota(hm[:, :], pattern=[[128, 2], [-DH, 8]], base=0, channel_multiplier=1).then_inc(s["raw"], 1)
            pool.memset(m.e_const[:, :], 2.718281828459045)
            pool.memset(m.mhalf[:, :], -0.5)
            link(pool.memset(m.ones_row[:, :], 1.0))

        @block.vector
        def _(dve):
            link = Link(dve, s["link"])
            dve.wait_ge(s["raw"], 2)
            dve.wait_ge(s["pool"], 2)
            dve.tensor_copy(m.iota_f[:, :], tmp[:, :])
            dve.tensor_copy(m.ident_b[:, :], m.ident[:, :])
            link(dve.tensor_copy(hf[:, :], hm[:, :]))
            link(dve.tensor_scalar(m.hmask[:, :], hf[:, :], -0.5, None, ALU.is_gt))
            link(dve.tensor_scalar(hf[:, :], hf[:, :], DH - 0.5, None, ALU.is_lt))
            link(dve.tensor_tensor(m.hmask[:, :], m.hmask[:, :], hf[:, :], ALU.mult))


def merge_path(nc, m, d):
    with ExitStack() as ctx:
        s = sems(nc, m, "path", "load pool link rows psb jt jtc jout g0 g1 g2 gt gc sent end")
        sb = lambda n, sh, dt: ctx.enter_context(nc.sbuf_tensor(f"path_{n}", sh, dt))
        last_i = sb("last_i", [1, TILES], I32)
        last_f = sb("last_f", [1, TILES], F32)
        tile_i = sb("tile_i", [1, TILES], I32)
        tile_f = sb("tile_f", [1, TILES], F32)
        step_i = sb("step_i", [P, SGROUPS], I32)
        step_f = sb("step_f", [P, SGROUPS], F32)
        ends = sb("ends", [P, TILES], F32)
        less = sb("less", [P, TILES], F32)
        tsel = sb("tsel", [P, SGROUPS], F32)
        bsel = sb("bsel", [P, SGROUPS], F32)
        tsel_i = m.tile_of_step
        jt = sb("jt", [SGROUPS, P], F32)
        jti = sb("jti", [SGROUPS, P], I32)
        sent = sb("sent", [1, 2], I32)
        raw = [sb(f"raw{i}", [P, SGROUPS, P], I32) for i in range(3)]
        rawf = [sb(f"rawf{i}", [P, SGROUPS, P], F32) for i in range(3)]
        pend = ctx.enter_context(nc.psum_tensor("path_pend", [P, 2, 512], F32))
        pjt = ctx.enter_context(nc.psum_tensor("path_pjt", [SGROUPS, P], F32))
        half = TILES // 2
        tables = (d["src"], d["dst"], d["typ"])
        path = ctx.enter_context(ExitStack())
        block = path.enter_context(nc.Block())

        @block.sync
        def _(sp):
            with nc.allow_non_contiguous_dma(reason="one column of the tiles' destinations"):
                sp.dma_start(last_i[:, :], d["dst"][0:TILES, P - 1:P].rearrange("t o -> o t")).then_inc(s["load"], 16)
            sp.wait_ge(s["jtc"], 1)
            sp.dma_start(d["jf"][:, :], jt[:, :]).then_inc(s["jout"], 16)
            sp.dma_start(d["ji"][:, :], jti[:, :]).then_inc(s["jout"], 16)
            sp.wait_ge(s["g1"], 16 * SGROUPS)
            sp.wait_ge(s["sent"], 1)
            for k in range(SGROUPS):
                rows = min(P, SPAD - k * P)
                sp.dma_start(d["dst_steps"][0:1, 1 + k * P * P:1 + (k * P + rows) * P].rearrange(
                    "o (p e) -> (o p) e", e=P), raw[1][0:rows, k, :]).then_inc(s["end"], 16)
            sp.dma_start(d["dst_steps"][0:1, 0:1], sent[0:1, 0:1]).then_inc(s["end"], 16)
            sp.dma_start(d["dst_steps"][0:1, 1 + SPAD * P:2 + SPAD * P], sent[0:1, 1:2]).then_inc(s["end"], 16)
            sp.wait_ge(s["jout"], 32)
            sp.dma_start(m.jrow[0:1, :], d["ji"].rearrange("k p -> (k p)")[0:SPAD].rearrange("(o s) -> o s", o=1)).then_inc(s["end"], 16)
            sp.dma_start(m.jb[:, :], d["jf"].rearrange("k p -> (k p)")[0:SPAD].rearrange("(o s) -> o s", o=1).to_broadcast([P, SPAD])).then_inc(s["end"], 16)
            sp.wait_ge(s["end"], 16 * (SGROUPS + 4))

        @block.gpsimd
        def _(pool):
            pool.iota(tile_i[:, :], pattern=[[1, TILES]], base=0, channel_multiplier=0).then_inc(s["pool"], 1)
            pool.iota(step_i[:, :], pattern=[[P, SGROUPS]], base=0, channel_multiplier=1).then_inc(s["pool"], 1)
            pool.wait_ge(s["rows"], 1)
            for t, table in enumerate(tables):
                for k in range(SGROUPS):
                    pool.indirect_dma_start(
                        out=raw[t][:, k, :], out_offset=None, in_=table[:, :],
                        in_offset=bass.IndirectOffsetOnAxis(ap=tsel_i[:, k:k + 1], axis=0)).then_inc((s["g0"], s["g1"], s["g2"])[t], 16)

        @block.vector
        def _(dve):
            link = Link(dve, s["link"])
            dve.memset(sent[0:1, 0:1], -1)
            dve.memset(sent[0:1, 1:2], 1 << 20).then_inc(s["sent"], 1)
            dve.wait_ge(s["load"], 16)
            dve.wait_ge(s["pool"], 2)
            link(dve.tensor_scalar(last_i[:, :], last_i[:, :], 7, None, ALU.arith_shift_right))
            link(dve.tensor_copy(last_f[:, :], last_i[:, :]))
            link(dve.tensor_copy(tile_f[:, :], tile_i[:, :]))
            link(dve.tensor_copy(step_f[:, :], step_i[:, :]))
            dve.tensor_tensor(last_f[:, :], last_f[:, :], tile_f[:, :], ALU.add).then_inc(s["psb"], 1)
            dve.wait_ge(s["psb"], 2)
            for c in range(2):
                link(dve.tensor_copy(ends[:, c * half:(c + 1) * half], pend[:, c, 0:half]))
            for k in range(SGROUPS):
                link(dve.tensor_scalar(less[:, :], ends[:, :], step_f[:, k:k + 1], 0.0, ALU.is_lt, ALU.add,
                                       accum_out=tsel[:, k:k + 1]))
            link(dve.tensor_tensor(bsel[:, :], step_f[:, :], tsel[:, :], ALU.subtract))
            link(dve.tensor_scalar(bsel[:, :], bsel[:, :], float(LAST_BLOCK), None, ALU.min))
            dve.tensor_copy(tsel_i[:, :], tsel[:, :]).then_inc(s["rows"], 1)
            dve.wait_ge(s["jt"], 1)
            link(dve.tensor_copy(jt[:, :], pjt[:, :]))
            dve.tensor_copy(jti[:, :], jt[:, :]).then_inc(s["jtc"], 1)
            for t, g in enumerate((s["g0"], s["g1"], s["g2"])):
                dve.wait_ge(g, 16 * SGROUPS)
                link(dve.tensor_copy(rawf[t][:, :, :], raw[t][:, :, :]))

        @block.tensor
        def _(pe):
            pe.wait_ge(s["psb"], 1)
            for c in range(2):
                mm = pe.matmul(pend[:, c, 0:half], m.ones_row[0:1, :], last_f[0:1, c * half:(c + 1) * half],
                               start=True, stop=True)
            mm.then_inc(s["psb"], 1)
            pe.wait_ge(s["rows"], 1)
            pe.transpose(pjt[:, :], bsel[:, :], m.ident[:, :]).then_inc(s["jt"], 1)

        path.close()

        ctx2 = ctx.enter_context(ExitStack())
        t = sems(nc, m, "turn", "tp tc link dve")
        pt = [ctx2.enter_context(nc.psum_tensor(f"turn_p{i}", [P, 512], F32)) for i in range(4)]
        typf = ctx2.enter_context(nc.sbuf_tensor("turn_typ", [P, SGROUPS * P], F32))
        srcf = ctx2.enter_context(nc.sbuf_tensor("turn_src", [P, SGROUPS * P], F32))
        dstf = ctx2.enter_context(nc.sbuf_tensor("turn_dst", [P, SGROUPS * P], F32))
        block2 = ctx2.enter_context(nc.Block())
        outs = (srcf, dstf, typf)

        @block2.tensor
        def _(pe):
            for i in range(3 * SGROUPS):
                if i >= 4:
                    pe.wait_ge(t["tc"], i - 3)
                pe.transpose(pt[i % 4][:, 0:P], rawf[i // SGROUPS][:, i % SGROUPS, :], m.ident[:, :]).then_inc(t["tp"], 1)

        @block2.vector
        def _(dve):
            for i in range(3 * SGROUPS):
                dve.wait_ge(t["tp"], i + 1)
                k = i % SGROUPS
                dve.tensor_copy(outs[i // SGROUPS][:, k * P:(k + 1) * P], pt[i % 4][:, 0:P]).then_inc(t["tc"], 1)
            dve.wait_ge(t["tc"], 3 * SGROUPS)
            link = Link(dve, t["link"])
            dve.tensor_copy(m.idx_src[:, :], srcf[:, 0:SPAD])
            link(dve.scalar_tensor_tensor(srcf[:, 0:SPAD], srcf[:, 0:SPAD], float(RELS), typf[:, 0:SPAD], ALU.mult, ALU.add))
            dve.tensor_copy(m.idx_rel[:, :], srcf[:, 0:SPAD])
            link(dve.scalar_tensor_tensor(m.dst_in[:, :], m.jb[:, :], -float(P), dstf[:, 0:SPAD], ALU.mult, ALU.add))
            link(dve.tensor_scalar(m.outside[:, :], m.dst_in[:, :], -0.5, -BIG, ALU.is_lt, ALU.mult))
            link(dve.tensor_scalar(dstf[:, 0:SPAD], m.dst_in[:, :], P - 0.5, -BIG, ALU.is_gt, ALU.mult))
            link(dve.tensor_tensor(m.outside[:, :], m.outside[:, :], dstf[:, 0:SPAD], ALU.add))
            tm = m.relmask[:, :].rearrange("p (s r) -> p s r", r=RELS)
            for r in range(RELS):
                link(dve.tensor_scalar(tm[:, :, r], typf[:, 0:SPAD], float(r), None, ALU.is_equal))


def segment_starts(nc, m, d):
    with ExitStack() as ctx:
        s = sems(nc, m, "starts", "load link")
        ids = ctx.enter_context(nc.sbuf_tensor("starts_ids", [P, CLEN + 2], I32))
        edge = ctx.enter_context(nc.sbuf_tensor("starts_edge", [1, 3, CHUNKS], I32))
        edgef = ctx.enter_context(nc.sbuf_tensor("starts_edgef", [1, 2, CHUNKS], F32))
        flat = d["dst_steps"].rearrange("o n -> (o n)")
        with nc.Block() as block:

            @block.sync
            def _(sp):
                chunks = flat[0:CHUNKS * CLEN].rearrange("(c n) -> c n", c=CHUNKS)
                after = flat[CLEN:(CHUNKS + 1) * CLEN].rearrange("(c n) -> c n", c=CHUNKS)[:, 0:2]
                for h in range(HEADS):
                    rows = slice(h * CHUNKS, (h + 1) * CHUNKS)
                    sp.dma_start(ids[rows, 0:CLEN], chunks).then_inc(s["load"], 16)
                    sp.dma_start(ids[rows, CLEN:CLEN + 2], after).then_inc(s["load"], 16)
                with nc.allow_non_contiguous_dma(reason="one destination per chunk"):
                    for i, first in enumerate((0, 1, CLEN)):
                        sp.dma_start(edge[0:1, i, :], flat[first:first + (CHUNKS - 1) * CLEN + 1:CLEN].rearrange(
                            "(o n) -> o n", o=1)).then_inc(s["load"], 16)
                sp.wait_ge(s["load"], 16 * (2 * HEADS + 3))

            @block.vector
            def _(dve):
                link = Link(dve, s["link"])
                dve.wait_ge(s["load"], 16 * (2 * HEADS + 3))
                link(dve.tensor_tensor(m.starts[:, :], ids[:, 1:CLEN + 2], ids[:, 0:CLEN + 1], ALU.not_equal))
                link(dve.tensor_scalar(m.starts[:, :], m.starts[:, :], -BIG, None, ALU.mult))
                link(dve.tensor_tensor(edgef[:, 0, :], edge[:, 0, :], edge[:, 2, :], ALU.not_equal))
                link(dve.memset(edgef[:, 1, :], 1.0))
                link(dve.tensor_tensor(edgef[:, 1, 0:CHUNKS - 1], edge[:, 1, 0:CHUNKS - 1], edge[:, 1, 1:CHUNKS],
                                       ALU.not_equal))
                for i, chain in enumerate((m.chain_fwd, m.chain_bwd)):
                    for h in range(HEADS):
                        link(dve.tensor_scalar(chain[:, h * CHUNKS:(h + 1) * CHUNKS], edgef[:, i, :], -BIG, None, ALU.mult))


def by_head(S):
    return S[:, :].rearrange("p (h s) -> p h s", h=HEADS)


def edge_bias(nc, m, d, S):
    with ExitStack() as ctx:
        s = sems(nc, m, "bias", "pool load link tsel g0 g1 tp tc")
        rows = ctx.enter_context(nc.sbuf_tensor("bias_rows", [P, 2, P * HEADS], F32))
        pt = [ctx.enter_context(nc.psum_tensor(f"bias_p{i}", [P, 4, P], F32)) for i in range(4)]
        Sv = by_head(S)
        n_groups = 2 * SGROUPS
        with nc.Block() as block:

            @block.gpsimd
            def _(pool):
                for k in range(SGROUPS):
                    if k >= 2:
                        pool.wait_ge(s["tp"], 2 * (k - 1))
                    pool.indirect_dma_start(out=rows[:, k % 2, :], out_offset=None, in_=d["attr"][:, :],
                                            in_offset=bass.IndirectOffsetOnAxis(ap=m.tile_of_step[:, k:k + 1], axis=0)
                                            ).then_inc((s["g0"], s["g1"])[k % 2], 16)

            @block.vector
            def _(dve):
                for g in range(n_groups):
                    k, hh = g // 2, g % 2
                    cols = min(P, SPAD - k * P)
                    dve.wait_ge(s["tp"], g + 1)
                    dve.tensor_tensor(Sv[:, 4 * hh:4 * hh + 4, k * P:k * P + cols], pt[g % 4][:, :, 0:cols],
                                      m.outside[:, k * P:k * P + cols].unsqueeze(1).to_broadcast([P, 4, cols]),
                                      ALU.add).then_inc(s["tc"], 1)

            @block.tensor
            def _(pe):
                for g in range(n_groups):
                    k, hh = g // 2, g % 2
                    pe.wait_ge((s["g0"], s["g1"])[k % 2], 16 * (k // 2 + 1))
                    if g >= 4:
                        pe.wait_ge(s["tc"], g - 3)
                    for h in range(4):
                        mm = pe.transpose(pt[g % 4][:, h, :],
                                          rows[:, k % 2, :].rearrange("p (e h) -> p e h", h=HEADS)[:, :, 4 * hh + h],
                                          m.ident[:, :])
                    mm.then_inc(s["tp"], 1)


def shared(nc, ctx, m):
    sb = lambda n, sh, dt: ctx.enter_context(nc.sbuf_tensor(n, sh, dt))
    m.phase_sems = []
    m.passed = ctx.enter_context(nc.semaphore("passed"))
    m.ident = sb("ident", [P, P], F32)
    m.ident_b = sb("ident_b", [P, P], BF16)
    m.iota_f = sb("iota_f", [P, P], F32)
    m.ones_row = sb("ones_row", [1, P], F32)
    m.e_const = sb("e_const", [P, HEADS], F32)
    m.mhalf = sb("mhalf", [P, 1], F32)
    m.hmask = sb("hmask", [P, 16], F32)
    m.tile_of_step = sb("tile_of_step", [P, SGROUPS], I32)
    m.jrow = sb("jrow", [1, SPAD], I32)
    m.jb = sb("jb", [P, SPAD], F32)
    m.idx_src = sb("idx_src", [P, SPAD], I32)
    m.idx_rel = sb("idx_rel", [P, SPAD], I32)
    m.dst_in = sb("dst_in", [P, SPAD], F32)
    m.outside = sb("outside", [P, SPAD], F32)
    m.relmask = sb("relmask", [P, SPAD * RELS], BF16)
    m.starts = sb("starts", [P, CLEN + 1], BF16)
    m.chain_fwd = sb("chain_fwd", [1, P], F32)
    m.chain_bwd = sb("chain_bwd", [1, P], F32)


def stage_halves(act, stage, idx, staged, gathered, it):
    for h in range(2):
        for slot in gathered[h]:
            act.wait_ge(slot[0], it * slot[1] + slot[2])
        act.copy(stage[:, 8 * h:8 * h + 8], idx[:, bass.ds(it * IT + (IT + 8 * h), 8)]).then_inc(staged, 1)


def scores_attention(nc, m, d, S):
    PAIRS = IT // 2
    with ExitStack() as ctx:
        s = sems(nc, m, "dot", "staged pair_used masks turned turned_sb q_rows summed added")
        k_in = [new_sem(nc, m, f"dot_k_in{i}") for i in range(8)]
        sb = lambda nm, sh, dt: ctx.enter_context(nc.sbuf_tensor(f"dot_{nm}", sh, dt))
        K = sb("K", [P, 8, FEAT], F32)
        stage = sb("stage", [P, IT], I32)
        OH = sb("OH", [P, IT, P], BF16)
        OHT = sb("OHT", [P, IT, P], F32)
        prod = sb("prod", [P, 2, 2 * FEAT], F32)
        ST = sb("ST", [P, IT * HEADS], F32)
        TP = [ctx.enter_context(nc.psum_tensor(f"dot_TP{i}", [P, 1024], BF16)) for i in range(2)]
        QP = [ctx.enter_context(nc.psum_tensor(f"dot_QP{i}", [P, 2 * FEAT], F32)) for i in range(4)]

        with nc.Block() as block:

            @block.gpsimd
            def _(pool):
                with pool.Fori(0, ITS) as it:
                    for u in range(IT):
                        if u % 8 == 0:
                            pool.wait_ge(s["staged"], it * 2 + (u // 8 + 1))
                        if u % 2 == 0:
                            pool.wait_ge(s["pair_used"], it * PAIRS + (u // 2 + 1))
                        if u % 2 == 0:
                            hold(pool, m)
                        pool.indirect_dma_start(out=K[:, u % 8, :], out_offset=None, in_=d["k_tab"][:, :],
                                                in_offset=bass.IndirectOffsetOnAxis(ap=stage[:, u:u + 1], axis=0)
                                                ).then_inc(k_in[u % 8], 16)

            @block.scalar
            def _(act):
                def to_sbuf(quad, slot):
                    act.wait_ge(s["turned"], quad + 1)
                    act.copy(OHT[:, 4 * slot:4 * slot + 4, :].rearrange("p a b -> p (a b)"),
                             TP[slot % 2][:, 0:512]).then_inc(s["turned_sb"], 1)

                for h in range(2):
                    act.copy(stage[:, 8 * h:8 * h + 8], m.idx_src[:, 8 * h:8 * h + 8]).then_inc(s["staged"], 1)
                for q in range(4):
                    to_sbuf(q, q)
                with act.Fori(0, ITS) as it:
                    for q in range(4):
                        act.wait_ge(s["q_rows"], it * PAIRS + (2 * q + 2))
                        to_sbuf(it * 4 + (4 + q), q)
                    stage_halves(act, stage, m.idx_src, s["staged"],
                                 [[(k, 32, 16) for k in k_in], [(k, 32, 32) for k in k_in]], it)

            @block.tensor
            def _(pe):
                def turn(quad, slot):
                    pe.wait_ge(s["masks"], quad + 1)
                    for i in range(4):
                        mm = pe.transpose(TP[slot % 2][:, i * P:(i + 1) * P], OH[:, 4 * slot + i, :], m.ident_b[:, :])
                    mm.then_inc(s["turned"], 1)

                for q in range(4):
                    if q >= 2:
                        pe.wait_ge(s["turned_sb"], q - 1)
                    turn(q, q)
                with pe.Fori(0, ITS) as it:
                    for q in range(4):
                        pe.wait_ge(s["turned_sb"], it * 4 + (q + 1))
                        for v in (2 * q, 2 * q + 1):
                            pe.wait_ge(s["pair_used"], it * PAIRS + (v + 1))
                            for i in range(2):
                                u = 2 * v + i
                                blk = pe.value_load(m.jrow[0:1, bass.ds(it * IT + u, 1)], min_val=0, max_val=LAST_BLOCK)
                                mm = pe.matmul(QP[v % 4][:, i * FEAT:(i + 1) * FEAT], OHT[:, u, :],
                                               m.node[:, bass.ds(blk * FEAT, FEAT)], start=True, stop=True)
                            mm.then_inc(s["q_rows"], 1)
                        pe.wait_ge(s["turned_sb"], it * 4 + (3 + q))
                        turn(it * 4 + (4 + q), q)

            @block.vector
            def _(dve):
                def make_masks(step, slot):
                    for i in range(4):
                        ins = dve.tensor_scalar(OH[:, slot + i, :], m.iota_f[:, :], m.dst_in[:, bass.ds(step + i, 1)],
                                                None, ALU.is_equal)
                    ins.then_inc(s["masks"], 1)

                for q in range(4):
                    make_masks(4 * q, 4 * q)
                dve.sem_inc(s["pair_used"], 4)
                dve.sem_inc(s["summed"], 2)
                dve.sem_inc(s["added"], 1)
                with dve.Fori(0, ITS) as it:
                    def sum_heads(v):
                        dve.wait_ge(s["pair_used"], it * PAIRS + (v + 5))
                        if v == 0:
                            dve.wait_ge(s["added"], it + 1)
                        dve.tensor_reduce(ST[:, v * 16:(v + 1) * 16], prod[:, v % 2, :].rearrange("p (a b) -> p a b", b=DH),
                                          AX.X, ALU.add).then_inc(s["summed"], 1)

                    for v in range(PAIRS):
                        if v % 2 == 0:
                            dve.wait_ge(s["turned"], it * 4 + (v // 2 + 1))
                            make_masks(it * IT + (IT + 2 * v), 2 * v)
                        dve.wait_ge(s["q_rows"], it * PAIRS + (v + 1))
                        dve.wait_ge(s["summed"], it * PAIRS + (v + 1))
                        for u in (2 * v, 2 * v + 1):
                            dve.wait_ge(k_in[u % 8], it * 32 + (u // 8 + 1) * 16)
                        at = (2 * v) % 8
                        dve.tensor_tensor(prod[:, v % 2, :], K[:, at:at + 2, :].rearrange("p a b -> p (a b)"),
                                          QP[v % 4][:, :], ALU.mult).then_inc(s["pair_used"], 1)
                        if v >= 1:
                            sum_heads(v - 1)
                    sum_heads(PAIRS - 1)
                    Sit = by_head(S)[:, :, bass.ds(it * IT, IT)]
                    dve.wait_ge(s["summed"], it * PAIRS + (PAIRS + 2))
                    dve.tensor_tensor(Sit, Sit, ST[:, :].rearrange("p (s h) -> p h s", h=HEADS), ALU.add).then_inc(s["added"], 1)


def scores_relational(nc, m, d, S):
    RH = RELS * HEADS
    NEG_SLOPE = 0.2
    with ExitStack() as ctx:
        s = sems(nc, m, "rel", "staged used masks turned turned_sb rows bank_used chain added")
        s_in = [new_sem(nc, m, f"rel_s_in{i}") for i in range(IT)]
        sb = lambda nm, sh, dt: ctx.enter_context(nc.sbuf_tensor(f"rel_{nm}", sh, dt))
        K = sb("K", [P, IT, HEADS], F32)
        stage = sb("stage", [P, IT], I32)
        OH = sb("OH", [P, IT, P], BF16)
        OHT = sb("OHT", [P, IT, P], F32)
        prod = sb("prod", [P, 2, 8 * RH], F32)
        ST = sb("ST", [P, 2, 8 * HEADS], F32)
        TP = [ctx.enter_context(nc.psum_tensor(f"rel_TP{i}", [P, 1024], BF16)) for i in range(2)]
        QP = [ctx.enter_context(nc.psum_tensor(f"rel_QP{i}", [P, 8 * RH], F32)) for i in range(4)]

        with nc.Block() as block:

            @block.gpsimd
            def _(pool):
                with pool.Fori(0, ITS) as it:
                    for u in range(IT):
                        if u % 8 == 0:
                            pool.wait_ge(s["staged"], it * 2 + (u // 8 + 1))
                            pool.wait_ge(s["used"], it * 2 + (u // 8 + 1))
                        if u % 2 == 0:
                            hold(pool, m)
                        pool.indirect_dma_start(out=K[:, u, :], out_offset=None, in_=d["s_tab"][:, :],
                                                in_offset=bass.IndirectOffsetOnAxis(ap=stage[:, u:u + 1], axis=0)
                                                ).then_inc(s_in[u], 16)

            @block.scalar
            def _(act):
                def to_sbuf(quad, slot):
                    act.wait_ge(s["turned"], quad + 1)
                    act.copy(OHT[:, 4 * slot:4 * slot + 4, :].rearrange("p a b -> p (a b)"),
                             TP[slot % 2][:, 0:512]).then_inc(s["turned_sb"], 1)

                for h in range(2):
                    act.copy(stage[:, 8 * h:8 * h + 8], m.idx_rel[:, 8 * h:8 * h + 8]).then_inc(s["staged"], 1)
                for q in range(4):
                    to_sbuf(q, q)
                with act.Fori(0, ITS) as it:
                    for q in range(4):
                        act.wait_ge(s["rows"], it * 4 + (q + 1))
                        to_sbuf(it * 4 + (4 + q), q)
                    stage_halves(act, stage, m.idx_rel, s["staged"],
                                 [[(k, 16, 16) for k in s_in[0:8]], [(k, 16, 16) for k in s_in[8:16]]], it)

            @block.tensor
            def _(pe):
                def turn(quad, slot):
                    pe.wait_ge(s["masks"], quad + 1)
                    for i in range(4):
                        mm = pe.transpose(TP[slot % 2][:, i * P:(i + 1) * P], OH[:, 4 * slot + i, :], m.ident_b[:, :])
                    mm.then_inc(s["turned"], 1)

                for q in range(4):
                    if q >= 2:
                        pe.wait_ge(s["turned_sb"], q - 1)
                    turn(q, q)
                with pe.Fori(0, ITS) as it:
                    for q in range(4):
                        pe.wait_ge(s["turned_sb"], it * 4 + (q + 1))
                        if q % 2 == 0:
                            pe.wait_ge(s["bank_used"], it * 2 + (q // 2 + 1))
                        for i in range(4):
                            u = 4 * q + i
                            blk = pe.value_load(m.jrow[0:1, bass.ds(it * IT + u, 1)], min_val=0, max_val=LAST_BLOCK)
                            mm = pe.matmul(QP[q // 2][:, (u % 8) * RH:(u % 8 + 1) * RH], OHT[:, u, :],
                                           m.node[:, bass.ds(blk * RH, RH)], start=True, stop=True)
                        mm.then_inc(s["rows"], 1)
                        pe.wait_ge(s["turned_sb"], it * 4 + (3 + q))
                        turn(it * 4 + (4 + q), q)

            @block.vector
            def _(dve):
                def make_masks(step, slot):
                    for i in range(4):
                        ins = dve.tensor_scalar(OH[:, slot + i, :], m.iota_f[:, :], m.dst_in[:, bass.ds(step + i, 1)],
                                                None, ALU.is_equal)
                    ins.then_inc(s["masks"], 1)

                for q in range(4):
                    make_masks(4 * q, 4 * q)
                dve.memset(by_head(S)[:, :, STEPS:], 0.0)
                dve.sem_inc(s["bank_used"], 2)
                dve.sem_inc(s["used"], 2)
                with dve.Fori(0, ITS) as it:
                    for g in range(2):
                        base = it * 8 + 4 * g
                        for q in (2 * g, 2 * g + 1):
                            dve.wait_ge(s["turned"], it * 4 + (q + 1))
                            make_masks(it * IT + (IT + 4 * q), 4 * q)
                        dve.wait_ge(s["rows"], it * 4 + (2 * g + 2))
                        rel = m.relmask[:, bass.ds(it * (IT * RELS) + g * RH, RH)]
                        dve.tensor_tensor(prod[:, g, :].rearrange("p (a h) -> p a h", h=HEADS),
                                          QP[g][:, :].rearrange("p (a h) -> p a h", h=HEADS),
                                          rel.unsqueeze(2).to_broadcast([P, RH, HEADS]), ALU.mult).then_inc(s["bank_used"], 1)
                        dve.wait_ge(s["bank_used"], it * 2 + (g + 3))
                        dve.tensor_reduce(ST[:, g, :].rearrange("p (s h) -> p s h", h=HEADS),
                                          prod[:, g, :].rearrange("p (s r h) -> p s h r", r=RELS, h=HEADS),
                                          AX.X, ALU.add).then_inc(s["chain"], 1)
                        for u in range(8 * g, 8 * g + 8):
                            dve.wait_ge(s_in[u], it * 16 + 16)
                        dve.wait_ge(s["chain"], base + 1)
                        dve.tensor_tensor(ST[:, g, :], ST[:, g, :], K[:, 8 * g:8 * g + 8, :].rearrange("p a h -> p (a h)"),
                                          ALU.add).then_inc(s["used"], 1)
                        dve.wait_ge(s["used"], it * 2 + (g + 3))
                        Sg = by_head(S)[:, :, bass.ds(it * IT + 8 * g, 8)]
                        sums = ST[:, g, :].rearrange("p (s h) -> p h s", h=HEADS)
                        dve.scalar_tensor_tensor(Sg, sums, NEG_SLOPE, sums, ALU.mult, ALU.max).then_inc(s["chain"], 1)
                        dve.wait_ge(s["chain"], base + 2)
                        dve.tensor_tensor(Sg, Sg, m.outside[:, bass.ds(it * IT + 8 * g, 8)].unsqueeze(1).to_broadcast(
                            [P, HEADS, 8]), ALU.add).then_inc(s["chain"], 2)


def segment_softmax(nc, m, S, floor, name):
    with ExitStack() as ctx:
        s = sems(nc, m, name, "turned copied dve pe rows neg exp back back_copied")
        sb = lambda nm, sh, dt: ctx.enter_context(nc.sbuf_tensor(f"{name}_{nm}", sh, dt))
        SC = sb("SC", [P, CLEN], F32)
        M = sb("M", [P, CLEN], F32)
        row = sb("row", [1, 2, P + 1], F32)
        col = sb("col", [P, 2], F32)
        pt = [ctx.enter_context(nc.psum_tensor(f"{name}_p{i}", [P, 512], F32)) for i in range(4)]
        pr = ctx.enter_context(nc.psum_tensor(f"{name}_pr", [1, P], F32))
        pc = ctx.enter_context(nc.psum_tensor(f"{name}_pc", [P, 1], F32))
        Sv = S[:, :].rearrange("p (hc g) -> p g hc", g=CS)
        QUADS = -(-CS // 4)
        quad = lambda q: range(4 * q, min(4 * q + 4, CS))
        cuts = [0, 14, 27, 40, CS]

        with nc.Block() as block:

            @block.tensor
            def _(pe):
                for q in range(QUADS):
                    if q >= 4:
                        pe.wait_ge(s["copied"], q - 3)
                    for i, g in enumerate(quad(q)):
                        mm = pe.transpose(pt[q % 4][:, i * P:(i + 1) * P], Sv[:, g, :], m.ident[:, :])
                    mm.then_inc(s["turned"], 1)
                for direction in range(2):
                    pe.wait_ge(s["dve"], 1 + 4 * direction)
                    pe.transpose(pr[:, :], M[:, CLEN - 1:CLEN] if direction == 0 else M[:, 0:1], m.ident[:, :]).then_inc(s["pe"], 1)
                    pe.wait_ge(s["dve"], 3 + 4 * direction)
                    pe.transpose(pc[:, :], row[0:1, 0, 0:P] if direction == 0 else row[0:1, 1, 1:P + 1],
                                 m.ident[0:1, 0:1]).then_inc(s["pe"], 1)
                for q in range(QUADS):
                    pe.wait_ge(s["exp"], sum(quad(q)[-1] >= c for c in cuts))
                    if q >= 4:
                        pe.wait_ge(s["back_copied"], q - 3)
                    for i, g in enumerate(quad(q)):
                        mm = pe.transpose(pt[q % 4][:, i * P:(i + 1) * P], SC[:, g * P:(g + 1) * P], m.ident[:, :])
                    mm.then_inc(s["back"], 1)

            @block.scalar
            def _(act):
                for q in range(QUADS):
                    act.wait_ge(s["turned"], q + 1)
                    n = len(quad(q)) * P
                    act.copy(SC[:, q * 512:q * 512 + n], pt[q % 4][:, 0:n]).then_inc(s["copied"], 1)
                for i in range(len(cuts) - 1):
                    a, b = cuts[i] * P, cuts[i + 1] * P
                    act.wait_ge(s["neg"], i + 1)
                    act.activation(SC[:, a:b], M[:, a:b], ACT.Exp, scale=-1.0).then_inc(s["exp"], 1)

            @block.vector
            def _(dve):
                done = 0

                def step(ins):
                    nonlocal done
                    done += 1
                    ins.then_inc(s["dve"], 1)
                    dve.wait_ge(s["dve"], done)

                dve.wait_ge(s["copied"], QUADS)
                for direction in range(2):
                    fwd = direction == 0
                    starts = m.starts[:, 0:CLEN] if fwd else m.starts[:, CLEN:0:-1]
                    src = SC[:, :] if fwd else M[:, ::-1]
                    out = M[:, :] if fwd else M[:, ::-1]
                    step(dve.tensor_tensor_scan(out, starts, src, -BIG, ALU.add, ALU.max))
                    dve.wait_ge(s["pe"], 1 + 2 * direction)
                    r = row[0:1, direction, :]
                    if fwd:
                        step(dve.memset(r[:, 0:1], -BIG))
                        step(dve.tensor_tensor_scan(r[:, 1:P + 1], m.chain_fwd[:, :], pr[0:1, :], -BIG, ALU.add, ALU.max))
                    else:
                        step(dve.memset(r[:, P:P + 1], -BIG))
                        step(dve.tensor_tensor_scan(r[:, P - 1::-1], m.chain_bwd[:, ::-1], pr[0:1, ::-1], -BIG,
                                                    ALU.add, ALU.max))
                    dve.wait_ge(s["pe"], 2 + 2 * direction)
                    step(dve.tensor_copy(col[:, direction:direction + 1], pc[:, :]))
                    if fwd:
                        dve.tensor_tensor_scan(out, starts, src, col[:, 0:1], ALU.add, ALU.max).then_inc(s["rows"], 1)
                        dve.wait_ge(s["rows"], 1)
                    else:
                        dve.tensor_tensor_scan(out, starts, src, col[:, 1:2], ALU.add, ALU.max).then_inc(s["rows"], 1)
                        dve.wait_ge(s["rows"], 2)
                for i in range(len(cuts) - 1):
                    a, b = cuts[i] * P, cuts[i + 1] * P
                    dve.scalar_tensor_tensor(M[:, a:b], M[:, a:b], floor, SC[:, a:b], ALU.max, ALU.subtract).then_inc(s["neg"], 1)
                for q in range(QUADS):
                    dve.wait_ge(s["back"], q + 1)
                    n = len(quad(q))
                    dve.tensor_copy(Sv[:, 4 * q:4 * q + n, :],
                                    pt[q % 4][:, 0:n * P].rearrange("p (g hc) -> p g hc", g=n)).then_inc(s["back_copied"], 1)


def aggregate(nc, m, S, table, idx, name):
    LEAD = 4
    PAIRS = IT // 2
    with ExitStack() as ctx:
        s = sems(nc, m, name, "staged masks weighted weights cleared sums added")
        v_in = [new_sem(nc, m, f"{name}_v_in{i}") for i in range(8)]
        sb = lambda nm, sh, dt: ctx.enter_context(nc.sbuf_tensor(f"{name}_{nm}", sh, dt))
        V = sb("V", [P, 8, FEAT], F32)
        stage = sb("stage", [P, IT], I32)
        OH = sb("OH", [P, IT, P], F32)
        U = sb("U", [P, 4, 2 * FEAT], F32)
        A = sb("A", [P, 2, 8 * HEADS], F32)
        AP_ = [ctx.enter_context(nc.psum_tensor(f"{name}_AP{i}", [P, 512], F32)) for i in range(2)]
        SP = [ctx.enter_context(nc.psum_tensor(f"{name}_SP{i}", [P, 512], F32)) for i in range(4)]

        with nc.Block() as block:

            @block.gpsimd
            def _(pool):
                def gather(u, new_half, half, pair):
                    if new_half:
                        pool.wait_ge(s["staged"], half)
                    if u % 2 == 0:
                        pool.wait_ge(s["weighted"], pair)
                    if u % 2 == 0:
                        hold(pool, m)
                    pool.indirect_dma_start(out=V[:, u % 8, :], out_offset=None, in_=table[:, :],
                                            in_offset=bass.IndirectOffsetOnAxis(ap=stage[:, u:u + 1], axis=0)
                                            ).then_inc(v_in[u % 8], 16)

                for u in range(LEAD):
                    gather(u, u == 0, 1, u // 2 + 1)
                with pool.Fori(0, ITS) as it:
                    for a in range(LEAD, LEAD + IT):
                        gather(a % IT, a % 8 == 0, it * 2 + (a // 8 + 1), it * PAIRS + (a // 2 + 1))

            @block.scalar
            def _(act):
                def weights(half, h):
                    w = by_head(S)[:, :, bass.ds(half * 8, 8)].rearrange("p h s -> p s h")
                    act.copy(AP_[h][:, 0:8 * HEADS].rearrange("p (s h) -> p s h", h=HEADS), w).then_inc(s["weights"], 1)
                    act.copy(A[:, h, :].rearrange("p (s h) -> p s h", h=HEADS), w).then_inc(s["weights"], 1)

                for h in range(2):
                    act.copy(stage[:, 8 * h:8 * h + 8], idx[:, 8 * h:8 * h + 8]).then_inc(s["staged"], 1)
                    weights(h, h)
                with act.Fori(0, ITS) as it:
                    for h in range(2):
                        for k in v_in:
                            act.wait_ge(k, it * 32 + 16 * (h + 1))
                        act.copy(stage[:, 8 * h:8 * h + 8], idx[:, bass.ds(it * IT + (IT + 8 * h), 8)]).then_inc(s["staged"], 1)
                        act.wait_ge(s["sums"], it * IT + 8 * (h + 1))
                        weights(it * 2 + (2 + h), h)

            @block.tensor
            def _(pe):
                def sum_step(u, masks, weighted, half, free):
                    if u % 4 == 0:
                        pe.wait_ge(s["masks"], masks)
                    if u % 2 == 0:
                        pe.wait_ge(s["weighted"], weighted)
                    if u % 8 == 0:
                        pe.wait_ge(s["weights"], half * 2)
                    pe.wait_ge(s["added"], free)
                    v = u // 2
                    pe.matmul(SP[u % 4][:, 0:FEAT], OH[:, u, :], U[:, v % 4, (u % 2) * FEAT:(u % 2 + 1) * FEAT],
                              start=True, stop=True, skip_group_check=True)
                    pe.matmul(SP[u % 4][:, FEAT:NUMC], OH[:, u, :], A[:, u // 8, (u % 8) * HEADS:(u % 8 + 1) * HEADS],
                              start=False, stop=True, skip_group_check=True).then_inc(s["sums"], 1)

                for u in range(LEAD):
                    sum_step(u, 1, u // 2 + 5, 1, u + 1)
                with pe.Fori(0, ITS) as it:
                    for a in range(LEAD, LEAD + IT):
                        sum_step(a % IT, it * 4 + (a // 4 + 1), it * PAIRS + (a // 2 + 5), it * 2 + (a // 8 + 1),
                                 it * IT + (a + 1))

            @block.vector
            def _(dve):
                def make_masks(step, slot):
                    for i in range(4):
                        ins = dve.tensor_scalar(OH[:, slot + i, :], m.iota_f[:, :], m.dst_in[:, bass.ds(step + i, 1)],
                                                None, ALU.is_equal)
                    ins.then_inc(s["masks"], 1)

                def weigh(v, rows_in, half):
                    if v % 4 == 0:
                        dve.wait_ge(s["weights"], half * 2)
                    for u in (2 * v, 2 * v + 1):
                        dve.wait_ge(v_in[u % 8], rows_in)
                    at = (2 * v) % 8
                    dve.tensor_tensor(U[:, v % 4, :].rearrange("p (a b) -> p a b", b=DH),
                                      V[:, at:at + 2, :].rearrange("p a b -> p (a b)").rearrange("p (a b) -> p a b", b=DH),
                                      AP_[(v // 4) % 2][:, (v % 4) * 16:(v % 4 + 1) * 16].unsqueeze(2).to_broadcast(
                                          [P, 2 * HEADS, DH]), ALU.mult).then_inc(s["weighted"], 1)

                dve.memset(m.node[:, :], 0.0).then_inc(s["cleared"], 1)
                dve.wait_ge(s["cleared"], 1)
                dve.sem_inc(s["weighted"], 4)
                dve.sem_inc(s["added"], 4)
                make_masks(0, 0)
                for v in range(2):
                    weigh(v, 16, 1)
                with dve.Fori(0, ITS) as it:
                    for q in range(4):
                        a = 4 * (q + 1)
                        make_masks(it * IT + a, a % IT)
                        for v in (a // 2, a // 2 + 1):
                            weigh(v % PAIRS, it * 32 + 16 * ((2 * v) // 8 + 1), it * 2 + (v // 4 + 1))
                        for u in range(4 * q, 4 * q + 4):
                            blk = dve.value_load(m.jrow[0:1, bass.ds(it * IT + u, 1)], min_val=0, max_val=LAST_BLOCK)
                            dve.wait_ge(s["sums"], it * IT + (u + 1))
                            dve.wait_ge(s["added"], it * IT + (u + 4))
                            acc = m.node[:, bass.ds(blk * NUMC, NUMC)]
                            dve.tensor_tensor(acc, acc, SP[u % 4][:, 0:NUMC], ALU.add).then_inc(s["added"], 1)


def norm_stats(dve, m, x, st, mv, sem_stats, n_stats, sem_mv):
    dve.bn_stats(st, x).then_inc(sem_stats, 1)
    dve.wait_ge(sem_stats, n_stats)
    hold(dve, m)
    dve.bn_aggr(mv, st).then_inc(sem_mv, 1)


def norm_scale(pool, m, mv, rstd, sem_eps, n_eps, sem_rstd):
    hold(pool, m)
    pool.tensor_scalar(rstd, mv[:, 1:2], LN_EPS, 1.0, ALU.add, ALU.mult).then_inc(sem_eps, 1)
    pool.wait_ge(sem_eps, n_eps)
    pool.tensor_tensor(rstd, rstd, m.mhalf[:, :], ALU.pow).then_inc(sem_rstd, 1)


def has(t, count):
    return not isinstance(t, int) or 0 <= t < count


def need(eng, sem, value):
    if not isinstance(value, int) or value > 0:
        eng.wait_ge(sem, value)


def pipeline(eng, body, lead, lag, count):
    turns = (count - lead - 4) // 2
    for t in range(-lead, 4):
        body(t, t % 2)
    with eng.Fori(0, turns) as it:
        for i in range(2):
            body(it * 2 + (4 + i), i)
    for t in range(4 + 2 * turns, count + lag):
        body(t, t % 2)


def slot_wait(eng, sem, t, per):
    if isinstance(t, int):
        eng.wait_ge(sem, (t // 2 + 1) * per)
    else:
        eng.wait_ge(sem, t // 2 * per + per)


def norm_front(nc, m, ctx, name, tiles):
    f = Shared()
    f.s = sems(nc, m, name, "stats mv eps rstd normed turned yT")
    sb = lambda nm, sh, dt: ctx.enter_context(nc.sbuf_tensor(f"{name}_{nm}", sh, dt))
    f.Y = sb("Y", [P, 2, FEAT], F32)
    f.YT = sb("YT", [P, 2, FEAT], F32)
    f.st = sb("st", [P, 2, 6], F32)
    f.mv = sb("mv", [P, 2, 2], F32)
    f.rstd = sb("rstd", [P, 2], F32)
    f.T = [ctx.enter_context(nc.psum_tensor(f"{name}_T{i}", [P, 512], F32)) for i in range(2)]
    f.tiles = tiles
    return f


def front_stats(dve, m, f, x, t, i):
    if has(t, f.tiles):
        norm_stats(dve, m, x, f.st[:, i, :], f.mv[:, i, :], f.s["stats"], t + 1, f.s["mv"])


def front_scale(pool, m, f, t, i):
    if has(t, f.tiles):
        pool.wait_ge(f.s["mv"], t + 1)
        need(pool, f.s["normed"], t - 1)
        norm_scale(pool, m, f.mv[:, i, :], f.rstd[:, i:i + 1], f.s["eps"], t + 1, f.s["rstd"])


def front_norm(dve, f, x, t, i):
    if has(t, f.tiles):
        dve.wait_ge(f.s["rstd"], t + 1)
        need(dve, f.s["turned"], t - 1)
        dve.tensor_scalar(f.Y[:, i, :], x, f.mv[:, i, 0:1], f.rstd[:, i:i + 1], ALU.subtract,
                          ALU.mult).then_inc(f.s["normed"], 1)


def front_turn(pe, m, f, t, i):
    if has(t, f.tiles):
        pe.wait_ge(f.s["normed"], t + 1)
        need(pe, f.s["yT"], t - 1)
        for k in range(2):
            mm = pe.transpose(f.T[i][:, k * P:(k + 1) * P], f.Y[:, i, k * P:(k + 1) * P], m.ident[:, :])
        mm.then_inc(f.s["turned"], 1)


def front_copy(eng, copy, f, t, i, used, per=1):
    if has(t, f.tiles):
        eng.wait_ge(f.s["turned"], t + 1)
        need(eng, used, (t - 1) * per)
        copy(f.YT[:, i, :], f.T[i][:, 0:FEAT]).then_inc(f.s["yT"], 1)


def project_attention(nc, m, d):
    with ExitStack() as ctx:
        s = sems(nc, m, "qkv", "w mm q_out kv_out kv_free stored0 stored1")
        x_in = [new_sem(nc, m, f"qkv_x_in{i}") for i in range(2)]
        stored = (s["stored0"], s["stored1"])
        sb = lambda nm, sh, dt: ctx.enter_context(nc.sbuf_tensor(f"qkv_{nm}", sh, dt))
        f = norm_front(nc, m, ctx, "qkv", BLOCKS)
        W = sb("W", [P, 2, 3 * FEAT], F32)
        X = sb("X", [P, 2, FEAT], F32)
        KV = sb("KV", [P, 2, 2 * FEAT], F32)
        Q = [ctx.enter_context(nc.psum_tensor(f"qkv_Q{i}", [P, 512], F32)) for i in range(2)]
        KVP = [ctx.enter_context(nc.psum_tensor(f"qkv_KV{i}", [P, 512], F32)) for i in range(2)]
        LEAD = 5
        with nc.Block() as block:

            @block.sync
            def _(sp):
                for k in range(2):
                    sp.dma_start(W[:, k, :], d["wqkv"][k * P:(k + 1) * P, :]).then_inc(s["w"], 16)

                def body(t, i):
                    n, j = t + 5, (i + 1) % 2
                    if has(n, BLOCKS):
                        need(sp, f.s["normed"], n - 1)
                        hold(sp, m)
                        sp.dma_start(X[:, j, :], d["x"][bass.ds(n * P, P), :]).then_inc(x_in[j], 16)
                    if has(t, BLOCKS):
                        sp.wait_ge(s["kv_out"], t + 1)
                        hold(sp, m)
                        sp.dma_start(d["k_tab"][bass.ds(t * P, P), :], KV[:, i, 0:FEAT]).then_inc(stored[i], 16)
                        sp.dma_start(d["v_tab"][bass.ds(t * P, P), :], KV[:, i, FEAT:]).then_inc(stored[i], 16)
                    n, j = t - 1, (i + 1) % 2
                    if has(n, BLOCKS):
                        slot_wait(sp, stored[j], n, 32)
                        sp.sem_inc(s["kv_free"], 1)

                pipeline(sp, body, LEAD, 1, BLOCKS)

            @block.gpsimd
            def _(pool):
                pipeline(pool, lambda t, i: front_scale(pool, m, f, t + 4, i), LEAD, 1, BLOCKS)

            @block.scalar
            def _(act):
                def body(t, i):
                    if has(t, BLOCKS):
                        act.wait_ge(s["mm"], t + 1)
                        need(act, s["kv_free"], t - 1)
                        act.copy(KV[:, i, :], KVP[i][:, :]).then_inc(s["kv_out"], 1)
                    front_copy(act, act.copy, f, t + 2, i, s["mm"])

                pipeline(act, body, LEAD, 1, BLOCKS)

            @block.vector
            def _(dve):
                def body(t, i):
                    front_norm(dve, f, X[:, (i + 1) % 2, :], t + 3, (i + 1) % 2)
                    if has(t + 4, BLOCKS):
                        slot_wait(dve, x_in[i], t + 4, 16)
                        front_stats(dve, m, f, X[:, i, :], t + 4, i)
                    if has(t, BLOCKS):
                        dve.wait_ge(s["mm"], t + 1)
                        dve.tensor_scalar(m.node[:, bass.ds(t * FEAT, FEAT)], Q[i][:, 0:FEAT], QSCALE, None,
                                          ALU.mult).then_inc(s["q_out"], 1)

                pipeline(dve, body, LEAD, 1, BLOCKS)

            @block.tensor
            def _(pe):
                pe.wait_ge(s["w"], 32)

                def body(t, i):
                    if has(t, BLOCKS):
                        pe.wait_ge(f.s["yT"], t + 1)
                        need(pe, s["q_out"], t - 1)
                        need(pe, s["kv_out"], t - 1)
                        for k in range(2):
                            pe.matmul(Q[i][:, 0:FEAT], f.YT[:, i, k * P:(k + 1) * P], W[:, k, 0:FEAT],
                                      start=(k == 0), stop=(k == 1))
                        for k in range(2):
                            mm = pe.matmul(KVP[i][:, :], f.YT[:, i, k * P:(k + 1) * P], W[:, k, FEAT:],
                                           start=(k == 0), stop=(k == 1))
                        mm.then_inc(s["mm"], 1)
                    front_turn(pe, m, f, t + 2, i)

                pipeline(pe, body, LEAD, 1, BLOCKS)


def top_experts(dve, m, s, t, probs, best, idx, idx_f, link):
    hold(dve, m)
    link(dve.max(best, probs))
    hold(dve, m)
    link(dve.max_index(idx, best, probs))
    link(dve.tensor_copy(idx_f, idx))


class LoopLink:

    def __init__(self, eng, sem, it, per):
        self.eng, self.sem, self.it, self.per, self.n = eng, sem, it, per, 0

    def __call__(self, ins):
        self.n += 1
        ins.then_inc(self.sem, 1)
        self.eng.wait_ge(self.sem, self.it * self.per + self.n)


def attend_and_route(nc, m, d):
    KC = HID // P
    with ExitStack() as ctx:
        s = sems(nc, m, "gate", "w zeroed filled clipped inverted o_ready o_turned oT attn_out x1 hidden gelu gated logits "
                 "saved0 saved1 y_saved")
        x_in = [new_sem(nc, m, f"gate_x_in{i}") for i in range(2)]
        saved = (s["saved0"], s["saved1"])
        sb = lambda nm, sh, dt: ctx.enter_context(nc.sbuf_tensor(f"gate_{nm}", sh, dt))
        f = norm_front(nc, m, ctx, "gate", BLOCKS)
        Wo = sb("Wo", [P, 2, FEAT], F32)
        W1 = sb("W1", [P, 2, HID], F32)
        b1 = sb("b1", [P, KC], F32)
        Wg = sb("Wg", [P, KC, EXPERTS], F32)
        bg = sb("bg", [P, EXPERTS], F32)
        zeros = sb("zeros", [P, SORTED * FEAT // 8], F32)
        X = sb("X", [P, 2, FEAT], F32)
        O = sb("O", [P, 2, FEAT], F32)
        OT = sb("OT", [P, 2, FEAT], F32)
        HT = sb("HT", [P, 2, HID], F32)
        r = sb("r", [P, 2, HEADS], F32)
        TO = ctx.enter_context(nc.psum_tensor("gate_TO", [P, 512], F32))
        OUT = ctx.enter_context(nc.psum_tensor("gate_OUT", [P, 512], F32))
        LG = ctx.enter_context(nc.psum_tensor("gate_LG", [P, 512], F32))
        HB = [ctx.enter_context(nc.psum_tensor(f"gate_HB{i}", [P, 512], F32)) for i in range(2)]
        LOADS = 7
        LEAD = 6
        node = lambda t, a, b: m.node[:, bass.ds(t * NUMC + a, b - a)]
        with nc.Block() as block:

            @block.sync
            def _(sp):
                for k in range(2):
                    sp.dma_start(Wo[:, k, :], d["wo"][k * P:(k + 1) * P, :]).then_inc(s["w"], 16)
                    sp.dma_start(W1[:, k, :], d["w1"][k * P:(k + 1) * P, :]).then_inc(s["w"], 16)
                sp.dma_start(b1[:, :], d["b1"][:, :]).then_inc(s["w"], 16)
                sp.dma_start(Wg[:, :, :].rearrange("p k e -> p (k e)"), d["wg"][:, :]).then_inc(s["w"], 16)
                sp.dma_start(bg[:, :], d["bg"][0:1, :].to_broadcast([P, EXPERTS])).then_inc(s["w"], 16)
                sp.wait_ge(s["zeroed"], 1)
                flat = d["y_sorted"].rearrange("(p n) c -> p (n c)", p=P)
                width = SORTED * FEAT // 8
                for k in range(8):
                    sp.dma_start(flat[:, k * width:(k + 1) * width], zeros[:, :]).then_inc(s["filled"], 16)

                def body(t, i):
                    n = t + 6
                    if has(n, BLOCKS):
                        need(sp, s["x1"], n - 1)
                        hold(sp, m)
                        sp.dma_start(X[:, i, :], d["x"][bass.ds(n * P, P), :]).then_inc(x_in[i], 16)
                    n, j = t + 3, (i + 1) % 2
                    if has(n, BLOCKS):
                        sp.wait_ge(f.s["normed"], n + 1)
                        hold(sp, m)
                        sp.dma_start(d["y_tab"][bass.ds(n * P, P), :], f.Y[:, j, :]).then_inc(saved[j], 16)
                    if has(t + 2, BLOCKS):
                        slot_wait(sp, saved[i], t + 2, 16)
                        sp.sem_inc(s["y_saved"], 1)

                pipeline(sp, body, LEAD, 1, BLOCKS)
                sp.wait_ge(s["filled"], 16 * 8)

            @block.gpsimd
            def _(pool):
                pool.memset(zeros[:, :], 0.0).then_inc(s["zeroed"], 1)
                pipeline(pool, lambda t, i: front_scale(pool, m, f, t + 4, i), LEAD, 1, BLOCKS)

            @block.scalar
            def _(act):
                act.wait_ge(s["w"], 16 * LOADS)

                def body(t, i):
                    if has(t, BLOCKS):
                        need(act, s["gated"], t - 1)
                        for c in range(KC):
                            if c % 4 == 0:
                                act.wait_ge(s["hidden"], t * 2 + (c // 4 + 1))
                            act.activation(HT[:, i, c * P:(c + 1) * P], HB[c // 4][:, (c % 4) * P:(c % 4 + 1) * P],
                                           ACT.Gelu, bias=b1[:, c:c + 1]).then_inc(s["gelu"], 1)

                pipeline(act, body, LEAD, 1, BLOCKS)

            @block.tensor
            def _(pe):
                pe.wait_ge(s["w"], 16 * LOADS)

                def body(t, i):
                    j = (i + 1) % 2
                    if has(t, BLOCKS):
                        hidden_features(pe, s, f.YT[:, i, :], W1, HB, f.s["yT"], t)
                    if has(t - 1, BLOCKS):
                        pe.wait_ge(s["gelu"], t * KC)
                        need(pe, s["logits"], t - 1)
                        for c in range(KC):
                            mm = pe.matmul(LG[:, 0:EXPERTS], HT[:, j, c * P:(c + 1) * P], Wg[:, c, :],
                                           start=(c == 0), stop=(c == KC - 1))
                        mm.then_inc(s["gated"], 1)
                    front_turn(pe, m, f, t + 2, i)
                    n = t + 4
                    if has(n, BLOCKS):
                        pe.wait_ge(s["oT"], n + 1)
                        need(pe, s["x1"], n)
                        for k in range(2):
                            mm = pe.matmul(OUT[:, 0:FEAT], OT[:, i, k * P:(k + 1) * P], Wo[:, k, :],
                                           start=(k == 0), stop=(k == 1))
                        mm.then_inc(s["attn_out"], 1)
                    n = t + 5
                    if has(n, BLOCKS):
                        pe.wait_ge(s["o_ready"], n + 1)
                        need(pe, s["oT"], n)
                        for k in range(2):
                            mm = pe.transpose(TO[:, k * P:(k + 1) * P], O[:, j, k * P:(k + 1) * P], m.ident[:, :])
                        mm.then_inc(s["o_turned"], 1)

                pipeline(pe, body, LEAD, 1, BLOCKS)

            @block.vector
            def _(dve):
                dve.wait_ge(s["w"], 16 * LOADS)

                def body(t, i):
                    j = (i + 1) % 2
                    if has(t + 3, BLOCKS):
                        need(dve, s["y_saved"], t + 2)
                        front_norm(dve, f, node(t + 3, 0, FEAT), t + 3, j)
                    if has(t - 1, BLOCKS):
                        dve.wait_ge(s["gated"], t)
                        dve.tensor_tensor(m.logits[:, bass.ds((t - 1) * EXPERTS, EXPERTS)], LG[:, 0:EXPERTS],
                                          bg[:, :], ALU.add).then_inc(s["logits"], 1)
                    front_copy(dve, dve.tensor_copy, f, t + 2, i, s["hidden"], 2)
                    n = t + 4
                    if has(n, BLOCKS):
                        dve.wait_ge(s["attn_out"], n + 1)
                        slot_wait(dve, x_in[i], n, 16)
                        dve.tensor_tensor(node(n, 0, FEAT), X[:, i, :], OUT[:, 0:FEAT], ALU.add).then_inc(s["x1"], 1)
                        dve.wait_ge(s["x1"], n + 1)
                        hold(dve, m)
                        front_stats(dve, m, f, node(n, 0, FEAT), n, i)
                    n = t + 5
                    if has(n, BLOCKS):
                        dve.wait_ge(s["o_turned"], n + 1)
                        need(dve, s["attn_out"], n - 1)
                        dve.tensor_copy(OT[:, j, :], TO[:, 0:FEAT]).then_inc(s["oT"], 1)
                    n = t + 6
                    if has(n, BLOCKS):
                        dve.tensor_scalar(r[:, i, :], node(n, FEAT, NUMC), 1e-30, None, ALU.max).then_inc(s["clipped"], 1)
                        dve.wait_ge(s["clipped"], n + 1)
                        dve.reciprocal(r[:, i, :], r[:, i, :]).then_inc(s["inverted"], 1)
                        dve.wait_ge(s["inverted"], n + 1)
                        need(dve, s["o_turned"], n - 1)
                        dve.tensor_tensor(O[:, i, :].rearrange("p (h c) -> p h c", c=DH),
                                          node(n, 0, FEAT).rearrange("p (h c) -> p h c", c=DH),
                                          r[:, i, :].unsqueeze(2).to_broadcast([P, HEADS, DH]),
                                          ALU.mult).then_inc(s["o_ready"], 1)

                pipeline(dve, body, LEAD, 1, BLOCKS)


def hidden_features(pe, s, yT, W1, HB, turned, t):
    KC = HID // P
    pe.wait_ge(turned, t + 1)
    for c in range(KC):
        if c % 4 == 0:
            need(pe, s["gelu"], t * KC + (c + 4 - KC))
        for k in range(2):
            mm = pe.matmul(HB[c // 4][:, (c % 4) * P:(c % 4 + 1) * P], W1[:, k, c * P:(c + 1) * P],
                           yT[:, k * P:(k + 1) * P], start=(k == 0), stop=(k == 1))
        if c % 4 == 3:
            mm.then_inc(s["hidden"], 1)


def sort_by_expert(nc, m, d):
    BE = BLOCKS * EXPERTS
    with ExitStack() as ctx:
        s = sems(nc, m, "sort", "link shifted powed pidx counted chosen")
        sb = lambda nm, sh, dt: ctx.enter_context(nc.sbuf_tensor(f"sort_{nm}", sh, dt))
        grid = lambda a: a[:, :].rearrange("p (b e) -> p b e", e=EXPERTS)
        per_row = lambda a: a[:, :].unsqueeze(2).to_broadcast([P, BLOCKS, EXPERTS])
        per_expert = lambda a: a[:, 0:EXPERTS].unsqueeze(1).to_broadcast([P, BLOCKS, EXPERTS])
        ex = sb("ex", [P, BE], F32)
        hot = sb("hot", [P, BE], F32)
        pick = sb("pick", [P, BE], F32)
        sums = [sb(f"sums{i}", [P, BE], F32) for i in range(2)]
        top = sb("top", [P, BLOCKS], F32)
        inv = sb("inv", [P, BLOCKS], F32)
        numbers = sb("numbers", [P, EXPERTS], F32)
        pidx_i = sb("pidx_i", [P, 1], I32)
        pidx = sb("pidx", [P, 1], F32)
        before = sb("before", [P, P], F32)
        ones = sb("ones", [P, P], F32)
        tiles_i = sb("tiles_i", [P, EXPERTS], I32)
        tiles = sb("tiles", [P, EXPERTS], F32)
        ends = [sb(f"ends{i}", [P, EXPERTS], F32) for i in range(2)]
        start = sb("start", [P, EXPERTS], F32)
        over = sb("over", [1, SORTED * EXPERTS], F32)
        tile_f = sb("tile_f", [1, SORTED], F32)
        WITHIN = ctx.enter_context(nc.psum_tensor("sort_within", [P, 512], F32))
        TOTAL = ctx.enter_context(nc.psum_tensor("sort_total", [P, 512], F32))
        with nc.Block() as block:

            @block.gpsimd
            def _(pool):
                pool.iota(pidx_i[:, :], pattern=[[1, 1]], base=0, channel_multiplier=1).then_inc(s["pidx"], 1)
                pool.wait_ge(s["shifted"], 1)
                pool.tensor_tensor(grid(ex), per_expert(m.e_const), grid(m.logits), ALU.pow).then_inc(s["powed"], 1)

            @block.tensor
            def _(pe):
                pe.wait_ge(s["chosen"], 1)
                pe.matmul(WITHIN[:, 0:BE], before[:, :], hot[:, :], start=True, stop=True)
                pe.matmul(TOTAL[:, 0:BE], ones[:, :], hot[:, :], start=True, stop=True).then_inc(s["counted"], 1)

            @block.vector
            def _(dve):
                link = Link(dve, s["link"])
                link(dve.tensor_reduce(top[:, :], grid(m.logits), AX.X, ALU.max))
                dve.tensor_tensor(grid(m.logits), grid(m.logits), per_row(top), ALU.subtract).then_inc(s["shifted"], 1)
                dve.wait_ge(s["pidx"], 1)
                link(dve.tensor_copy(pidx[:, :], pidx_i[:, :]))
                link(dve.tensor_scalar(before[:, :], m.iota_f[:, :], pidx[:, 0:1], None, ALU.is_gt))
                link(dve.memset(ones[:, :], 1.0))
                link(dve.tensor_scalar(numbers[:, :], m.iota_f[:, 0:EXPERTS], -float(EXPERTS), None, ALU.add))
                dve.wait_ge(s["powed"], 1)
                link(dve.tensor_reduce(inv[:, :], grid(ex), AX.X, ALU.add))
                link(dve.reciprocal(inv[:, :], inv[:, :]))
                link(dve.tensor_tensor(grid(ex), grid(ex), per_row(inv), ALU.mult))
                link(dve.tensor_reduce(m.prob[:, :], grid(ex), AX.X, ALU.max))
                link(dve.tensor_tensor(grid(hot), grid(ex), per_row(m.prob), ALU.is_equal))
                link(dve.tensor_tensor(grid(pick), grid(hot), per_expert(numbers), ALU.mult))
                link(dve.tensor_reduce(top[:, :], grid(pick), AX.X, ALU.min))
                link(dve.tensor_tensor(grid(hot), per_expert(numbers), per_row(top), ALU.is_equal))
                dve.sem_inc(s["chosen"], 1)
                dve.wait_ge(s["counted"], 1)
                link(dve.tensor_copy(sums[0][:, :], TOTAL[:, 0:BE]))
                step, a, b = EXPERTS, 0, 1
                while step < BE:
                    link(dve.tensor_copy(sums[b][:, 0:step], sums[a][:, 0:step]))
                    link(dve.tensor_tensor(sums[b][:, step:], sums[a][:, step:], sums[a][:, 0:BE - step], ALU.add))
                    step, a, b = 2 * step, b, a
                count = sums[a][:, BE - EXPERTS:BE]
                link(dve.tensor_scalar(start[:, :], count, float(P - 1), None, ALU.add))
                link(dve.tensor_copy(tiles_i[:, :], start[:, :]))
                link(dve.tensor_scalar(tiles_i[:, :], tiles_i[:, :], 7, None, ALU.arith_shift_right))
                link(dve.tensor_copy(tiles[:, :], tiles_i[:, :]))
                link(dve.tensor_copy(ends[0][:, :], tiles[:, :]))
                step, ea, eb = 1, 0, 1
                while step < EXPERTS:
                    link(dve.tensor_copy(ends[eb][:, 0:step], ends[ea][:, 0:step]))
                    link(dve.tensor_tensor(ends[eb][:, step:], ends[ea][:, step:], ends[ea][:, 0:EXPERTS - step], ALU.add))
                    step, ea, eb = 2 * step, eb, ea
                link(dve.tensor_tensor(start[:, :], ends[ea][:, :], tiles[:, :], ALU.subtract))
                link(dve.tensor_scalar(start[:, :], start[:, :], float(P), None, ALU.mult))
                link(dve.tensor_tensor(sums[a][:, :], sums[a][:, :], TOTAL[:, 0:BE], ALU.subtract))
                link(dve.tensor_tensor(sums[a][:, :], sums[a][:, :], WITHIN[:, 0:BE], ALU.add))
                link(dve.tensor_tensor(grid(sums[a]), grid(sums[a]), per_expert(start), ALU.add))
                link(dve.tensor_tensor(sums[a][:, :], sums[a][:, :], hot[:, :], ALU.mult))
                link(dve.tensor_reduce(top[:, :], grid(sums[a]), AX.X, ALU.add))
                link(dve.tensor_copy(m.slot[:, :], top[:, :]))
                link(dve.tensor_tensor(over[0:1, :].rearrange("p (t e) -> p t e", e=EXPERTS),
                                       m.iota_f[0:1, 0:SORTED].unsqueeze(2).to_broadcast([1, SORTED, EXPERTS]),
                                       ends[ea][0:1, :].unsqueeze(1).to_broadcast([1, SORTED, EXPERTS]), ALU.is_ge))
                link(dve.tensor_reduce(tile_f[:, :], over[0:1, :].rearrange("p (t e) -> p t e", e=EXPERTS), AX.X, ALU.add))
                link(dve.tensor_scalar(tile_f[:, :], tile_f[:, :], float(EXPERTS - 1), None, ALU.min))
                link(dve.tensor_copy(m.tile_expert[:, :], tile_f[:, :]))


def scatter_rows(nc, m, d):
    SLOTS = 5
    ROUNDS = BLOCKS // SLOTS
    assert ROUNDS * SLOTS == BLOCKS
    with ExitStack() as ctx:
        s = sems(nc, m, "scatter", "staged sent")
        y_in = [new_sem(nc, m, f"scatter_in{i}") for i in range(SLOTS)]
        out = [new_sem(nc, m, f"scatter_out{i}") for i in range(SLOTS)]
        Y = ctx.enter_context(nc.sbuf_tensor("scatter_Y", [P, SLOTS, FEAT], F32))
        to = ctx.enter_context(nc.sbuf_tensor("scatter_to", [P, SLOTS], I32))
        with nc.Block() as block:

            @block.sync
            def _(sp):
                def load(n, q):
                    sp.dma_start(Y[:, q, :], d["y_tab"][bass.ds(n * P, P), :]).then_inc(y_in[q], 16)

                for q in range(SLOTS):
                    load(q, q)
                with sp.Fori(0, ROUNDS - 1) as it:
                    for q in range(SLOTS):
                        sp.wait_ge(out[q], it * 16 + 16)
                        hold(sp, m)
                        load(it * SLOTS + (SLOTS + q), q)

            @block.vector
            def _(dve):
                def stage(n, q):
                    dve.tensor_copy(to[:, q:q + 1], m.slot[:, bass.ds(n, 1)]).then_inc(s["staged"], 1)

                for q in range(SLOTS):
                    stage(q, q)
                with dve.Fori(0, ROUNDS - 1) as it:
                    for q in range(SLOTS):
                        dve.wait_ge(out[q], it * 16 + 16)
                        stage(it * SLOTS + (SLOTS + q), q)

            @block.gpsimd
            def _(pool):
                def scatter(q):
                    pool.indirect_dma_start(out=d["y_sorted"][:, :],
                                            out_offset=bass.IndirectOffsetOnAxis(ap=to[:, q:q + 1], axis=0),
                                            in_=Y[:, q, :], in_offset=None).then_inc(out[q], 16)

                with pool.Fori(0, ROUNDS) as it:
                    for q in range(SLOTS):
                        pool.wait_ge(s["staged"], it * SLOTS + (q + 1))
                        pool.wait_ge(y_in[q], it * 16 + 16)
                        hold(pool, m)
                        scatter(q)
                for q in range(SLOTS):
                    pool.wait_ge(out[q], 16 * ROUNDS)


def expert_of_sorted(nc, m, d):
    KC = HID // P
    with ExitStack() as ctx:
        s = sems(nc, m, "exp", "w yT hidden gelu turned made out stored0 stored1 row_free")
        y_in = [new_sem(nc, m, f"exp_y_in{i}") for i in range(2)]
        stored = (s["stored0"], s["stored1"])
        sb = lambda nm, sh, dt: ctx.enter_context(nc.sbuf_tensor(f"exp_{nm}", sh, dt))
        W1 = sb("W1", [P, 2, HID], F32)
        b1 = sb("b1", [P, KC], F32)
        Wd = sb("Wd", [P, KC, EXPERTS * FEAT], F32)
        bd = sb("bd", [1, EXPERTS * FEAT], F32)
        Y = sb("Y", [P, 2, FEAT], F32)
        YT = sb("YT", [P, 2, FEAT], F32)
        HT = sb("HT", [P, 2, HID], F32)
        R = sb("R", [P, 2, FEAT], F32)
        T = [ctx.enter_context(nc.psum_tensor(f"exp_T{i}", [P, 512], F32)) for i in range(2)]
        HB = [ctx.enter_context(nc.psum_tensor(f"exp_HB{i}", [P, 512], F32)) for i in range(2)]
        RB = [ctx.enter_context(nc.psum_tensor(f"exp_RB{i}", [P, 512], F32)) for i in range(2)]
        LOADS = 4 + KC
        LEAD = 4
        with nc.Block() as block:

            @block.sync
            def _(sp):
                for k in range(2):
                    sp.dma_start(W1[:, k, :], d["w1"][k * P:(k + 1) * P, :]).then_inc(s["w"], 16)
                sp.dma_start(b1[:, :], d["b1"][:, :]).then_inc(s["w"], 16)
                sp.dma_start(bd[:, :], d["bd"][:, :]).then_inc(s["w"], 16)
                for k in range(KC):
                    sp.dma_start(Wd[:, k, :], d["wd"][k * P:(k + 1) * P, :]).then_inc(s["w"], 16)

                def body(t, i):
                    n, j = t + 4, (i + 1) % 2
                    if has(n, SORTED):
                        need(sp, s["turned"], n - 1)
                        hold(sp, m)
                        sp.dma_start(Y[:, i, :], d["y_sorted"][bass.ds(n * P, P), :]).then_inc(y_in[i], 16)
                    n = t - 1
                    if has(n, SORTED):
                        sp.wait_ge(s["out"], t)
                        hold(sp, m)
                        sp.dma_start(d["r_tab"][bass.ds(n * P, P), :], R[:, j, :]).then_inc(stored[j], 16)
                    n = t - 2
                    if has(n, SORTED):
                        slot_wait(sp, stored[i], n, 16)
                        sp.sem_inc(s["row_free"], 1)

                pipeline(sp, body, LEAD, 2, SORTED)

            @block.scalar
            def _(act):
                act.wait_ge(s["w"], 16 * LOADS)

                def body(t, i):
                    if has(t, SORTED):
                        need(act, s["made"], t - 1)
                        for c in range(KC):
                            if c % 4 == 0:
                                act.wait_ge(s["hidden"], t * 2 + (c // 4 + 1))
                            act.activation(HT[:, i, c * P:(c + 1) * P], HB[c // 4][:, (c % 4) * P:(c % 4 + 1) * P],
                                           ACT.Gelu, bias=b1[:, c:c + 1]).then_inc(s["gelu"], 1)

                pipeline(act, body, LEAD, 2, SORTED)

            @block.tensor
            def _(pe):
                pe.wait_ge(s["w"], 16 * LOADS)

                def body(t, i):
                    j = (i + 1) % 2
                    if has(t, SORTED):
                        hidden_features(pe, s, YT[:, i, :], W1, HB, s["yT"], t)
                    if has(t - 1, SORTED):
                        e = pe.value_load(m.tile_expert[0:1, bass.ds(t - 1, 1)], min_val=0, max_val=EXPERTS - 1)
                        pe.wait_ge(s["gelu"], t * KC)
                        need(pe, s["out"], t - 2)
                        pe.matmul(RB[j][:, 0:FEAT], m.ones_row[0:1, :], bd[0:1, bass.ds(e * FEAT, FEAT)],
                                  start=True, stop=False)
                        for c in range(KC):
                            mm = pe.matmul(RB[j][:, 0:FEAT], HT[:, j, c * P:(c + 1) * P],
                                           Wd[:, c, bass.ds(e * FEAT, FEAT)], start=False, stop=(c == KC - 1))
                        mm.then_inc(s["made"], 1)
                    n = t + 2
                    if has(n, SORTED):
                        slot_wait(pe, y_in[i], n, 16)
                        need(pe, s["yT"], n - 1)
                        for k in range(2):
                            mm = pe.transpose(T[i][:, k * P:(k + 1) * P], Y[:, i, k * P:(k + 1) * P], m.ident[:, :])
                        mm.then_inc(s["turned"], 1)

                pipeline(pe, body, LEAD, 2, SORTED)

            @block.vector
            def _(dve):
                def body(t, i):
                    j = (i + 1) % 2
                    if has(t - 1, SORTED):
                        dve.wait_ge(s["made"], t)
                        need(dve, s["row_free"], t - 2)
                        dve.tensor_copy(R[:, j, :], RB[j][:, 0:FEAT]).then_inc(s["out"], 1)
                    n = t + 2
                    if has(n, SORTED):
                        dve.wait_ge(s["turned"], n + 1)
                        need(dve, s["hidden"], (n - 1) * 2)
                        dve.tensor_copy(YT[:, i, :], T[i][:, 0:FEAT]).then_inc(s["yT"], 1)

                pipeline(dve, body, LEAD, 2, SORTED)


def project_relations(nc, m, d):
    RH = RELS * HEADS
    COLS = RELS * FEAT + 2 * RH
    with ExitStack() as ctx:
        s = sems(nc, m, "pr", "w a fold folded mm sc_mm h_out sc_out d_out stored0 stored1 rows_free "
                 "staged x2 kept0 kept1 x2_kept link")
        r_in = [new_sem(nc, m, f"pr_r_in{i}") for i in range(2)]
        kept = (s["kept0"], s["kept1"])
        stored = (s["stored0"], s["stored1"])
        sb = lambda nm, sh, dt: ctx.enter_context(nc.sbuf_tensor(f"pr_{nm}", sh, dt))
        f = norm_front(nc, m, ctx, "pr", BLOCKS)
        WX = sb("WX", [P, 2, COLS], F32)
        WN = sb("WN", [P, 2, RELS * FEAT], F32)
        a = sb("a", [P, 4], F32)
        AB = sb("AB", [P, 2, 2 * HEADS], F32)
        R = sb("R", [P, 2, FEAT], F32)
        row_of = sb("row_of", [P, 2], I32)
        H = sb("H", [P, 2, RELS * FEAT], F32)
        SC = sb("SC", [P, 2, RH], F32)
        HP = [ctx.enter_context(nc.psum_tensor(f"pr_H{i}", [P, 512], F32)) for i in range(4)]
        SP_ = [ctx.enter_context(nc.psum_tensor(f"pr_S{i}", [P, 512], F32)) for i in range(2)]
        fold = lambda h, r: SP_[h][:, r * 2 * HEADS:(r + 1) * 2 * HEADS]
        h_rows = d["h_tab"].rearrange("(n r) c -> n (r c)", r=RELS)
        s_rows = d["s_tab"].rearrange("(n r) c -> n (r c)", r=RELS)
        node = lambda t: m.node[:, bass.ds(t * NUMC, FEAT)]
        LEAD = 7
        with nc.Block() as block:

            @block.sync
            def _(sp):
                for k in range(2):
                    sp.dma_start(WX[:, k, 0:RELS * FEAT], d["wr_t"][k * P:(k + 1) * P, :]).then_inc(s["w"], 16)
                    sp.dma_start(WN[:, k, :], d["wr_n"][k * P:(k + 1) * P, :]).then_inc(s["w"], 16)
                sp.dma_start(a[:, :], d["att"][:, :]).then_inc(s["a"], 16)

                def body(t, i):
                    n, j = t + 3, (i + 1) % 2
                    if has(n, BLOCKS):
                        sp.wait_ge(s["x2"], n + 1)
                        hold(sp, m)
                        sp.dma_start(d["x2"][bass.ds(n * P, P), :], node(n)).then_inc(kept[j], 16)
                    if has(t + 2, BLOCKS):
                        slot_wait(sp, kept[i], t + 2, 16)
                        sp.sem_inc(s["x2_kept"], 1)
                    if has(t, BLOCKS):
                        sp.wait_ge(s["sc_out"], t + 1)
                        sp.wait_ge(s["h_out"], t * 4 + 4)
                        hold(sp, m)
                        sp.dma_start(s_rows[bass.ds(t * P, P), :], SC[:, i, :]).then_inc(stored[i], 16)
                        sp.dma_start(h_rows[bass.ds(t * P, P), :], H[:, i, :]).then_inc(stored[i], 16)
                    n, j = t - 1, (i + 1) % 2
                    if has(n, BLOCKS):
                        slot_wait(sp, stored[j], n, 32)
                        sp.sem_inc(s["rows_free"], 1)

                pipeline(sp, body, LEAD, 1, BLOCKS)

            @block.gpsimd
            def _(pool):
                def body(t, i):
                    n = t + 6
                    if has(n, BLOCKS):
                        pool.wait_ge(s["staged"], n + 1)
                        need(pool, s["x2"], n - 1)
                        hold(pool, m)
                        pool.indirect_dma_start(out=R[:, i, :], out_offset=None, in_=d["r_tab"][:, :],
                                                in_offset=bass.IndirectOffsetOnAxis(ap=row_of[:, i:i + 1], axis=0)
                                                ).then_inc(r_in[i], 16)
                    front_scale(pool, m, f, t + 4, i)

                pipeline(pool, body, LEAD, 1, BLOCKS)

            @block.scalar
            def _(act):
                def body(t, i):
                    if has(t, BLOCKS):
                        need(act, s["rows_free"], t - 1)
                        for g in range(4):
                            act.wait_ge(s["mm"], t * 4 + (g + 1))
                            act.copy(H[:, i, g * 512:(g + 1) * 512], HP[g][:, :]).then_inc(s["h_out"], 1)
                    front_copy(act, act.copy, f, t + 2, i, s["mm"], 4)

                pipeline(act, body, LEAD, 1, BLOCKS)

            @block.vector
            def _(dve):
                link = Link(dve, s["link"])
                dve.wait_ge(s["a"], 16)
                for k in range(2):
                    for j in range(2):
                        link(dve.tensor_scalar(AB[:, k, j * HEADS:(j + 1) * HEADS], m.hmask[:, k * HEADS:(k + 1) * HEADS],
                                               a[:, 2 * j + k:2 * j + k + 1], None, ALU.mult))
                dve.wait_ge(s["fold"], 2)
                for h in range(2):
                    for j in range(2):
                        at = RELS * FEAT + j * RH
                        dve.tensor_copy(WX[:, h, at:at + RH].rearrange("p (r h) -> p r h", h=HEADS),
                                        SP_[h][:, 0:2 * RH].rearrange("p (r h) -> p r h", h=2 * HEADS)[
                                            :, :, j * HEADS:(j + 1) * HEADS]).then_inc(s["folded"], 1)

                def body(t, i):
                    j = (i + 1) % 2
                    if has(t + 3, BLOCKS):
                        front_norm(dve, f, node(t + 3), t + 3, j)
                    if has(t + 4, BLOCKS):
                        dve.wait_ge(s["x2"], t + 5)
                        hold(dve, m)
                        front_stats(dve, m, f, node(t + 4), t + 4, i)
                    n = t + 5
                    if has(n, BLOCKS):
                        slot_wait(dve, r_in[j], n, 16)
                        dve.scalar_tensor_tensor(node(n), R[:, j, :], m.prob[:, bass.ds(n, 1)], node(n), ALU.mult,
                                                 ALU.add).then_inc(s["x2"], 1)
                    n = t + 7
                    if has(n, BLOCKS):
                        if has(n - 2, BLOCKS):
                            slot_wait(dve, r_in[j], n - 2, 16)
                        dve.tensor_copy(row_of[:, j:j + 1], m.slot[:, bass.ds(n, 1)]).then_inc(s["staged"], 1)
                    if has(t, BLOCKS):
                        dve.wait_ge(s["sc_mm"], t + 1)
                        need(dve, s["rows_free"], t - 1)
                        dve.tensor_copy(SC[:, i, :], SP_[i][:, 0:RH]).then_inc(s["sc_out"], 1)
                        dve.wait_ge(s["x2_kept"], t + 1)
                        dve.tensor_copy(m.node[:, bass.ds(t * RH, RH)], SP_[i][:, RH:2 * RH]).then_inc(s["d_out"], 1)

                pipeline(dve, body, LEAD, 1, BLOCKS)

            @block.tensor
            def _(pe):
                pe.wait_ge(s["w"], 64)
                pe.wait_ge(s["link"], 4)
                for h in range(2):
                    for r in range(RELS):
                        for k in range(2):
                            mm = pe.matmul(fold(h, r), WN[:, k, r * FEAT + h * P:r * FEAT + (h + 1) * P], AB[:, k, :],
                                           start=(k == 0), stop=(k == 1))
                    mm.then_inc(s["fold"], 1)
                pe.wait_ge(s["folded"], 4)

                def body(t, i):
                    if has(t, BLOCKS):
                        pe.wait_ge(f.s["yT"], t + 1)
                        need(pe, s["sc_out"], t - 1)
                        need(pe, s["d_out"], t - 1)
                        for k in range(2):
                            mm = pe.matmul(SP_[i][:, 0:2 * RH], f.YT[:, i, k * P:(k + 1) * P], WX[:, k, RELS * FEAT:],
                                           start=(k == 0), stop=(k == 1))
                        mm.then_inc(s["sc_mm"], 1)
                        for g in range(4):
                            need(pe, s["h_out"], t * 4 + (g - 3))
                            for k in range(2):
                                mm = pe.matmul(HP[g][:, :], f.YT[:, i, k * P:(k + 1) * P], WX[:, k, g * 512:(g + 1) * 512],
                                               start=(k == 0), stop=(k == 1))
                            mm.then_inc(s["mm"], 1)
                    front_turn(pe, m, f, t + 2, i)

                pipeline(pe, body, LEAD, 1, BLOCKS)


def feed_forward_top2(nc, m, d):
    PER = 22 + EXPERTS
    with ExitStack() as ctx:
        s = sems(nc, m, "moe", "w x_in mixed stats mv eps rstd normed y_turned yT hidden gelu logits shifted powed "
                 "chosen c_turned cT bias_out experts stored result_free link")
        sb = lambda nm, sh, dt: ctx.enter_context(nc.sbuf_tensor(f"moe_{nm}", sh, dt))
        Wr = sb("Wr", [P, 2, EXPERTS], F32)
        W1 = sb("W1", [P, 2, EXPERTS * FEAT], F32)
        b1 = sb("b1", [P, 2 * EXPERTS], F32)
        W2 = sb("W2", [P, 2, EXPERTS * FEAT], F32)
        b2 = sb("b2", [EXPERTS, FEAT], F32)
        X = sb("X", [P, FEAT], F32)
        O = sb("O", [P, FEAT], F32)
        Y = sb("Y", [P, FEAT], F32)
        YT = sb("YT", [P, 2 * P], F32)
        HT = sb("HT", [P, 2 * EXPERTS, P], F32)
        X2 = sb("X2", [P, FEAT], F32)
        st = sb("st", [P, 6], F32)
        mv = sb("mv", [P, 2], F32)
        rstd = sb("rstd", [P, 1], F32)
        r = sb("r", [P, HEADS], F32)
        L = sb("L", [P, EXPERTS], F32)
        best = sb("best", [P, 8], F32)
        idx = sb("idx", [P, 8], U32)
        idx_f = sb("idx_f", [P, 8], F32)
        ex = sb("ex", [P, EXPERTS], F32)
        p = sb("p", [P, 4], F32)
        C = sb("C", [P, EXPERTS], F32)
        C2 = sb("C2", [P, EXPERTS], F32)
        CT = sb("CT", [EXPERTS, P], F32)
        T = ctx.enter_context(nc.psum_tensor("moe_T", [P, 512], F32))
        OUT = ctx.enter_context(nc.psum_tensor("moe_OUT", [P, 512], F32))
        HB = [ctx.enter_context(nc.psum_tensor(f"moe_HB{i}", [P, 512], F32)) for i in range(2)]
        YE = [ctx.enter_context(nc.psum_tensor(f"moe_YE{i}", [P, 512], F32)) for i in range(4)]
        with nc.Block() as block:

            @block.sync
            def _(sp):
                n = 0

                def load(dst, src):
                    nonlocal n
                    n += 1
                    sp.dma_start(dst, src).then_inc(s["w"], 16)

                for k in range(2):
                    load(Wr[:, k, :], d["router"][k * P:(k + 1) * P, :])
                    load(W1[:, k, :], d["m1"][k * P:(k + 1) * P, :])
                    load(W2[:, k, :], d["m2"][k * P:(k + 1) * P, :])
                load(b1[:, :], d["mb1"][:, :])
                load(b2[:, :], d["mb2"][:, :])
                m.moe_loads = n
                with sp.Fori(0, BLOCKS) as it:
                    sp.wait_ge(s["mixed"], it + 1)
                    hold(sp, m)
                    sp.dma_start(X[:, :], d["x2"][bass.ds(it * P, P), :]).then_inc(s["x_in"], 16)
                    sp.wait_ge(s["mixed"], it + 2)
                    hold(sp, m)
                    sp.dma_start(d["out"][bass.ds(it * P, P), :], X2[:, :]).then_inc(s["stored"], 16)
                    sp.wait_ge(s["stored"], it * 16 + 16)
                    sp.sem_inc(s["result_free"], 1)
                sp.wait_ge(s["stored"], 16 * BLOCKS)

            @block.gpsimd
            def _(pool):
                with pool.Fori(0, BLOCKS) as it:
                    pool.wait_ge(s["mv"], it + 1)
                    norm_scale(pool, m, mv[:, :], rstd[:, :], s["eps"], it + 1, s["rstd"])
                    pool.wait_ge(s["shifted"], it + 1)
                    pool.tensor_tensor(ex[:, :], m.e_const[:, :], L[:, :], ALU.pow).then_inc(s["powed"], 1)

            @block.scalar
            def _(act):
                act.wait_ge(s["w"], 16 * m.moe_loads)
                with act.Fori(0, BLOCKS) as it:
                    act.wait_ge(s["y_turned"], it + 1)
                    act.copy(YT[:, :], T[:, 0:2 * P]).then_inc(s["yT"], 1)
                    for c in range(2 * EXPERTS):
                        if c % 4 == 0:
                            act.wait_ge(s["hidden"], it * 4 + (c // 4 + 1))
                        act.activation(HT[:, c, :], HB[(c // 4) % 2][:, (c % 4) * P:(c % 4 + 1) * P], ACT.Gelu,
                                       bias=b1[:, c:c + 1]).then_inc(s["gelu"], 1)
                    act.wait_ge(s["c_turned"], it + 1)
                    act.copy(CT[:, :], T[0:EXPERTS, 0:P]).then_inc(s["cT"], 1)

            @block.tensor
            def _(pe):
                pe.wait_ge(s["w"], 16 * m.moe_loads)
                with pe.Fori(0, BLOCKS) as it:
                    pe.wait_ge(s["normed"], it + 1)
                    for k in range(2):
                        mm = pe.transpose(T[:, k * P:(k + 1) * P], Y[:, k * P:(k + 1) * P], m.ident[:, :])
                    mm.then_inc(s["y_turned"], 1)
                    pe.wait_ge(s["yT"], it + 1)
                    for k in range(2):
                        mm = pe.matmul(OUT[:, FEAT:FEAT + EXPERTS], YT[:, k * P:(k + 1) * P], Wr[:, k, :],
                                       start=(k == 0), stop=(k == 1))
                    mm.then_inc(s["logits"], 1)
                    for g in range(4):
                        if g >= 2:
                            pe.wait_ge(s["gelu"], it * 16 + (4 * g - 4))
                        for c in range(4 * g, 4 * g + 4):
                            for k in range(2):
                                mm = pe.matmul(HB[g % 2][:, (c % 4) * P:(c % 4 + 1) * P], W1[:, k, c * P:(c + 1) * P],
                                               YT[:, k * P:(k + 1) * P], start=(k == 0), stop=(k == 1))
                        mm.then_inc(s["hidden"], 1)
                    for e in range(EXPERTS):
                        pe.wait_ge(s["gelu"], it * 16 + (2 * e + 2))
                        for k in range(2):
                            mm = pe.matmul(YE[e // 2][:, (e % 2) * FEAT:(e % 2 + 1) * FEAT], HT[:, 2 * e + k, :],
                                           W2[:, k, e * FEAT:(e + 1) * FEAT], start=(k == 0), stop=(k == 1))
                    mm.then_inc(s["experts"], 1)
                    pe.wait_ge(s["chosen"], it + 1)
                    pe.transpose(T[0:EXPERTS, 0:P], C[:, :], m.ident[:, :]).then_inc(s["c_turned"], 1)
                    pe.wait_ge(s["cT"], it + 1)
                    pe.matmul(OUT[:, 0:FEAT], CT[:, :], b2[:, :], start=True, stop=True).then_inc(s["bias_out"], 1)

            @block.vector
            def _(dve):
                dve.sem_inc(s["mixed"], 1)
                dve.sem_inc(s["result_free"], 1)
                with dve.Fori(0, BLOCKS) as it:
                    link = LoopLink(dve, s["link"], it, PER)
                    node = m.node[:, bass.ds(it * NUMC, NUMC)]
                    link(dve.tensor_scalar(r[:, :], node[:, FEAT:NUMC], 1e-12, None, ALU.add))
                    link(dve.reciprocal(r[:, :], r[:, :]))
                    link(dve.tensor_tensor(O[:, :].rearrange("p (h c) -> p h c", c=DH), node[:, 0:FEAT].rearrange("p (h c) -> p h c", c=DH),
                                           r[:, :].unsqueeze(2).to_broadcast([P, HEADS, DH]), ALU.mult))
                    dve.wait_ge(s["x_in"], it * 16 + 16)
                    link(dve.tensor_tensor(X[:, :], X[:, :], O[:, :], ALU.add))
                    norm_stats(dve, m, X[:, :], st[:, :], mv[:, :], s["stats"], it + 1, s["mv"])
                    dve.wait_ge(s["rstd"], it + 1)
                    dve.tensor_scalar(Y[:, :], X[:, :], mv[:, 0:1], rstd[:, :], ALU.subtract, ALU.mult).then_inc(s["normed"], 1)
                    dve.wait_ge(s["logits"], it + 1)
                    link(dve.tensor_copy(L[:, :], OUT[:, FEAT:FEAT + EXPERTS]))
                    link(dve.tensor_reduce(p[:, 0:1], L[:, :], AX.X, ALU.max))
                    link(dve.tensor_scalar(L[:, :], L[:, :], p[:, 0:1], None, ALU.subtract))
                    dve.sem_inc(s["shifted"], 1)
                    dve.wait_ge(s["powed"], it + 1)
                    link(dve.tensor_reduce(p[:, 1:2], ex[:, :], AX.X, ALU.add))
                    link(dve.reciprocal(p[:, 1:2], p[:, 1:2]))
                    link(dve.tensor_scalar(ex[:, :], ex[:, :], p[:, 1:2], None, ALU.mult))
                    top_experts(dve, m, s, it, ex[:, :], best[:, :], idx[:, :], idx_f[:, :], link)
                    link(dve.tensor_tensor(p[:, 2:3], best[:, 0:1], best[:, 1:2], ALU.add))
                    link(dve.tensor_scalar(p[:, 2:3], p[:, 2:3], 1e-12, None, ALU.max))
                    link(dve.reciprocal(p[:, 3:4], p[:, 2:3]))
                    link(dve.tensor_scalar(C[:, :], m.iota_f[:, 0:EXPERTS], idx_f[:, 0:1], best[:, 0:1], ALU.is_equal, ALU.mult))
                    link(dve.tensor_scalar(C2[:, :], m.iota_f[:, 0:EXPERTS], idx_f[:, 1:2], best[:, 1:2], ALU.is_equal, ALU.mult))
                    link(dve.tensor_tensor(C[:, :], C[:, :], C2[:, :], ALU.add))
                    link(dve.tensor_scalar(C[:, :], C[:, :], p[:, 3:4], None, ALU.mult))
                    dve.sem_inc(s["chosen"], 1)
                    link(dve.tensor_tensor(Y[:, :], Y[:, :], X[:, :], ALU.add))
                    dve.wait_ge(s["bias_out"], it + 1)
                    dve.wait_ge(s["result_free"], it + 1)
                    link(dve.tensor_tensor(X2[:, :], Y[:, :], OUT[:, 0:FEAT], ALU.add))
                    dve.wait_ge(s["experts"], it + 1)
                    for e in range(EXPERTS):
                        link(dve.scalar_tensor_tensor(X2[:, :], YE[e // 2][:, (e % 2) * FEAT:(e % 2 + 1) * FEAT],
                                                      C[:, e:e + 1], X2[:, :], ALU.mult, ALU.add))
                    dve.sem_inc(s["mixed"], 1)
                    assert link.n == PER


def program(nc, d):
    with ExitStack() as ctx:
        m = Shared()
        shared(nc, ctx, m)
        constants(nc, m)
        end_phase(nc, m)
        merge_path(nc, m, d)
        end_phase(nc, m)
        segment_starts(nc, m, d)
        end_phase(nc, m)
        m.node = ctx.enter_context(nc.sbuf_tensor("node", [P, BLOCKS * NUMC], F32))
        with ExitStack() as layer:
            S = layer.enter_context(nc.sbuf_tensor("S0", [P, SPAD * HEADS], F32))
            edge_bias(nc, m, d, S)
            end_phase(nc, m)
            project_attention(nc, m, d)
            end_phase(nc, m)
            scores_attention(nc, m, d, S)
            end_phase(nc, m)
            segment_softmax(nc, m, S, -1e38, "seg0")
            end_phase(nc, m)
            aggregate(nc, m, S, d["v_tab"], m.idx_src, "attn")
            end_phase(nc, m)
        with ExitStack() as routes:
            sb = lambda nm, sh, dt: routes.enter_context(nc.sbuf_tensor(nm, sh, dt))
            m.logits = sb("logits", [P, BLOCKS * EXPERTS], F32)
            m.prob = sb("prob", [P, BLOCKS], F32)
            m.slot = sb("slot", [P, BLOCKS], I32)
            m.tile_expert = sb("tile_expert", [1, SORTED], I32)
            attend_and_route(nc, m, d)
            end_phase(nc, m)
            sort_by_expert(nc, m, d)
            end_phase(nc, m)
            scatter_rows(nc, m, d)
            end_phase(nc, m)
            expert_of_sorted(nc, m, d)
            end_phase(nc, m)
            project_relations(nc, m, d)
            end_phase(nc, m)
        with ExitStack() as layer:
            S = layer.enter_context(nc.sbuf_tensor("S1", [P, SPAD * HEADS], F32))
            scores_relational(nc, m, d, S)
            end_phase(nc, m)
            segment_softmax(nc, m, S, 0.0, "seg1")
            end_phase(nc, m)
            aggregate(nc, m, S, d["h_tab"], m.idx_rel, "relagg")
            end_phase(nc, m)
        feed_forward_top2(nc, m, d)


def by_partition(w):
    return w.reshape(-1, P, w.shape[-1]).transpose(1, 0, 2).reshape(P, -1)


LAYOUT = {
    "wqkv": lambda g: stacked([g["L0_gnn_Wq"].T, g["L0_gnn_Wk"].T, g["L0_gnn_Wv"].T]),
    "wo": lambda g: g["L0_gnn_Wo"].T,
    "w1": lambda g: g["L0_ffn_W1"],
    "b1": lambda g: g["L0_ffn_b1"].reshape(HID // P, P).T,
    "wg": lambda g: by_partition(g["L0_ffn_Wg"]),
    "bg": lambda g: g["L0_ffn_bg"].reshape(1, -1),
    "wd": lambda g: g["L0_ffn_Wd"].transpose(1, 0, 2).reshape(HID, EXPERTS * FEAT),
    "bd": lambda g: g["L0_ffn_bd"].reshape(1, -1),
    "wr_t": lambda g: g["L1_gnn_W"].transpose(2, 0, 1).reshape(FEAT, RELS * FEAT),
    "wr_n": lambda g: g["L1_gnn_W"].transpose(1, 0, 2).reshape(FEAT, RELS * FEAT),
    "att": lambda g: stacked([g["L1_gnn_attn_src"].reshape(2, P).T, g["L1_gnn_attn_dst"].reshape(2, P).T]),
    "router": lambda g: g["L1_ffn_router_w"].T,
    "m1": lambda g: g["L1_ffn_w1"].transpose(1, 0, 2).reshape(FEAT, EXPERTS * FEAT),
    "mb1": lambda g: g["L1_ffn_b1"].reshape(EXPERTS * 2, P).T,
    "m2": lambda g: g["L1_ffn_w2"].transpose(1, 0, 2).reshape(FEAT, EXPERTS * FEAT),
    "mb2": lambda g: g["L1_ffn_b2"],
}


def stacked(parts):
    import numpy as _np
    return _np.concatenate(parts, axis=1)


SCRATCH = {
    "jf": ((SGROUPS, P), F32),
    "ji": ((SGROUPS, P), I32),
    "dst_steps": ((1, (CHUNKS + 1) * CLEN), I32),
    "k_tab": ((NPAD, FEAT), F32),
    "v_tab": ((NPAD, FEAT), F32),
    "x2": ((NPAD, FEAT), F32),
    "y_tab": ((NPAD, FEAT), F32),
    "y_sorted": ((SORTED * P, FEAT), F32),
    "r_tab": ((SORTED * P, FEAT), F32),
    "h_tab": ((NPAD * RELS, FEAT), F32),
    "s_tab": ((NPAD * RELS, HEADS), F32),
}
OUTS = {"out": ((NPAD, FEAT), F32)}


def kernel(**inputs):
    import numpy as _np
    import concourse.bacc as _bacc
    from concourse import mybir as _mybir
    from concourse.bass_utils import run_bass_kernel_spmd as _run

    def rows(a, n, fill=0):
        out = _np.full((n,) + a.shape[1:], fill, a.dtype)
        out[:a.shape[0]] = a
        return out

    g = {k: _np.asarray(v) for k, v in inputs.items()}
    arrays = {
        "x": rows(g["x"], NPAD),
        "src": rows(g["src"], TROWS * P).reshape(TROWS, P),
        "dst": rows(g["dst"], TROWS * P, PAD_NODE).reshape(TROWS, P),
        "typ": rows(g["edge_type_8"], TROWS * P).reshape(TROWS, P),
        "attr": rows(g["edge_attr_8"], TROWS * P).reshape(TROWS, P * HEADS),
    }
    for k, v in LAYOUT.items():
        arrays[k] = _np.ascontiguousarray(v(g))
    nc = _bacc.Bacc("TRN2", target_bir_lowering=False, num_devices=1)
    dram = {k: nc.dram_tensor(f"in_{k}", a.shape, _mybir.dt.from_np(a.dtype), kind="ExternalInput").ap()
            for k, a in arrays.items()}
    for k, (shape, dt) in SCRATCH.items():
        dram[k] = nc.dram_tensor(k, shape, dt, kind="Internal").ap()
    for k, (shape, dt) in OUTS.items():
        dram[k] = nc.dram_tensor(k, shape, dt, kind="ExternalOutput").ap()
    program(nc, dram)
    r = _run(nc, [{f"in_{k}": a for k, a in arrays.items()}], core_ids=[0])
    return r.results[0]["out"][:N]
```

```python
from contextlib import ExitStack

import concourse.bass as bass
from concourse import mybir

ALU = mybir.AluOpType
ACT = mybir.ActivationFunctionType
AX = mybir.AxisListType
F32 = mybir.dt.float32
BF16 = mybir.dt.bfloat16
I32 = mybir.dt.int32
U32 = mybir.dt.uint32

P = 128
N, FEAT, HEADS = 6250, 256, 8
DH = FEAT // HEADS
E = 100000
RELS = 8
EXPERTS = 8
HID = 1024
BLOCKS = 50
NPAD = BLOCKS * P
LAST_BLOCK = (N - 1) // P
PAD_NODE = LAST_BLOCK * P + P - 1
TILES = -(-E // P)
TROWS = TILES + 1
IT = 16
CHUNKS = 16
STEPS = -(-(TILES + LAST_BLOCK) // IT) * IT
ITS = STEPS // IT
SPAD = STEPS + IT
CS = SPAD // CHUNKS
SGROUPS = -(-SPAD // P)
CLEN = CS * P
assert CS * CHUNKS == SPAD
BIG = 1e30
SORTED = (NPAD + EXPERTS * (P - 1)) // P
SORTED += SORTED % 2
PACK = 64
assert BLOCKS <= PACK and PACK ** 4 <= 2 ** 24
QSCALE = float(DH) ** 0.5
LN_EPS = 1e-5
NUMC = FEAT + HEADS


class Shared:
    pass


def new_sem(nc, m, name):
    m.phase_sems.append(nc.alloc_semaphore(name=name))
    return m.phase_sems[-1]


def end_phase(nc, m):
    nc.clear_and_free_semaphores(m.phase_sems)
    m.phase_sems = []
    nc.all_engine_barrier()


def sems(nc, m, prefix, names):
    return {n: new_sem(nc, m, f"{prefix}_{n}") for n in names.split()}


def hold(eng, m):
    eng.sem_inc(m.passed, 1)


class Link:

    def __init__(self, eng, sem):
        self.eng, self.sem, self.n = eng, sem, 0

    def __call__(self, ins):
        self.n += 1
        ins.then_inc(self.sem, 1)
        self.eng.wait_ge(self.sem, self.n)


def constants(nc, m):
    with ExitStack() as ctx:
        s = sems(nc, m, "const", "raw pool link")
        tmp = ctx.enter_context(nc.sbuf_tensor("const_i", [P, 128], I32))
        hm = ctx.enter_context(nc.sbuf_tensor("const_h", [P, 16], I32))
        hf = ctx.enter_context(nc.sbuf_tensor("const_hf", [P, 16], F32))
        block = ctx.enter_context(nc.Block())

        @block.gpsimd
        def _(pool):
            link = Link(pool, s["pool"])
            link(pool.memset(m.ident[:, :], 0.0))
            link(pool.affine_select(out=m.ident[:, :], in_=m.ident[:, :], compare_op=ALU.not_equal, fill=1.0,
                                    base=0, pattern=[[-1, 128]], channel_multiplier=1))
            pool.iota(tmp[:, :], pattern=[[1, 128]], base=0, channel_multiplier=0).then_inc(s["raw"], 1)
            pool.iota(hm[:, :], pattern=[[128, 2], [-DH, 8]], base=0, channel_multiplier=1).then_inc(s["raw"], 1)
            pool.memset(m.e_const[:, :], 2.718281828459045)
            pool.memset(m.mhalf[:, :], -0.5)
            link(pool.memset(m.ones_row[:, :], 1.0))

        @block.vector
        def _(dve):
            link = Link(dve, s["link"])
            dve.wait_ge(s["raw"], 2)
            dve.wait_ge(s["pool"], 2)
            dve.tensor_copy(m.iota_f[:, :], tmp[:, :])
            dve.tensor_copy(m.ident_b[:, :], m.ident[:, :])
            link(dve.tensor_copy(hf[:, :], hm[:, :]))
            link(dve.tensor_scalar(m.hmask[:, :], hf[:, :], -0.5, None, ALU.is_gt))
            link(dve.tensor_scalar(hf[:, :], hf[:, :], DH - 0.5, None, ALU.is_lt))
            link(dve.tensor_tensor(m.hmask[:, :], m.hmask[:, :], hf[:, :], ALU.mult))


def merge_path(nc, m, d):
    with ExitStack() as ctx:
        s = sems(nc, m, "path", "load pool link rows psb jt jtc jout g0 g1 g2 gt gc sent end")
        sb = lambda n, sh, dt: ctx.enter_context(nc.sbuf_tensor(f"path_{n}", sh, dt))
        last_i = sb("last_i", [1, TILES], I32)
        last_f = sb("last_f", [1, TILES], F32)
        tile_i = sb("tile_i", [1, TILES], I32)
        tile_f = sb("tile_f", [1, TILES], F32)
        step_i = sb("step_i", [P, SGROUPS], I32)
        step_f = sb("step_f", [P, SGROUPS], F32)
        ends = sb("ends", [P, TILES], F32)
        less = sb("less", [P, TILES], F32)
        tsel = sb("tsel", [P, SGROUPS], F32)
        bsel = sb("bsel", [P, SGROUPS], F32)
        tsel_i = m.tile_of_step
        jt = sb("jt", [SGROUPS, P], F32)
        jti = sb("jti", [SGROUPS, P], I32)
        pack = sb("pack", [SGROUPS, P // 4], F32)
        pack_i = sb("pack_i", [SGROUPS, P // 4], I32)
        sent = sb("sent", [1, 2], I32)
        raw = [sb(f"raw{i}", [P, SGROUPS, P], I32) for i in range(3)]
        rawf = [sb(f"rawf{i}", [P, SGROUPS, P], F32) for i in range(3)]
        pend = ctx.enter_context(nc.psum_tensor("path_pend", [P, 2, 512], F32))
        pjt = ctx.enter_context(nc.psum_tensor("path_pjt", [SGROUPS, P], F32))
        half = TILES // 2
        tables = (d["src"], d["dst"], d["typ"])
        path = ctx.enter_context(ExitStack())
        block = path.enter_context(nc.Block())

        @block.sync
        def _(sp):
            with nc.allow_non_contiguous_dma(reason="one column of the tiles' destinations"):
                sp.dma_start(last_i[:, :], d["dst"][0:TILES, P - 1:P].rearrange("t o -> o t")).then_inc(s["load"], 16)
            sp.wait_ge(s["jtc"], 1)
            sp.dma_start(d["jf"][:, :], jt[:, :]).then_inc(s["jout"], 16)
            sp.dma_start(d["ji"][:, :], jti[:, :]).then_inc(s["jout"], 16)
            sp.dma_start(d["jp"][:, :], pack_i[:, :]).then_inc(s["jout"], 16)
            sp.wait_ge(s["g1"], 16 * SGROUPS)
            sp.wait_ge(s["sent"], 1)
            for k in range(SGROUPS):
                rows = min(P, SPAD - k * P)
                sp.dma_start(d["dst_steps"][0:1, 1 + k * P * P:1 + (k * P + rows) * P].rearrange(
                    "o (p e) -> (o p) e", e=P), raw[1][0:rows, k, :]).then_inc(s["end"], 16)
            sp.dma_start(d["dst_steps"][0:1, 0:1], sent[0:1, 0:1]).then_inc(s["end"], 16)
            sp.dma_start(d["dst_steps"][0:1, 1 + SPAD * P:2 + SPAD * P], sent[0:1, 1:2]).then_inc(s["end"], 16)
            sp.wait_ge(s["jout"], 48)
            sp.dma_start(m.jquad[0:1, :], d["jp"].rearrange("k p -> (k p)")[0:SPAD // 4].rearrange("(o s) -> o s", o=1)).then_inc(s["end"], 16)
            sp.dma_start(m.jrow[0:1, :], d["ji"].rearrange("k p -> (k p)")[0:SPAD].rearrange("(o s) -> o s", o=1)).then_inc(s["end"], 16)
            sp.dma_start(m.jb[:, :], d["jf"].rearrange("k p -> (k p)")[0:SPAD].rearrange("(o s) -> o s", o=1).to_broadcast([P, SPAD])).then_inc(s["end"], 16)
            sp.wait_ge(s["end"], 16 * (SGROUPS + 5))

        @block.gpsimd
        def _(pool):
            pool.iota(tile_i[:, :], pattern=[[1, TILES]], base=0, channel_multiplier=0).then_inc(s["pool"], 1)
            pool.iota(step_i[:, :], pattern=[[P, SGROUPS]], base=0, channel_multiplier=1).then_inc(s["pool"], 1)
            pool.wait_ge(s["rows"], 1)
            for t, table in enumerate(tables):
                for k in range(SGROUPS):
                    pool.indirect_dma_start(
                        out=raw[t][:, k, :], out_offset=None, in_=table[:, :],
                        in_offset=bass.IndirectOffsetOnAxis(ap=tsel_i[:, k:k + 1], axis=0)).then_inc((s["g0"], s["g1"], s["g2"])[t], 16)

        @block.vector
        def _(dve):
            link = Link(dve, s["link"])
            dve.memset(sent[0:1, 0:1], -1)
            dve.memset(sent[0:1, 1:2], 1 << 20).then_inc(s["sent"], 1)
            dve.wait_ge(s["load"], 16)
            dve.wait_ge(s["pool"], 2)
            link(dve.tensor_scalar(last_i[:, :], last_i[:, :], 7, None, ALU.arith_shift_right))
            link(dve.tensor_copy(last_f[:, :], last_i[:, :]))
            link(dve.tensor_copy(tile_f[:, :], tile_i[:, :]))
            link(dve.tensor_copy(step_f[:, :], step_i[:, :]))
            dve.tensor_tensor(last_f[:, :], last_f[:, :], tile_f[:, :], ALU.add).then_inc(s["psb"], 1)
            dve.wait_ge(s["psb"], 2)
            for c in range(2):
                link(dve.tensor_copy(ends[:, c * half:(c + 1) * half], pend[:, c, 0:half]))
            for k in range(SGROUPS):
                link(dve.tensor_scalar(less[:, :], ends[:, :], step_f[:, k:k + 1], 0.0, ALU.is_lt, ALU.add,
                                       accum_out=tsel[:, k:k + 1]))
            link(dve.tensor_tensor(bsel[:, :], step_f[:, :], tsel[:, :], ALU.subtract))
            link(dve.tensor_scalar(bsel[:, :], bsel[:, :], float(LAST_BLOCK), None, ALU.min))
            dve.tensor_copy(tsel_i[:, :], tsel[:, :]).then_inc(s["rows"], 1)
            dve.wait_ge(s["jt"], 1)
            link(dve.tensor_copy(jt[:, :], pjt[:, :]))
            link(dve.tensor_copy(jti[:, :], jt[:, :]))
            of = lambda i: jt[:, :].rearrange("k (q i) -> k q i", i=4)[:, :, i]
            link(dve.tensor_copy(pack[:, :], of(3)))
            for i in (2, 1, 0):
                link(dve.scalar_tensor_tensor(pack[:, :], pack[:, :], float(PACK), of(i), ALU.mult, ALU.add))
            dve.tensor_copy(pack_i[:, :], pack[:, :]).then_inc(s["jtc"], 1)
            for t, g in enumerate((s["g0"], s["g1"], s["g2"])):
                dve.wait_ge(g, 16 * SGROUPS)
                link(dve.tensor_copy(rawf[t][:, :, :], raw[t][:, :, :]))

        @block.tensor
        def _(pe):
            pe.wait_ge(s["psb"], 1)
            for c in range(2):
                mm = pe.matmul(pend[:, c, 0:half], m.ones_row[0:1, :], last_f[0:1, c * half:(c + 1) * half],
                               start=True, stop=True)
            mm.then_inc(s["psb"], 1)
            pe.wait_ge(s["rows"], 1)
            pe.transpose(pjt[:, :], bsel[:, :], m.ident[:, :]).then_inc(s["jt"], 1)

        path.close()

        ctx2 = ctx.enter_context(ExitStack())
        t = sems(nc, m, "turn", "tp tc link dve")
        pt = [ctx2.enter_context(nc.psum_tensor(f"turn_p{i}", [P, 512], F32)) for i in range(4)]
        typf = ctx2.enter_context(nc.sbuf_tensor("turn_typ", [P, SGROUPS * P], F32))
        srcf = ctx2.enter_context(nc.sbuf_tensor("turn_src", [P, SGROUPS * P], F32))
        dstf = ctx2.enter_context(nc.sbuf_tensor("turn_dst", [P, SGROUPS * P], F32))
        block2 = ctx2.enter_context(nc.Block())
        outs = (srcf, dstf, typf)

        @block2.tensor
        def _(pe):
            for i in range(3 * SGROUPS):
                if i >= 4:
                    pe.wait_ge(t["tc"], i - 3)
                pe.transpose(pt[i % 4][:, 0:P], rawf[i // SGROUPS][:, i % SGROUPS, :], m.ident[:, :]).then_inc(t["tp"], 1)

        @block2.vector
        def _(dve):
            for i in range(3 * SGROUPS):
                dve.wait_ge(t["tp"], i + 1)
                k = i % SGROUPS
                dve.tensor_copy(outs[i // SGROUPS][:, k * P:(k + 1) * P], pt[i % 4][:, 0:P]).then_inc(t["tc"], 1)
            dve.wait_ge(t["tc"], 3 * SGROUPS)
            link = Link(dve, t["link"])
            dve.tensor_copy(m.idx_src[:, :], srcf[:, 0:SPAD])
            link(dve.scalar_tensor_tensor(srcf[:, 0:SPAD], srcf[:, 0:SPAD], float(RELS), typf[:, 0:SPAD], ALU.mult, ALU.add))
            dve.tensor_copy(m.idx_rel[:, :], srcf[:, 0:SPAD])
            link(dve.scalar_tensor_tensor(m.dst_in[:, :], m.jb[:, :], -float(P), dstf[:, 0:SPAD], ALU.mult, ALU.add))
            link(dve.tensor_scalar(m.outside[:, :], m.dst_in[:, :], -0.5, -BIG, ALU.is_lt, ALU.mult))
            link(dve.tensor_scalar(dstf[:, 0:SPAD], m.dst_in[:, :], P - 0.5, -BIG, ALU.is_gt, ALU.mult))
            link(dve.tensor_tensor(m.outside[:, :], m.outside[:, :], dstf[:, 0:SPAD], ALU.add))
            tm = m.relmask[:, :].rearrange("p (s r) -> p s r", r=RELS)
            for r in range(RELS):
                link(dve.tensor_scalar(tm[:, :, r], typf[:, 0:SPAD], float(r), None, ALU.is_equal))


def segment_starts(nc, m, d):
    with ExitStack() as ctx:
        s = sems(nc, m, "starts", "load link")
        ids = ctx.enter_context(nc.sbuf_tensor("starts_ids", [P, CLEN + 2], I32))
        edge = ctx.enter_context(nc.sbuf_tensor("starts_edge", [1, 3, CHUNKS], I32))
        edgef = ctx.enter_context(nc.sbuf_tensor("starts_edgef", [1, 2, CHUNKS], F32))
        flat = d["dst_steps"].rearrange("o n -> (o n)")
        with nc.Block() as block:

            @block.sync
            def _(sp):
                chunks = flat[0:CHUNKS * CLEN].rearrange("(c n) -> c n", c=CHUNKS)
                after = flat[CLEN:(CHUNKS + 1) * CLEN].rearrange("(c n) -> c n", c=CHUNKS)[:, 0:2]
                for h in range(HEADS):
                    rows = slice(h * CHUNKS, (h + 1) * CHUNKS)
                    sp.dma_start(ids[rows, 0:CLEN], chunks).then_inc(s["load"], 16)
                    sp.dma_start(ids[rows, CLEN:CLEN + 2], after).then_inc(s["load"], 16)
                with nc.allow_non_contiguous_dma(reason="one destination per chunk"):
                    for i, first in enumerate((0, 1, CLEN)):
                        sp.dma_start(edge[0:1, i, :], flat[first:first + (CHUNKS - 1) * CLEN + 1:CLEN].rearrange(
                            "(o n) -> o n", o=1)).then_inc(s["load"], 16)
                sp.wait_ge(s["load"], 16 * (2 * HEADS + 3))

            @block.vector
            def _(dve):
                link = Link(dve, s["link"])
                dve.wait_ge(s["load"], 16 * (2 * HEADS + 3))
                link(dve.tensor_tensor(m.starts[:, :], ids[:, 1:CLEN + 2], ids[:, 0:CLEN + 1], ALU.not_equal))
                link(dve.tensor_scalar(m.starts[:, :], m.starts[:, :], -BIG, None, ALU.mult))
                link(dve.tensor_tensor(edgef[:, 0, :], edge[:, 0, :], edge[:, 2, :], ALU.not_equal))
                link(dve.memset(edgef[:, 1, :], 1.0))
                link(dve.tensor_tensor(edgef[:, 1, 0:CHUNKS - 1], edge[:, 1, 0:CHUNKS - 1], edge[:, 1, 1:CHUNKS],
                                       ALU.not_equal))
                for i, chain in enumerate((m.chain_fwd, m.chain_bwd)):
                    for h in range(HEADS):
                        link(dve.tensor_scalar(chain[:, h * CHUNKS:(h + 1) * CHUNKS], edgef[:, i, :], -BIG, None, ALU.mult))


def by_head(S):
    return S[:, :].rearrange("p (h s) -> p h s", h=HEADS)


def edge_bias(nc, m, d, S):
    with ExitStack() as ctx:
        s = sems(nc, m, "bias", "pool load link tsel g0 g1 tp tc")
        rows = ctx.enter_context(nc.sbuf_tensor("bias_rows", [P, 2, P * HEADS], F32))
        pt = [ctx.enter_context(nc.psum_tensor(f"bias_p{i}", [P, 4, P], F32)) for i in range(4)]
        Sv = by_head(S)
        n_groups = 2 * SGROUPS
        with nc.Block() as block:

            @block.gpsimd
            def _(pool):
                for k in range(SGROUPS):
                    if k >= 2:
                        pool.wait_ge(s["tp"], 2 * (k - 1))
                    pool.indirect_dma_start(out=rows[:, k % 2, :], out_offset=None, in_=d["attr"][:, :],
                                            in_offset=bass.IndirectOffsetOnAxis(ap=m.tile_of_step[:, k:k + 1], axis=0)
                                            ).then_inc((s["g0"], s["g1"])[k % 2], 16)

            @block.vector
            def _(dve):
                for g in range(n_groups):
                    k, hh = g // 2, g % 2
                    cols = min(P, SPAD - k * P)
                    dve.wait_ge(s["tp"], g + 1)
                    dve.tensor_tensor(Sv[:, 4 * hh:4 * hh + 4, k * P:k * P + cols], pt[g % 4][:, :, 0:cols],
                                      m.outside[:, k * P:k * P + cols].unsqueeze(1).to_broadcast([P, 4, cols]),
                                      ALU.add).then_inc(s["tc"], 1)

            @block.tensor
            def _(pe):
                for g in range(n_groups):
                    k, hh = g // 2, g % 2
                    pe.wait_ge((s["g0"], s["g1"])[k % 2], 16 * (k // 2 + 1))
                    if g >= 4:
                        pe.wait_ge(s["tc"], g - 3)
                    for h in range(4):
                        mm = pe.transpose(pt[g % 4][:, h, :],
                                          rows[:, k % 2, :].rearrange("p (e h) -> p e h", h=HEADS)[:, :, 4 * hh + h],
                                          m.ident[:, :])
                    mm.then_inc(s["tp"], 1)


def shared(nc, ctx, m):
    sb = lambda n, sh, dt: ctx.enter_context(nc.sbuf_tensor(n, sh, dt))
    m.phase_sems = []
    m.passed = ctx.enter_context(nc.semaphore("passed"))
    m.ident = sb("ident", [P, P], F32)
    m.ident_b = sb("ident_b", [P, P], BF16)
    m.iota_f = sb("iota_f", [P, P], F32)
    m.ones_row = sb("ones_row", [1, P], F32)
    m.e_const = sb("e_const", [P, HEADS], F32)
    m.mhalf = sb("mhalf", [P, 1], F32)
    m.hmask = sb("hmask", [P, 16], F32)
    m.tile_of_step = sb("tile_of_step", [P, SGROUPS], I32)
    m.jrow = sb("jrow", [1, SPAD], I32)
    m.jquad = sb("jquad", [1, SPAD // 4], I32)
    m.jb = sb("jb", [P, SPAD], F32)
    m.idx_src = sb("idx_src", [P, SPAD], I32)
    m.idx_rel = sb("idx_rel", [P, SPAD], I32)
    m.dst_in = sb("dst_in", [P, SPAD], F32)
    m.outside = sb("outside", [P, SPAD], F32)
    m.relmask = sb("relmask", [P, SPAD * RELS], BF16)
    m.starts = sb("starts", [P, CLEN + 1], BF16)
    m.chain_fwd = sb("chain_fwd", [1, P], F32)
    m.chain_bwd = sb("chain_bwd", [1, P], F32)


def stage_half(act, stage, idx, staged, gathered, it, h):
    for sem, value in gathered:
        act.wait_ge(sem, value)
    act.copy(stage[:, 8 * h:8 * h + 8], idx[:, bass.ds(it * IT + (IT + 8 * h), 8)]).then_inc(staged, 1)


def scores_attention(nc, m, d, S):
    PAIRS = IT // 2
    with ExitStack() as ctx:
        s = sems(nc, m, "dot", "staged pair_used masks turned turned_sb q_rows summed added")
        k_in = [new_sem(nc, m, f"dot_k_in{i}") for i in range(8)]
        sb = lambda nm, sh, dt: ctx.enter_context(nc.sbuf_tensor(f"dot_{nm}", sh, dt))
        K = sb("K", [P, 8, FEAT], F32)
        stage = sb("stage", [P, IT], I32)
        OH = sb("OH", [P, IT, P], BF16)
        OHT = sb("OHT", [P, IT, P], F32)
        prod = sb("prod", [P, 2, 2 * FEAT], F32)
        ST = sb("ST", [P, IT * HEADS], F32)
        TP = [ctx.enter_context(nc.psum_tensor(f"dot_TP{i}", [P, 1024], BF16)) for i in range(2)]
        QP = [ctx.enter_context(nc.psum_tensor(f"dot_QP{i}", [P, 2 * FEAT], F32)) for i in range(4)]

        with nc.Block() as block:

            @block.gpsimd
            def _(pool):
                with pool.Fori(0, ITS) as it:
                    for u in range(IT):
                        if u % 8 == 0:
                            pool.wait_ge(s["staged"], it * 2 + (u // 8 + 1))
                        if u % 2 == 0:
                            pool.wait_ge(s["pair_used"], it * PAIRS + (u // 2 + 1))
                        if u % 2 == 0:
                            hold(pool, m)
                        pool.indirect_dma_start(out=K[:, u % 8, :], out_offset=None, in_=d["k_tab"][:, :],
                                                in_offset=bass.IndirectOffsetOnAxis(ap=stage[:, u:u + 1], axis=0)
                                                ).then_inc(k_in[u % 8], 16)

            @block.scalar
            def _(act):
                def to_sbuf(quad, slot):
                    act.wait_ge(s["turned"], quad + 1)
                    act.copy(OHT[:, 4 * slot:4 * slot + 4, :].rearrange("p a b -> p (a b)"),
                             TP[slot % 2][:, 0:512]).then_inc(s["turned_sb"], 1)

                for h in range(2):
                    act.copy(stage[:, 8 * h:8 * h + 8], m.idx_src[:, 8 * h:8 * h + 8]).then_inc(s["staged"], 1)
                for q in range(4):
                    to_sbuf(q, q)
                with act.Fori(0, ITS) as it:
                    for q in range(4):
                        act.wait_ge(s["q_rows"], it * PAIRS + (2 * q + 2))
                        to_sbuf(it * 4 + (4 + q), q)
                        if q % 2 == 1:
                            stage_half(act, stage, m.idx_src, s["staged"],
                                       [(k, it * 32 + 16 * (q // 2 + 1)) for k in k_in], it, q // 2)

            @block.tensor
            def _(pe):
                def turn(quad, slot):
                    pe.wait_ge(s["masks"], quad + 1)
                    for i in range(4):
                        mm = pe.transpose(TP[slot % 2][:, i * P:(i + 1) * P], OH[:, 4 * slot + i, :], m.ident_b[:, :])
                    mm.then_inc(s["turned"], 1)

                for q in range(4):
                    if q >= 2:
                        pe.wait_ge(s["turned_sb"], q - 1)
                    turn(q, q)
                with pe.Fori(0, ITS) as it:
                    for q in range(4):
                        pe.wait_ge(s["turned_sb"], it * 4 + (q + 1))
                        for v in (2 * q, 2 * q + 1):
                            pe.wait_ge(s["pair_used"], it * PAIRS + (v + 1))
                            for i in range(2):
                                u = 2 * v + i
                                blk = pe.value_load(m.jrow[0:1, bass.ds(it * IT + u, 1)], min_val=0, max_val=LAST_BLOCK)
                                mm = pe.matmul(QP[v % 4][:, i * FEAT:(i + 1) * FEAT], OHT[:, u, :],
                                               m.node[:, bass.ds(blk * FEAT, FEAT)], start=True, stop=True)
                            mm.then_inc(s["q_rows"], 1)
                        pe.wait_ge(s["turned_sb"], it * 4 + (3 + q))
                        turn(it * 4 + (4 + q), q)

            @block.vector
            def _(dve):
                def make_masks(step, slot):
                    for i in range(4):
                        ins = dve.tensor_scalar(OH[:, slot + i, :], m.iota_f[:, :], m.dst_in[:, bass.ds(step + i, 1)],
                                                None, ALU.is_equal)
                    ins.then_inc(s["masks"], 1)

                for q in range(4):
                    make_masks(4 * q, 4 * q)
                dve.sem_inc(s["pair_used"], 4)
                dve.sem_inc(s["summed"], 2)
                dve.sem_inc(s["added"], 1)
                with dve.Fori(0, ITS) as it:
                    def sum_heads(v):
                        dve.wait_ge(s["pair_used"], it * PAIRS + (v + 5))
                        if v == 0:
                            dve.wait_ge(s["added"], it + 1)
                        dve.tensor_reduce(ST[:, v * 16:(v + 1) * 16], prod[:, v % 2, :].rearrange("p (a b) -> p a b", b=DH),
                                          AX.X, ALU.add).then_inc(s["summed"], 1)

                    for v in range(PAIRS):
                        if v % 2 == 0:
                            dve.wait_ge(s["turned"], it * 4 + (v // 2 + 1))
                            make_masks(it * IT + (IT + 2 * v), 2 * v)
                        dve.wait_ge(s["q_rows"], it * PAIRS + (v + 1))
                        dve.wait_ge(s["summed"], it * PAIRS + (v + 1))
                        for u in (2 * v, 2 * v + 1):
                            dve.wait_ge(k_in[u % 8], it * 32 + (u // 8 + 1) * 16)
                        at = (2 * v) % 8
                        dve.tensor_tensor(prod[:, v % 2, :], K[:, at:at + 2, :].rearrange("p a b -> p (a b)"),
                                          QP[v % 4][:, :], ALU.mult).then_inc(s["pair_used"], 1)
                        if v >= 1:
                            sum_heads(v - 1)
                    sum_heads(PAIRS - 1)
                    Sit = by_head(S)[:, :, bass.ds(it * IT, IT)]
                    dve.wait_ge(s["summed"], it * PAIRS + (PAIRS + 2))
                    dve.tensor_tensor(Sit, Sit, ST[:, :].rearrange("p (s h) -> p h s", h=HEADS), ALU.add).then_inc(s["added"], 1)


def scores_relational(nc, m, d, S):
    RH = RELS * HEADS
    NEG_SLOPE = 0.2
    with ExitStack() as ctx:
        s = sems(nc, m, "rel", "staged used masks turned turned_sb rows bank_used chain added")
        s_in = [new_sem(nc, m, f"rel_s_in{i}") for i in range(IT)]
        sb = lambda nm, sh, dt: ctx.enter_context(nc.sbuf_tensor(f"rel_{nm}", sh, dt))
        K = sb("K", [P, IT, HEADS], F32)
        stage = sb("stage", [P, IT], I32)
        OH = sb("OH", [P, IT, P], BF16)
        OHT = sb("OHT", [P, IT, P], F32)
        prod = sb("prod", [P, 2, 8 * RH], F32)
        ST = sb("ST", [P, 2, 8 * HEADS], F32)
        TP = [ctx.enter_context(nc.psum_tensor(f"rel_TP{i}", [P, 1024], BF16)) for i in range(2)]
        QP = [ctx.enter_context(nc.psum_tensor(f"rel_QP{i}", [P, 8 * RH], F32)) for i in range(4)]

        with nc.Block() as block:

            @block.gpsimd
            def _(pool):
                with pool.Fori(0, ITS) as it:
                    for u in range(IT):
                        if u % 8 == 0:
                            pool.wait_ge(s["staged"], it * 2 + (u // 8 + 1))
                            pool.wait_ge(s["used"], it * 2 + (u // 8 + 1))
                        if u % 2 == 0:
                            hold(pool, m)
                        pool.indirect_dma_start(out=K[:, u, :], out_offset=None, in_=d["s_tab"][:, :],
                                                in_offset=bass.IndirectOffsetOnAxis(ap=stage[:, u:u + 1], axis=0)
                                                ).then_inc(s_in[u], 16)

            @block.scalar
            def _(act):
                def to_sbuf(quad, slot):
                    act.wait_ge(s["turned"], quad + 1)
                    act.copy(OHT[:, 4 * slot:4 * slot + 4, :].rearrange("p a b -> p (a b)"),
                             TP[slot % 2][:, 0:512]).then_inc(s["turned_sb"], 1)

                for h in range(2):
                    act.copy(stage[:, 8 * h:8 * h + 8], m.idx_rel[:, 8 * h:8 * h + 8]).then_inc(s["staged"], 1)
                for q in range(4):
                    to_sbuf(q, q)
                with act.Fori(0, ITS) as it:
                    for q in range(4):
                        act.wait_ge(s["rows"], it * 4 + (q + 1))
                        to_sbuf(it * 4 + (4 + q), q)
                        if q % 2 == 1:
                            stage_half(act, stage, m.idx_rel, s["staged"],
                                       [(k, it * 16 + 16) for k in s_in[4 * q - 4:4 * q + 4]], it, q // 2)

            @block.tensor
            def _(pe):
                def turn(quad, slot):
                    pe.wait_ge(s["masks"], quad + 1)
                    for i in range(4):
                        mm = pe.transpose(TP[slot % 2][:, i * P:(i + 1) * P], OH[:, 4 * slot + i, :], m.ident_b[:, :])
                    mm.then_inc(s["turned"], 1)

                for q in range(4):
                    if q >= 2:
                        pe.wait_ge(s["turned_sb"], q - 1)
                    turn(q, q)
                with pe.Fori(0, ITS) as it:
                    for q in range(4):
                        pe.wait_ge(s["turned_sb"], it * 4 + (q + 1))
                        if q % 2 == 0:
                            pe.wait_ge(s["bank_used"], it * 2 + (q // 2 + 1))
                        for i in range(4):
                            u = 4 * q + i
                            blk = pe.value_load(m.jrow[0:1, bass.ds(it * IT + u, 1)], min_val=0, max_val=LAST_BLOCK)
                            mm = pe.matmul(QP[q // 2][:, (u % 8) * RH:(u % 8 + 1) * RH], OHT[:, u, :],
                                           m.node[:, bass.ds(blk * RH, RH)], start=True, stop=True)
                        mm.then_inc(s["rows"], 1)
                        pe.wait_ge(s["turned_sb"], it * 4 + (3 + q))
                        turn(it * 4 + (4 + q), q)

            @block.vector
            def _(dve):
                def make_masks(step, slot):
                    for i in range(4):
                        ins = dve.tensor_scalar(OH[:, slot + i, :], m.iota_f[:, :], m.dst_in[:, bass.ds(step + i, 1)],
                                                None, ALU.is_equal)
                    ins.then_inc(s["masks"], 1)

                for q in range(4):
                    make_masks(4 * q, 4 * q)
                dve.memset(by_head(S)[:, :, STEPS:], 0.0)
                dve.sem_inc(s["bank_used"], 2)
                dve.sem_inc(s["used"], 2)
                with dve.Fori(0, ITS) as it:
                    for g in range(2):
                        base = it * 8 + 4 * g
                        for q in (2 * g, 2 * g + 1):
                            dve.wait_ge(s["turned"], it * 4 + (q + 1))
                            make_masks(it * IT + (IT + 4 * q), 4 * q)
                        dve.wait_ge(s["rows"], it * 4 + (2 * g + 2))
                        rel = m.relmask[:, bass.ds(it * (IT * RELS) + g * RH, RH)]
                        dve.tensor_tensor(prod[:, g, :].rearrange("p (a h) -> p a h", h=HEADS),
                                          QP[g][:, :].rearrange("p (a h) -> p a h", h=HEADS),
                                          rel.unsqueeze(2).to_broadcast([P, RH, HEADS]), ALU.mult).then_inc(s["bank_used"], 1)
                        dve.wait_ge(s["bank_used"], it * 2 + (g + 3))
                        dve.tensor_reduce(ST[:, g, :].rearrange("p (s h) -> p s h", h=HEADS),
                                          prod[:, g, :].rearrange("p (s r h) -> p s h r", r=RELS, h=HEADS),
                                          AX.X, ALU.add).then_inc(s["chain"], 1)
                        for u in range(8 * g, 8 * g + 8):
                            dve.wait_ge(s_in[u], it * 16 + 16)
                        dve.wait_ge(s["chain"], base + 1)
                        dve.tensor_tensor(ST[:, g, :], ST[:, g, :], K[:, 8 * g:8 * g + 8, :].rearrange("p a h -> p (a h)"),
                                          ALU.add).then_inc(s["used"], 1)
                        dve.wait_ge(s["used"], it * 2 + (g + 3))
                        Sg = by_head(S)[:, :, bass.ds(it * IT + 8 * g, 8)]
                        sums = ST[:, g, :].rearrange("p (s h) -> p h s", h=HEADS)
                        dve.scalar_tensor_tensor(Sg, sums, NEG_SLOPE, sums, ALU.mult, ALU.max).then_inc(s["chain"], 1)
                        dve.wait_ge(s["chain"], base + 2)
                        dve.tensor_tensor(Sg, Sg, m.outside[:, bass.ds(it * IT + 8 * g, 8)].unsqueeze(1).to_broadcast(
                            [P, HEADS, 8]), ALU.add).then_inc(s["chain"], 2)


def segment_softmax(nc, m, S, floor, name):
    with ExitStack() as ctx:
        s = sems(nc, m, name, "turned copied dve pe rows neg exp back back_copied")
        sb = lambda nm, sh, dt: ctx.enter_context(nc.sbuf_tensor(f"{name}_{nm}", sh, dt))
        SC = sb("SC", [P, CLEN], F32)
        M = sb("M", [P, CLEN], F32)
        row = sb("row", [1, 2, P + 1], F32)
        col = sb("col", [P, 2], F32)
        pt = [ctx.enter_context(nc.psum_tensor(f"{name}_p{i}", [P, 512], F32)) for i in range(4)]
        pr = ctx.enter_context(nc.psum_tensor(f"{name}_pr", [1, P], F32))
        pc = ctx.enter_context(nc.psum_tensor(f"{name}_pc", [P, 1], F32))
        Sv = S[:, :].rearrange("p (hc g) -> p g hc", g=CS)
        QUADS = -(-CS // 4)
        quad = lambda q: range(4 * q, min(4 * q + 4, CS))
        cuts = [0, 14, 27, 40, CS]

        with nc.Block() as block:

            @block.tensor
            def _(pe):
                for q in range(QUADS):
                    if q >= 4:
                        pe.wait_ge(s["copied"], q - 3)
                    for i, g in enumerate(quad(q)):
                        mm = pe.transpose(pt[q % 4][:, i * P:(i + 1) * P], Sv[:, g, :], m.ident[:, :])
                    mm.then_inc(s["turned"], 1)
                for direction in range(2):
                    pe.wait_ge(s["dve"], 1 + 4 * direction)
                    pe.transpose(pr[:, :], M[:, CLEN - 1:CLEN] if direction == 0 else M[:, 0:1], m.ident[:, :]).then_inc(s["pe"], 1)
                    pe.wait_ge(s["dve"], 3 + 4 * direction)
                    pe.transpose(pc[:, :], row[0:1, 0, 0:P] if direction == 0 else row[0:1, 1, 1:P + 1],
                                 m.ident[0:1, 0:1]).then_inc(s["pe"], 1)
                for q in range(QUADS):
                    pe.wait_ge(s["exp"], sum(quad(q)[-1] >= c for c in cuts))
                    if q >= 4:
                        pe.wait_ge(s["back_copied"], q - 3)
                    for i, g in enumerate(quad(q)):
                        mm = pe.transpose(pt[q % 4][:, i * P:(i + 1) * P], SC[:, g * P:(g + 1) * P], m.ident[:, :])
                    mm.then_inc(s["back"], 1)

            @block.scalar
            def _(act):
                for q in range(QUADS):
                    act.wait_ge(s["turned"], q + 1)
                    n = len(quad(q)) * P
                    act.copy(SC[:, q * 512:q * 512 + n], pt[q % 4][:, 0:n]).then_inc(s["copied"], 1)
                for i in range(len(cuts) - 1):
                    a, b = cuts[i] * P, cuts[i + 1] * P
                    act.wait_ge(s["neg"], i + 1)
                    act.activation(SC[:, a:b], M[:, a:b], ACT.Exp, scale=-1.0).then_inc(s["exp"], 1)

            @block.vector
            def _(dve):
                done = 0

                def step(ins):
                    nonlocal done
                    done += 1
                    ins.then_inc(s["dve"], 1)
                    dve.wait_ge(s["dve"], done)

                dve.wait_ge(s["copied"], QUADS)
                for direction in range(2):
                    fwd = direction == 0
                    starts = m.starts[:, 0:CLEN] if fwd else m.starts[:, CLEN:0:-1]
                    src = SC[:, :] if fwd else M[:, ::-1]
                    out = M[:, :] if fwd else M[:, ::-1]
                    step(dve.tensor_tensor_scan(out, starts, src, -BIG, ALU.add, ALU.max))
                    dve.wait_ge(s["pe"], 1 + 2 * direction)
                    r = row[0:1, direction, :]
                    if fwd:
                        step(dve.memset(r[:, 0:1], -BIG))
                        step(dve.tensor_tensor_scan(r[:, 1:P + 1], m.chain_fwd[:, :], pr[0:1, :], -BIG, ALU.add, ALU.max))
                    else:
                        step(dve.memset(r[:, P:P + 1], -BIG))
                        step(dve.tensor_tensor_scan(r[:, P - 1::-1], m.chain_bwd[:, ::-1], pr[0:1, ::-1], -BIG,
                                                    ALU.add, ALU.max))
                    dve.wait_ge(s["pe"], 2 + 2 * direction)
                    step(dve.tensor_copy(col[:, direction:direction + 1], pc[:, :]))
                    if fwd:
                        dve.tensor_tensor_scan(out, starts, src, col[:, 0:1], ALU.add, ALU.max).then_inc(s["rows"], 1)
                        dve.wait_ge(s["rows"], 1)
                    else:
                        dve.tensor_tensor_scan(out, starts, src, col[:, 1:2], ALU.add, ALU.max).then_inc(s["rows"], 1)
                        dve.wait_ge(s["rows"], 2)
                for i in range(len(cuts) - 1):
                    a, b = cuts[i] * P, cuts[i + 1] * P
                    dve.scalar_tensor_tensor(M[:, a:b], M[:, a:b], floor, SC[:, a:b], ALU.max, ALU.subtract).then_inc(s["neg"], 1)
                for q in range(QUADS):
                    dve.wait_ge(s["back"], q + 1)
                    n = len(quad(q))
                    dve.tensor_copy(Sv[:, 4 * q:4 * q + n, :],
                                    pt[q % 4][:, 0:n * P].rearrange("p (g hc) -> p g hc", g=n)).then_inc(s["back_copied"], 1)


def aggregate(nc, m, S, table, idx, name):
    LEAD = 4
    PAIRS = IT // 2
    with ExitStack() as ctx:
        s = sems(nc, m, name, "staged masks weighted weights cleared sums added")
        v_in = [new_sem(nc, m, f"{name}_v_in{i}") for i in range(IT)]
        sb = lambda nm, sh, dt: ctx.enter_context(nc.sbuf_tensor(f"{name}_{nm}", sh, dt))
        V = sb("V", [P, IT, FEAT], F32)
        stage = sb("stage", [P, IT], I32)
        OH = sb("OH", [P, IT, P], F32)
        U = sb("U", [P, IT, NUMC], F32)
        AP_ = [ctx.enter_context(nc.psum_tensor(f"{name}_AP{i}", [P, 512], F32)) for i in range(2)]
        SP = [ctx.enter_context(nc.psum_tensor(f"{name}_SP{i}", [P, 512], F32)) for i in range(4)]

        with nc.Block() as block:

            @block.gpsimd
            def _(pool):
                def gather(u, new_half, half, pair):
                    if new_half:
                        pool.wait_ge(s["staged"], half)
                    if u % 2 == 0:
                        pool.wait_ge(s["weighted"], pair)
                    if u % 2 == 0:
                        hold(pool, m)
                    pool.indirect_dma_start(out=V[:, u, :], out_offset=None, in_=table[:, :],
                                            in_offset=bass.IndirectOffsetOnAxis(ap=stage[:, u:u + 1], axis=0)
                                            ).then_inc(v_in[u], 16)

                for u in range(LEAD):
                    gather(u, u == 0, 1, u // 2 + 1)
                with pool.Fori(0, ITS) as it:
                    for a in range(LEAD, LEAD + IT):
                        gather(a % IT, a % 8 == 0, it * 2 + (a // 8 + 1), it * PAIRS + (a // 2 + 1))

            @block.scalar
            def _(act):
                def weights(half, h):
                    w = by_head(S)[:, :, bass.ds(half * 8, 8)].rearrange("p h s -> p s h")
                    act.copy(AP_[h][:, 0:8 * HEADS].rearrange("p (s h) -> p s h", h=HEADS), w).then_inc(s["weights"], 1)
                    act.copy(U[:, 8 * h:8 * h + 8, FEAT:NUMC], w).then_inc(s["weights"], 1)

                for h in range(2):
                    act.copy(stage[:, 8 * h:8 * h + 8], idx[:, 8 * h:8 * h + 8]).then_inc(s["staged"], 1)
                    weights(h, h)
                def stage_ahead(half, h, it, done):
                    for k in v_in[8 * h:8 * h + 8]:
                        act.wait_ge(k, it * 16 + done)
                    act.copy(stage[:, 8 * h:8 * h + 8], idx[:, bass.ds(half * 8, 8)]).then_inc(s["staged"], 1)

                stage_ahead(2, 0, 0, 16)
                with act.Fori(0, ITS - 1) as it:
                    for h in range(2):
                        stage_ahead(it * 2 + (3 + h), 1 - h, it, 16 * (h + 1))
                        act.wait_ge(s["sums"], it * IT + 8 * (h + 1))
                        weights(it * 2 + (2 + h), h)
                act.wait_ge(s["sums"], (ITS - 1) * IT + 8)
                weights(2 * ITS, 0)

            @block.tensor
            def _(pe):
                def sum_step(u, masks, weighted, half, free):
                    pe.wait_ge(s["masks"], masks)
                    if u % 2 == 0:
                        pe.wait_ge(s["weighted"], weighted)
                    if u % 8 == 0:
                        pe.wait_ge(s["weights"], half * 2)
                    pe.wait_ge(s["added"], free)
                    pe.matmul(SP[u % 4][:, 0:NUMC], OH[:, u, :], U[:, u, :], start=True, stop=True).then_inc(s["sums"], 1)

                for u in range(LEAD):
                    sum_step(u, u + 1, u // 2 + (PAIRS + 1), 1, u + 1)
                with pe.Fori(0, ITS) as it:
                    for a in range(LEAD, LEAD + IT):
                        sum_step(a % IT, it * IT + (a + 1), it * PAIRS + (a // 2 + PAIRS + 1), it * 2 + (a // 8 + 1),
                                 it * IT + (a + 1))

            @block.vector
            def _(dve):
                def make_mask(step, slot):
                    dve.tensor_scalar(OH[:, slot, :], m.iota_f[:, :], m.dst_in[:, bass.ds(step, 1)], None,
                                      ALU.is_equal).then_inc(s["masks"], 1)

                def weigh(v, rows_in, half):
                    if v % 4 == 0:
                        dve.wait_ge(s["weights"], half * 2)
                    for u in (2 * v, 2 * v + 1):
                        dve.wait_ge(v_in[u], rows_in)
                    at = 2 * v
                    dve.tensor_tensor(U[:, at:at + 2, 0:FEAT].rearrange("p s (a b) -> p s a b", b=DH),
                                      V[:, at:at + 2, :].rearrange("p s (a b) -> p s a b", b=DH),
                                      AP_[(v // 4) % 2][:, (v % 4) * 16:(v % 4 + 1) * 16].rearrange(
                                          "p (s a) -> p s a", a=HEADS).unsqueeze(3).to_broadcast([P, 2, HEADS, DH]),
                                      ALU.mult).then_inc(s["weighted"], 1)

                dve.memset(m.node[:, :], 0.0).then_inc(s["cleared"], 1)
                dve.wait_ge(s["cleared"], 1)
                dve.sem_inc(s["weighted"], PAIRS)
                dve.sem_inc(s["added"], 4)
                for u in range(2 * LEAD):
                    make_mask(u, u)
                for v in range(2):
                    weigh(v, 16, 1)
                with dve.Fori(0, ITS) as it:
                    _, packed = nc.values_load_multi_w_load_instructions(
                        m.jquad[0:1, bass.ds(it * (IT // 4), IT // 4)], engines=[mybir.EngineType.DVE],
                        min_val=0, max_val=PACK ** 4 - 1)
                    for q in range(4):
                        for i in range(4):
                            u = 4 * q + i
                            if i % 2 == 0:
                                v = u // 2 + LEAD // 2
                                weigh(v % PAIRS, it * 16 + 16 * (v // PAIRS + 1), it * 2 + (v // 4 + 1))
                            dve.wait_ge(s["sums"], it * IT + (u + 1))
                            dve.wait_ge(s["added"], it * IT + (u + 4))
                            blk = nc.s_assert_within((packed[q] >> (6 * i)) & (PACK - 1), 0, LAST_BLOCK,
                                                     skip_runtime_bounds_check_because="each is a step's block number")
                            acc = m.node[:, bass.ds(blk * NUMC, NUMC)]
                            dve.tensor_tensor(acc, acc, SP[u % 4][:, 0:NUMC], ALU.add).then_inc(s["added"], 1)
                            if i % 2 == 0:
                                for n in (u + 2 * LEAD, u + 2 * LEAD + 1):
                                    make_mask(it * IT + n, n % IT)


def norm_stats(dve, m, x, st, mv, sem_stats, n_stats, sem_mv):
    dve.bn_stats(st, x).then_inc(sem_stats, 1)
    dve.wait_ge(sem_stats, n_stats)
    hold(dve, m)
    dve.bn_aggr(mv, st).then_inc(sem_mv, 1)


def norm_scale(pool, m, mv, rstd, sem_eps, n_eps, sem_rstd):
    hold(pool, m)
    pool.tensor_scalar(rstd, mv[:, 1:2], LN_EPS, 1.0, ALU.add, ALU.mult).then_inc(sem_eps, 1)
    pool.wait_ge(sem_eps, n_eps)
    pool.tensor_tensor(rstd, rstd, m.mhalf[:, :], ALU.pow).then_inc(sem_rstd, 1)


def has(t, count):
    return not isinstance(t, int) or 0 <= t < count


def need(eng, sem, value):
    if not isinstance(value, int) or value > 0:
        eng.wait_ge(sem, value)


def pipeline(eng, body, lead, lag, count):
    turns = (count - lead - 4) // 2
    for t in range(-lead, 4):
        body(t, t % 2)
    with eng.Fori(0, turns) as it:
        for i in range(2):
            body(it * 2 + (4 + i), i)
    for t in range(4 + 2 * turns, count + lag):
        body(t, t % 2)


def slot_wait(eng, sem, t, per):
    if isinstance(t, int):
        eng.wait_ge(sem, (t // 2 + 1) * per)
    else:
        eng.wait_ge(sem, t // 2 * per + per)


def norm_front(nc, m, ctx, name, tiles, banks=2):
    f = Shared()
    f.s = sems(nc, m, name, "stats mv eps rstd normed turned yT")
    sb = lambda nm, sh, dt: ctx.enter_context(nc.sbuf_tensor(f"{name}_{nm}", sh, dt))
    f.Y = sb("Y", [P, 2, FEAT], F32)
    f.YT = sb("YT", [P, 2, FEAT], F32)
    f.st = sb("st", [P, 2, 6], F32)
    f.mv = sb("mv", [P, 2, 2], F32)
    f.rstd = sb("rstd", [P, 2], F32)
    T = [ctx.enter_context(nc.psum_tensor(f"{name}_T{i}", [P, 512], F32)) for i in range(banks)]
    f.T = [T[i * (banks - 1)][:, (2 - banks) * i * FEAT:(2 - banks) * i * FEAT + FEAT] for i in range(2)]
    f.tiles, f.banks = tiles, banks
    return f


def front_stats(dve, m, f, x, t, i):
    if has(t, f.tiles):
        norm_stats(dve, m, x, f.st[:, i, :], f.mv[:, i, :], f.s["stats"], t + 1, f.s["mv"])


def front_scale(pool, m, f, t, i):
    if has(t, f.tiles):
        pool.wait_ge(f.s["mv"], t + 1)
        need(pool, f.s["normed"], t - 1)
        norm_scale(pool, m, f.mv[:, i, :], f.rstd[:, i:i + 1], f.s["eps"], t + 1, f.s["rstd"])


def front_norm(dve, f, x, t, i):
    if has(t, f.tiles):
        dve.wait_ge(f.s["rstd"], t + 1)
        need(dve, f.s["turned"], t - 1)
        dve.tensor_scalar(f.Y[:, i, :], x, f.mv[:, i, 0:1], f.rstd[:, i:i + 1], ALU.subtract,
                          ALU.mult).then_inc(f.s["normed"], 1)


def front_turn(pe, m, f, t, i):
    if has(t, f.tiles):
        pe.wait_ge(f.s["normed"], t + 1)
        need(pe, f.s["yT"], t + 1 - f.banks)
        for k in range(2):
            mm = pe.transpose(f.T[i][:, k * P:(k + 1) * P], f.Y[:, i, k * P:(k + 1) * P], m.ident[:, :])
        mm.then_inc(f.s["turned"], 1)


def front_copy(eng, copy, f, t, i, used, per=1):
    if has(t, f.tiles):
        eng.wait_ge(f.s["turned"], t + 1)
        need(eng, used, (t - 1) * per)
        copy(f.YT[:, i, :], f.T[i][:, 0:FEAT]).then_inc(f.s["yT"], 1)


def project_attention(nc, m, d):
    with ExitStack() as ctx:
        s = sems(nc, m, "qkv", "w mm q_out kv_out kv_free stored0 stored1")
        x_in = [new_sem(nc, m, f"qkv_x_in{i}") for i in range(2)]
        stored = (s["stored0"], s["stored1"])
        sb = lambda nm, sh, dt: ctx.enter_context(nc.sbuf_tensor(f"qkv_{nm}", sh, dt))
        f = norm_front(nc, m, ctx, "qkv", BLOCKS)
        W = sb("W", [P, 2, 3 * FEAT], F32)
        X = sb("X", [P, 2, FEAT], F32)
        KV = sb("KV", [P, 2, 2 * FEAT], F32)
        Q = [ctx.enter_context(nc.psum_tensor(f"qkv_Q{i}", [P, 512], F32)) for i in range(2)]
        KVP = [ctx.enter_context(nc.psum_tensor(f"qkv_KV{i}", [P, 512], F32)) for i in range(2)]
        LEAD = 5
        with nc.Block() as block:

            @block.sync
            def _(sp):
                for k in range(2):
                    sp.dma_start(W[:, k, :], d["wqkv"][k * P:(k + 1) * P, :]).then_inc(s["w"], 16)

                def body(t, i):
                    n, j = t + 5, (i + 1) % 2
                    if has(n, BLOCKS):
                        need(sp, f.s["normed"], n - 1)
                        hold(sp, m)
                        sp.dma_start(X[:, j, :], d["x"][bass.ds(n * P, P), :]).then_inc(x_in[j], 16)
                    if has(t, BLOCKS):
                        sp.wait_ge(s["kv_out"], t + 1)
                        hold(sp, m)
                        sp.dma_start(d["k_tab"][bass.ds(t * P, P), :], KV[:, i, 0:FEAT]).then_inc(stored[i], 16)
                        sp.dma_start(d["v_tab"][bass.ds(t * P, P), :], KV[:, i, FEAT:]).then_inc(stored[i], 16)
                    n, j = t - 1, (i + 1) % 2
                    if has(n, BLOCKS):
                        slot_wait(sp, stored[j], n, 32)
                        sp.sem_inc(s["kv_free"], 1)

                pipeline(sp, body, LEAD, 1, BLOCKS)

            @block.gpsimd
            def _(pool):
                pipeline(pool, lambda t, i: front_scale(pool, m, f, t + 4, i), LEAD, 1, BLOCKS)

            @block.scalar
            def _(act):
                def body(t, i):
                    if has(t, BLOCKS):
                        act.wait_ge(s["mm"], t + 1)
                        need(act, s["kv_free"], t - 1)
                        act.copy(KV[:, i, :], KVP[i][:, :]).then_inc(s["kv_out"], 1)
                    front_copy(act, act.copy, f, t + 2, i, s["mm"])

                pipeline(act, body, LEAD, 1, BLOCKS)

            @block.vector
            def _(dve):
                def body(t, i):
                    front_norm(dve, f, X[:, (i + 1) % 2, :], t + 3, (i + 1) % 2)
                    if has(t + 4, BLOCKS):
                        slot_wait(dve, x_in[i], t + 4, 16)
                        front_stats(dve, m, f, X[:, i, :], t + 4, i)
                    if has(t, BLOCKS):
                        dve.wait_ge(s["mm"], t + 1)
                        dve.tensor_scalar(m.node[:, bass.ds(t * FEAT, FEAT)], Q[i][:, 0:FEAT], QSCALE, None,
                                          ALU.mult).then_inc(s["q_out"], 1)

                pipeline(dve, body, LEAD, 1, BLOCKS)

            @block.tensor
            def _(pe):
                pe.wait_ge(s["w"], 32)

                def body(t, i):
                    if has(t, BLOCKS):
                        pe.wait_ge(f.s["yT"], t + 1)
                        need(pe, s["q_out"], t - 1)
                        need(pe, s["kv_out"], t - 1)
                        for k in range(2):
                            pe.matmul(Q[i][:, 0:FEAT], f.YT[:, i, k * P:(k + 1) * P], W[:, k, 0:FEAT],
                                      start=(k == 0), stop=(k == 1))
                        for k in range(2):
                            mm = pe.matmul(KVP[i][:, :], f.YT[:, i, k * P:(k + 1) * P], W[:, k, FEAT:],
                                           start=(k == 0), stop=(k == 1))
                        mm.then_inc(s["mm"], 1)
                    front_turn(pe, m, f, t + 2, i)

                pipeline(pe, body, LEAD, 1, BLOCKS)


def top_experts(dve, m, probs, best, idx, idx_f, link):
    hold(dve, m)
    link(dve.max(best, probs))
    hold(dve, m)
    link(dve.max_index(idx, best, probs))
    link(dve.tensor_copy(idx_f, idx))


class LoopLink:

    def __init__(self, eng, sem, it, per):
        self.eng, self.sem, self.it, self.per, self.n = eng, sem, it, per, 0

    def __call__(self, ins):
        self.n += 1
        ins.then_inc(self.sem, 1)
        self.eng.wait_ge(self.sem, self.it * self.per + self.n)


def attend_and_route(nc, m, d):
    KC = HID // P
    with ExitStack() as ctx:
        s = sems(nc, m, "gate", "w zeroed filled clipped inverted o_ready o_turned oT attn_out x1 hidden gelu gated logits "
                 "saved0 saved1 y_saved")
        x_in = [new_sem(nc, m, f"gate_x_in{i}") for i in range(2)]
        saved = (s["saved0"], s["saved1"])
        sb = lambda nm, sh, dt: ctx.enter_context(nc.sbuf_tensor(f"gate_{nm}", sh, dt))
        f = norm_front(nc, m, ctx, "gate", BLOCKS)
        Wo = sb("Wo", [P, 2, FEAT], F32)
        W1 = sb("W1", [P, 2, HID], F32)
        b1 = sb("b1", [P, KC], F32)
        Wg = sb("Wg", [P, KC, EXPERTS], F32)
        bg = sb("bg", [P, EXPERTS], F32)
        zeros = sb("zeros", [P, SORTED * FEAT // 8], F32)
        X = sb("X", [P, 2, FEAT], F32)
        O = sb("O", [P, 2, FEAT], F32)
        OT = sb("OT", [P, 2, FEAT], F32)
        HT = sb("HT", [P, 2, HID], F32)
        r = sb("r", [P, 2, HEADS], F32)
        TO = ctx.enter_context(nc.psum_tensor("gate_TO", [P, 512], F32))
        OUT = ctx.enter_context(nc.psum_tensor("gate_OUT", [P, 512], F32))
        LG = ctx.enter_context(nc.psum_tensor("gate_LG", [P, 512], F32))
        HB = [ctx.enter_context(nc.psum_tensor(f"gate_HB{i}", [P, 512], F32)) for i in range(2)]
        LOADS = 7
        LEAD = 6
        node = lambda t, a, b: m.node[:, bass.ds(t * NUMC + a, b - a)]
        with nc.Block() as block:

            @block.sync
            def _(sp):
                for k in range(2):
                    sp.dma_start(Wo[:, k, :], d["wo"][k * P:(k + 1) * P, :]).then_inc(s["w"], 16)
                    sp.dma_start(W1[:, k, :], d["w1"][k * P:(k + 1) * P, :]).then_inc(s["w"], 16)
                sp.dma_start(b1[:, :], d["b1"][:, :]).then_inc(s["w"], 16)
                sp.dma_start(Wg[:, :, :].rearrange("p k e -> p (k e)"), d["wg"][:, :]).then_inc(s["w"], 16)
                sp.dma_start(bg[:, :], d["bg"][0:1, :].to_broadcast([P, EXPERTS])).then_inc(s["w"], 16)
                sp.wait_ge(s["zeroed"], 1)
                flat = d["y_sorted"].rearrange("(p n) c -> p (n c)", p=P)
                width = SORTED * FEAT // 8
                for k in range(8):
                    sp.dma_start(flat[:, k * width:(k + 1) * width], zeros[:, :]).then_inc(s["filled"], 16)

                def body(t, i):
                    n = t + 6
                    if has(n, BLOCKS):
                        need(sp, s["x1"], n - 1)
                        hold(sp, m)
                        sp.dma_start(X[:, i, :], d["x"][bass.ds(n * P, P), :]).then_inc(x_in[i], 16)
                    n, j = t + 3, (i + 1) % 2
                    if has(n, BLOCKS):
                        sp.wait_ge(f.s["normed"], n + 1)
                        hold(sp, m)
                        sp.dma_start(d["y_tab"][bass.ds(n * P, P), :], f.Y[:, j, :]).then_inc(saved[j], 16)
                    if has(t + 2, BLOCKS):
                        slot_wait(sp, saved[i], t + 2, 16)
                        sp.sem_inc(s["y_saved"], 1)

                pipeline(sp, body, LEAD, 1, BLOCKS)
                sp.wait_ge(s["filled"], 16 * 8)

            @block.gpsimd
            def _(pool):
                pool.memset(zeros[:, :], 0.0).then_inc(s["zeroed"], 1)
                pipeline(pool, lambda t, i: front_scale(pool, m, f, t + 4, i), LEAD, 1, BLOCKS)

            @block.scalar
            def _(act):
                act.wait_ge(s["w"], 16 * LOADS)

                def body(t, i):
                    if has(t, BLOCKS):
                        need(act, s["gated"], t - 1)
                        for c in range(KC):
                            if c % 4 == 0:
                                act.wait_ge(s["hidden"], t * 2 + (c // 4 + 1))
                            act.activation(HT[:, i, c * P:(c + 1) * P], HB[c // 4][:, (c % 4) * P:(c % 4 + 1) * P],
                                           ACT.Gelu, bias=b1[:, c:c + 1]).then_inc(s["gelu"], 1)

                pipeline(act, body, LEAD, 1, BLOCKS)

            @block.tensor
            def _(pe):
                pe.wait_ge(s["w"], 16 * LOADS)

                def body(t, i):
                    j = (i + 1) % 2
                    if has(t, BLOCKS):
                        hidden_features(pe, s, f.YT[:, i, :], W1, HB, f.s["yT"], t)
                    if has(t - 1, BLOCKS):
                        pe.wait_ge(s["gelu"], t * KC)
                        need(pe, s["logits"], t - 1)
                        for c in range(KC):
                            mm = pe.matmul(LG[:, 0:EXPERTS], HT[:, j, c * P:(c + 1) * P], Wg[:, c, :],
                                           start=(c == 0), stop=(c == KC - 1))
                        mm.then_inc(s["gated"], 1)
                    front_turn(pe, m, f, t + 2, i)
                    n = t + 4
                    if has(n, BLOCKS):
                        pe.wait_ge(s["oT"], n + 1)
                        need(pe, s["x1"], n)
                        for k in range(2):
                            mm = pe.matmul(OUT[:, 0:FEAT], OT[:, i, k * P:(k + 1) * P], Wo[:, k, :],
                                           start=(k == 0), stop=(k == 1))
                        mm.then_inc(s["attn_out"], 1)
                    n = t + 5
                    if has(n, BLOCKS):
                        pe.wait_ge(s["o_ready"], n + 1)
                        need(pe, s["oT"], n)
                        for k in range(2):
                            mm = pe.transpose(TO[:, k * P:(k + 1) * P], O[:, j, k * P:(k + 1) * P], m.ident[:, :])
                        mm.then_inc(s["o_turned"], 1)

                pipeline(pe, body, LEAD, 1, BLOCKS)

            @block.vector
            def _(dve):
                dve.wait_ge(s["w"], 16 * LOADS)

                def body(t, i):
                    j = (i + 1) % 2
                    if has(t + 3, BLOCKS):
                        need(dve, s["y_saved"], t + 2)
                        front_norm(dve, f, node(t + 3, 0, FEAT), t + 3, j)
                    if has(t - 1, BLOCKS):
                        dve.wait_ge(s["gated"], t)
                        dve.tensor_tensor(m.logits[:, bass.ds((t - 1) * EXPERTS, EXPERTS)], LG[:, 0:EXPERTS],
                                          bg[:, :], ALU.add).then_inc(s["logits"], 1)
                    front_copy(dve, dve.tensor_copy, f, t + 2, i, s["hidden"], 2)
                    n = t + 4
                    if has(n, BLOCKS):
                        dve.wait_ge(s["attn_out"], n + 1)
                        slot_wait(dve, x_in[i], n, 16)
                        dve.tensor_tensor(node(n, 0, FEAT), X[:, i, :], OUT[:, 0:FEAT], ALU.add).then_inc(s["x1"], 1)
                        dve.wait_ge(s["x1"], n + 1)
                        hold(dve, m)
                        front_stats(dve, m, f, node(n, 0, FEAT), n, i)
                    n = t + 5
                    if has(n, BLOCKS):
                        dve.wait_ge(s["o_turned"], n + 1)
                        need(dve, s["attn_out"], n - 1)
                        dve.tensor_copy(OT[:, j, :], TO[:, 0:FEAT]).then_inc(s["oT"], 1)
                    n = t + 6
                    if has(n, BLOCKS):
                        dve.tensor_scalar(r[:, i, :], node(n, FEAT, NUMC), 1e-30, None, ALU.max).then_inc(s["clipped"], 1)
                        dve.wait_ge(s["clipped"], n + 1)
                        dve.reciprocal(r[:, i, :], r[:, i, :]).then_inc(s["inverted"], 1)
                        dve.wait_ge(s["inverted"], n + 1)
                        need(dve, s["o_turned"], n - 1)
                        dve.tensor_tensor(O[:, i, :].rearrange("p (h c) -> p h c", c=DH),
                                          node(n, 0, FEAT).rearrange("p (h c) -> p h c", c=DH),
                                          r[:, i, :].unsqueeze(2).to_broadcast([P, HEADS, DH]),
                                          ALU.mult).then_inc(s["o_ready"], 1)

                pipeline(dve, body, LEAD, 1, BLOCKS)


def hidden_features(pe, s, yT, W1, HB, turned, t):
    KC = HID // P
    pe.wait_ge(turned, t + 1)
    for c in range(KC):
        if c % 4 == 0:
            need(pe, s["gelu"], t * KC + (c + 4 - KC))
        for k in range(2):
            mm = pe.matmul(HB[c // 4][:, (c % 4) * P:(c % 4 + 1) * P], W1[:, k, c * P:(c + 1) * P],
                           yT[:, k * P:(k + 1) * P], start=(k == 0), stop=(k == 1))
        if c % 4 == 3:
            mm.then_inc(s["hidden"], 1)


def sort_by_expert(nc, m, d):
    BE = BLOCKS * EXPERTS
    with ExitStack() as ctx:
        s = sems(nc, m, "sort", "link shifted powed pidx counted chosen")
        sb = lambda nm, sh, dt: ctx.enter_context(nc.sbuf_tensor(f"sort_{nm}", sh, dt))
        grid = lambda a: a[:, :].rearrange("p (b e) -> p b e", e=EXPERTS)
        per_row = lambda a: a[:, :].unsqueeze(2).to_broadcast([P, BLOCKS, EXPERTS])
        per_expert = lambda a: a[:, 0:EXPERTS].unsqueeze(1).to_broadcast([P, BLOCKS, EXPERTS])
        ex = sb("ex", [P, BE], F32)
        hot = sb("hot", [P, BE], F32)
        pick = sb("pick", [P, BE], F32)
        sums = [sb(f"sums{i}", [P, BE], F32) for i in range(2)]
        top = sb("top", [P, BLOCKS], F32)
        inv = sb("inv", [P, BLOCKS], F32)
        numbers = sb("numbers", [P, EXPERTS], F32)
        pidx_i = sb("pidx_i", [P, 1], I32)
        pidx = sb("pidx", [P, 1], F32)
        before = sb("before", [P, P], F32)
        ones = sb("ones", [P, P], F32)
        tiles_i = sb("tiles_i", [P, EXPERTS], I32)
        tiles = sb("tiles", [P, EXPERTS], F32)
        ends = [sb(f"ends{i}", [P, EXPERTS], F32) for i in range(2)]
        start = sb("start", [P, EXPERTS], F32)
        over = sb("over", [1, SORTED * EXPERTS], F32)
        tile_f = sb("tile_f", [1, SORTED], F32)
        WITHIN = ctx.enter_context(nc.psum_tensor("sort_within", [P, 512], F32))
        TOTAL = ctx.enter_context(nc.psum_tensor("sort_total", [P, 512], F32))
        with nc.Block() as block:

            @block.gpsimd
            def _(pool):
                pool.iota(pidx_i[:, :], pattern=[[1, 1]], base=0, channel_multiplier=1).then_inc(s["pidx"], 1)
                pool.wait_ge(s["shifted"], 1)
                pool.tensor_tensor(grid(ex), per_expert(m.e_const), grid(m.logits), ALU.pow).then_inc(s["powed"], 1)

            @block.tensor
            def _(pe):
                pe.wait_ge(s["chosen"], 1)
                pe.matmul(WITHIN[:, 0:BE], before[:, :], hot[:, :], start=True, stop=True)
                pe.matmul(TOTAL[:, 0:BE], ones[:, :], hot[:, :], start=True, stop=True).then_inc(s["counted"], 1)

            @block.vector
            def _(dve):
                link = Link(dve, s["link"])
                link(dve.tensor_reduce(top[:, :], grid(m.logits), AX.X, ALU.max))
                dve.tensor_tensor(grid(m.logits), grid(m.logits), per_row(top), ALU.subtract).then_inc(s["shifted"], 1)
                dve.wait_ge(s["pidx"], 1)
                link(dve.tensor_copy(pidx[:, :], pidx_i[:, :]))
                link(dve.tensor_scalar(before[:, :], m.iota_f[:, :], pidx[:, 0:1], None, ALU.is_gt))
                link(dve.memset(ones[:, :], 1.0))
                link(dve.tensor_scalar(numbers[:, :], m.iota_f[:, 0:EXPERTS], -float(EXPERTS), None, ALU.add))
                dve.wait_ge(s["powed"], 1)
                link(dve.tensor_reduce(inv[:, :], grid(ex), AX.X, ALU.add))
                link(dve.reciprocal(inv[:, :], inv[:, :]))
                link(dve.tensor_tensor(grid(ex), grid(ex), per_row(inv), ALU.mult))
                link(dve.tensor_reduce(m.prob[:, :], grid(ex), AX.X, ALU.max))
                link(dve.tensor_tensor(grid(hot), grid(ex), per_row(m.prob), ALU.is_equal))
                link(dve.tensor_tensor(grid(pick), grid(hot), per_expert(numbers), ALU.mult))
                link(dve.tensor_reduce(top[:, :], grid(pick), AX.X, ALU.min))
                link(dve.tensor_tensor(grid(hot), per_expert(numbers), per_row(top), ALU.is_equal))
                dve.sem_inc(s["chosen"], 1)
                dve.wait_ge(s["counted"], 1)
                link(dve.tensor_copy(sums[0][:, :], TOTAL[:, 0:BE]))
                step, a, b = EXPERTS, 0, 1
                while step < BE:
                    link(dve.tensor_copy(sums[b][:, 0:step], sums[a][:, 0:step]))
                    link(dve.tensor_tensor(sums[b][:, step:], sums[a][:, step:], sums[a][:, 0:BE - step], ALU.add))
                    step, a, b = 2 * step, b, a
                count = sums[a][:, BE - EXPERTS:BE]
                link(dve.tensor_scalar(start[:, :], count, float(P - 1), None, ALU.add))
                link(dve.tensor_copy(tiles_i[:, :], start[:, :]))
                link(dve.tensor_scalar(tiles_i[:, :], tiles_i[:, :], 7, None, ALU.arith_shift_right))
                link(dve.tensor_copy(tiles[:, :], tiles_i[:, :]))
                link(dve.tensor_copy(ends[0][:, :], tiles[:, :]))
                step, ea, eb = 1, 0, 1
                while step < EXPERTS:
                    link(dve.tensor_copy(ends[eb][:, 0:step], ends[ea][:, 0:step]))
                    link(dve.tensor_tensor(ends[eb][:, step:], ends[ea][:, step:], ends[ea][:, 0:EXPERTS - step], ALU.add))
                    step, ea, eb = 2 * step, eb, ea
                link(dve.tensor_tensor(start[:, :], ends[ea][:, :], tiles[:, :], ALU.subtract))
                link(dve.tensor_scalar(start[:, :], start[:, :], float(P), None, ALU.mult))
                link(dve.tensor_tensor(sums[a][:, :], sums[a][:, :], TOTAL[:, 0:BE], ALU.subtract))
                link(dve.tensor_tensor(sums[a][:, :], sums[a][:, :], WITHIN[:, 0:BE], ALU.add))
                link(dve.tensor_tensor(grid(sums[a]), grid(sums[a]), per_expert(start), ALU.add))
                link(dve.tensor_tensor(sums[a][:, :], sums[a][:, :], hot[:, :], ALU.mult))
                link(dve.tensor_reduce(top[:, :], grid(sums[a]), AX.X, ALU.add))
                link(dve.tensor_copy(m.slot[:, :], top[:, :]))
                link(dve.tensor_tensor(over[0:1, :].rearrange("p (t e) -> p t e", e=EXPERTS),
                                       m.iota_f[0:1, 0:SORTED].unsqueeze(2).to_broadcast([1, SORTED, EXPERTS]),
                                       ends[ea][0:1, :].unsqueeze(1).to_broadcast([1, SORTED, EXPERTS]), ALU.is_ge))
                link(dve.tensor_reduce(tile_f[:, :], over[0:1, :].rearrange("p (t e) -> p t e", e=EXPERTS), AX.X, ALU.add))
                link(dve.tensor_scalar(tile_f[:, :], tile_f[:, :], float(EXPERTS - 1), None, ALU.min))
                link(dve.tensor_copy(m.tile_expert[:, :], tile_f[:, :]))


def scatter_rows(nc, m, d):
    SLOTS = 5
    ROUNDS = BLOCKS // SLOTS
    assert ROUNDS * SLOTS == BLOCKS
    with ExitStack() as ctx:
        s = sems(nc, m, "scatter", "staged sent")
        y_in = [new_sem(nc, m, f"scatter_in{i}") for i in range(SLOTS)]
        out = [new_sem(nc, m, f"scatter_out{i}") for i in range(SLOTS)]
        Y = ctx.enter_context(nc.sbuf_tensor("scatter_Y", [P, SLOTS, FEAT], F32))
        to = ctx.enter_context(nc.sbuf_tensor("scatter_to", [P, SLOTS], I32))
        with nc.Block() as block:

            @block.sync
            def _(sp):
                def load(n, q):
                    sp.dma_start(Y[:, q, :], d["y_tab"][bass.ds(n * P, P), :]).then_inc(y_in[q], 16)

                for q in range(SLOTS):
                    load(q, q)
                with sp.Fori(0, ROUNDS - 1) as it:
                    for q in range(SLOTS):
                        sp.wait_ge(out[q], it * 16 + 16)
                        hold(sp, m)
                        load(it * SLOTS + (SLOTS + q), q)

            @block.vector
            def _(dve):
                def stage(n, q):
                    dve.tensor_copy(to[:, q:q + 1], m.slot[:, bass.ds(n, 1)]).then_inc(s["staged"], 1)

                for q in range(SLOTS):
                    stage(q, q)
                with dve.Fori(0, ROUNDS - 1) as it:
                    for q in range(SLOTS):
                        dve.wait_ge(out[q], it * 16 + 16)
                        stage(it * SLOTS + (SLOTS + q), q)

            @block.gpsimd
            def _(pool):
                def scatter(q):
                    pool.indirect_dma_start(out=d["y_sorted"][:, :],
                                            out_offset=bass.IndirectOffsetOnAxis(ap=to[:, q:q + 1], axis=0),
                                            in_=Y[:, q, :], in_offset=None).then_inc(out[q], 16)

                with pool.Fori(0, ROUNDS) as it:
                    for q in range(SLOTS):
                        pool.wait_ge(s["staged"], it * SLOTS + (q + 1))
                        pool.wait_ge(y_in[q], it * 16 + 16)
                        hold(pool, m)
                        scatter(q)
                for q in range(SLOTS):
                    pool.wait_ge(out[q], 16 * ROUNDS)


def expert_of_sorted(nc, m, d):
    KC = HID // P
    with ExitStack() as ctx:
        s = sems(nc, m, "exp", "w yT hidden gelu turned made out stored0 stored1 row_free")
        y_in = [new_sem(nc, m, f"exp_y_in{i}") for i in range(2)]
        stored = (s["stored0"], s["stored1"])
        sb = lambda nm, sh, dt: ctx.enter_context(nc.sbuf_tensor(f"exp_{nm}", sh, dt))
        W1 = sb("W1", [P, 2, HID], F32)
        b1 = sb("b1", [P, KC], F32)
        Wd = sb("Wd", [P, KC, EXPERTS * FEAT], F32)
        bd = sb("bd", [1, EXPERTS * FEAT], F32)
        Y = sb("Y", [P, 2, FEAT], F32)
        YT = sb("YT", [P, 2, FEAT], F32)
        HT = sb("HT", [P, 2, HID], F32)
        R = sb("R", [P, 2, FEAT], F32)
        T = [ctx.enter_context(nc.psum_tensor(f"exp_T{i}", [P, 512], F32)) for i in range(2)]
        HB = [ctx.enter_context(nc.psum_tensor(f"exp_HB{i}", [P, 512], F32)) for i in range(2)]
        RB = [ctx.enter_context(nc.psum_tensor(f"exp_RB{i}", [P, 512], F32)) for i in range(2)]
        LOADS = 4 + KC
        LEAD = 4
        with nc.Block() as block:

            @block.sync
            def _(sp):
                for k in range(2):
                    sp.dma_start(W1[:, k, :], d["w1"][k * P:(k + 1) * P, :]).then_inc(s["w"], 16)
                sp.dma_start(b1[:, :], d["b1"][:, :]).then_inc(s["w"], 16)
                sp.dma_start(bd[:, :], d["bd"][:, :]).then_inc(s["w"], 16)
                for k in range(KC):
                    sp.dma_start(Wd[:, k, :], d["wd"][k * P:(k + 1) * P, :]).then_inc(s["w"], 16)

                def body(t, i):
                    n, j = t + 4, (i + 1) % 2
                    if has(n, SORTED):
                        need(sp, s["turned"], n - 1)
                        hold(sp, m)
                        sp.dma_start(Y[:, i, :], d["y_sorted"][bass.ds(n * P, P), :]).then_inc(y_in[i], 16)
                    n = t - 1
                    if has(n, SORTED):
                        sp.wait_ge(s["out"], t)
                        hold(sp, m)
                        sp.dma_start(d["r_tab"][bass.ds(n * P, P), :], R[:, j, :]).then_inc(stored[j], 16)
                    n = t - 2
                    if has(n, SORTED):
                        slot_wait(sp, stored[i], n, 16)
                        sp.sem_inc(s["row_free"], 1)

                pipeline(sp, body, LEAD, 2, SORTED)

            @block.scalar
            def _(act):
                act.wait_ge(s["w"], 16 * LOADS)

                def body(t, i):
                    if has(t, SORTED):
                        need(act, s["made"], t - 1)
                        for c in range(KC):
                            if c % 4 == 0:
                                act.wait_ge(s["hidden"], t * 2 + (c // 4 + 1))
                            act.activation(HT[:, i, c * P:(c + 1) * P], HB[c // 4][:, (c % 4) * P:(c % 4 + 1) * P],
                                           ACT.Gelu, bias=b1[:, c:c + 1]).then_inc(s["gelu"], 1)

                pipeline(act, body, LEAD, 2, SORTED)

            @block.tensor
            def _(pe):
                pe.wait_ge(s["w"], 16 * LOADS)

                def body(t, i):
                    j = (i + 1) % 2
                    if has(t, SORTED):
                        hidden_features(pe, s, YT[:, i, :], W1, HB, s["yT"], t)
                    if has(t - 1, SORTED):
                        e = pe.value_load(m.tile_expert[0:1, bass.ds(t - 1, 1)], min_val=0, max_val=EXPERTS - 1)
                        pe.wait_ge(s["gelu"], t * KC)
                        need(pe, s["out"], t - 2)
                        pe.matmul(RB[j][:, 0:FEAT], m.ones_row[0:1, :], bd[0:1, bass.ds(e * FEAT, FEAT)],
                                  start=True, stop=False)
                        for c in range(KC):
                            mm = pe.matmul(RB[j][:, 0:FEAT], HT[:, j, c * P:(c + 1) * P],
                                           Wd[:, c, bass.ds(e * FEAT, FEAT)], start=False, stop=(c == KC - 1))
                        mm.then_inc(s["made"], 1)
                    n = t + 2
                    if has(n, SORTED):
                        slot_wait(pe, y_in[i], n, 16)
                        need(pe, s["yT"], n - 1)
                        for k in range(2):
                            mm = pe.transpose(T[i][:, k * P:(k + 1) * P], Y[:, i, k * P:(k + 1) * P], m.ident[:, :])
                        mm.then_inc(s["turned"], 1)

                pipeline(pe, body, LEAD, 2, SORTED)

            @block.vector
            def _(dve):
                def body(t, i):
                    j = (i + 1) % 2
                    if has(t - 1, SORTED):
                        dve.wait_ge(s["made"], t)
                        need(dve, s["row_free"], t - 2)
                        dve.tensor_copy(R[:, j, :], RB[j][:, 0:FEAT]).then_inc(s["out"], 1)
                    n = t + 2
                    if has(n, SORTED):
                        dve.wait_ge(s["turned"], n + 1)
                        need(dve, s["hidden"], (n - 1) * 2)
                        dve.tensor_copy(YT[:, i, :], T[i][:, 0:FEAT]).then_inc(s["yT"], 1)

                pipeline(dve, body, LEAD, 2, SORTED)


def project_relations(nc, m, d):
    RH = RELS * HEADS
    COLS = RELS * FEAT + 2 * RH
    with ExitStack() as ctx:
        s = sems(nc, m, "pr", "w a fold folded mm sc_mm h_out sc_out d_out stored0 stored1 rows_free "
                 "staged x2 kept0 kept1 x2_kept link")
        r_in = [new_sem(nc, m, f"pr_r_in{i}") for i in range(2)]
        kept = (s["kept0"], s["kept1"])
        stored = (s["stored0"], s["stored1"])
        sb = lambda nm, sh, dt: ctx.enter_context(nc.sbuf_tensor(f"pr_{nm}", sh, dt))
        f = norm_front(nc, m, ctx, "pr", BLOCKS)
        WX = sb("WX", [P, 2, COLS], F32)
        WN = sb("WN", [P, 2, RELS * FEAT], F32)
        a = sb("a", [P, 4], F32)
        AB = sb("AB", [P, 2, 2 * HEADS], F32)
        R = sb("R", [P, 2, FEAT], F32)
        row_of = sb("row_of", [P, 2], I32)
        H = sb("H", [P, 2, RELS * FEAT], F32)
        SC = sb("SC", [P, 2, RH], F32)
        HP = [ctx.enter_context(nc.psum_tensor(f"pr_H{i}", [P, 512], F32)) for i in range(4)]
        SP_ = [ctx.enter_context(nc.psum_tensor(f"pr_S{i}", [P, 512], F32)) for i in range(2)]
        fold = lambda h, r: SP_[h][:, r * 2 * HEADS:(r + 1) * 2 * HEADS]
        h_rows = d["h_tab"].rearrange("(n r) c -> n (r c)", r=RELS)
        s_rows = d["s_tab"].rearrange("(n r) c -> n (r c)", r=RELS)
        node = lambda t: m.node[:, bass.ds(t * NUMC, FEAT)]
        LEAD = 7
        with nc.Block() as block:

            @block.sync
            def _(sp):
                for k in range(2):
                    sp.dma_start(WX[:, k, 0:RELS * FEAT], d["wr_t"][k * P:(k + 1) * P, :]).then_inc(s["w"], 16)
                    sp.dma_start(WN[:, k, :], d["wr_n"][k * P:(k + 1) * P, :]).then_inc(s["w"], 16)
                sp.dma_start(a[:, :], d["att"][:, :]).then_inc(s["a"], 16)

                def body(t, i):
                    n, j = t + 3, (i + 1) % 2
                    if has(n, BLOCKS):
                        sp.wait_ge(s["x2"], n + 1)
                        hold(sp, m)
                        sp.dma_start(d["x2"][bass.ds(n * P, P), :], node(n)).then_inc(kept[j], 16)
                    if has(t + 2, BLOCKS):
                        slot_wait(sp, kept[i], t + 2, 16)
                        sp.sem_inc(s["x2_kept"], 1)
                    if has(t, BLOCKS):
                        sp.wait_ge(s["sc_out"], t + 1)
                        sp.wait_ge(s["h_out"], t * 4 + 4)
                        hold(sp, m)
                        sp.dma_start(s_rows[bass.ds(t * P, P), :], SC[:, i, :]).then_inc(stored[i], 16)
                        sp.dma_start(h_rows[bass.ds(t * P, P), :], H[:, i, :]).then_inc(stored[i], 16)
                    n, j = t - 1, (i + 1) % 2
                    if has(n, BLOCKS):
                        slot_wait(sp, stored[j], n, 32)
                        sp.sem_inc(s["rows_free"], 1)

                pipeline(sp, body, LEAD, 1, BLOCKS)

            @block.gpsimd
            def _(pool):
                def body(t, i):
                    n = t + 6
                    if has(n, BLOCKS):
                        pool.wait_ge(s["staged"], n + 1)
                        need(pool, s["x2"], n - 1)
                        hold(pool, m)
                        pool.indirect_dma_start(out=R[:, i, :], out_offset=None, in_=d["r_tab"][:, :],
                                                in_offset=bass.IndirectOffsetOnAxis(ap=row_of[:, i:i + 1], axis=0)
                                                ).then_inc(r_in[i], 16)
                    front_scale(pool, m, f, t + 4, i)

                pipeline(pool, body, LEAD, 1, BLOCKS)

            @block.scalar
            def _(act):
                def body(t, i):
                    if has(t, BLOCKS):
                        need(act, s["rows_free"], t - 1)
                        for g in range(4):
                            act.wait_ge(s["mm"], t * 4 + (g + 1))
                            act.copy(H[:, i, g * 512:(g + 1) * 512], HP[g][:, :]).then_inc(s["h_out"], 1)
                    front_copy(act, act.copy, f, t + 2, i, s["mm"], 4)

                pipeline(act, body, LEAD, 1, BLOCKS)

            @block.vector
            def _(dve):
                link = Link(dve, s["link"])
                dve.wait_ge(s["a"], 16)
                for k in range(2):
                    for j in range(2):
                        link(dve.tensor_scalar(AB[:, k, j * HEADS:(j + 1) * HEADS], m.hmask[:, k * HEADS:(k + 1) * HEADS],
                                               a[:, 2 * j + k:2 * j + k + 1], None, ALU.mult))
                dve.wait_ge(s["fold"], 2)
                for h in range(2):
                    for j in range(2):
                        at = RELS * FEAT + j * RH
                        dve.tensor_copy(WX[:, h, at:at + RH].rearrange("p (r h) -> p r h", h=HEADS),
                                        SP_[h][:, 0:2 * RH].rearrange("p (r h) -> p r h", h=2 * HEADS)[
                                            :, :, j * HEADS:(j + 1) * HEADS]).then_inc(s["folded"], 1)

                def body(t, i):
                    j = (i + 1) % 2
                    if has(t + 3, BLOCKS):
                        front_norm(dve, f, node(t + 3), t + 3, j)
                    if has(t + 4, BLOCKS):
                        dve.wait_ge(s["x2"], t + 5)
                        hold(dve, m)
                        front_stats(dve, m, f, node(t + 4), t + 4, i)
                    n = t + 5
                    if has(n, BLOCKS):
                        slot_wait(dve, r_in[j], n, 16)
                        dve.scalar_tensor_tensor(node(n), R[:, j, :], m.prob[:, bass.ds(n, 1)], node(n), ALU.mult,
                                                 ALU.add).then_inc(s["x2"], 1)
                    n = t + 7
                    if has(n, BLOCKS):
                        if has(n - 2, BLOCKS):
                            slot_wait(dve, r_in[j], n - 2, 16)
                        dve.tensor_copy(row_of[:, j:j + 1], m.slot[:, bass.ds(n, 1)]).then_inc(s["staged"], 1)
                    if has(t, BLOCKS):
                        dve.wait_ge(s["sc_mm"], t + 1)
                        need(dve, s["rows_free"], t - 1)
                        dve.tensor_copy(SC[:, i, :], SP_[i][:, 0:RH]).then_inc(s["sc_out"], 1)
                        dve.wait_ge(s["x2_kept"], t + 1)
                        dve.tensor_copy(m.node[:, bass.ds(t * RH, RH)], SP_[i][:, RH:2 * RH]).then_inc(s["d_out"], 1)

                pipeline(dve, body, LEAD, 1, BLOCKS)

            @block.tensor
            def _(pe):
                pe.wait_ge(s["w"], 64)
                pe.wait_ge(s["link"], 4)
                for h in range(2):
                    for r in range(RELS):
                        for k in range(2):
                            mm = pe.matmul(fold(h, r), WN[:, k, r * FEAT + h * P:r * FEAT + (h + 1) * P], AB[:, k, :],
                                           start=(k == 0), stop=(k == 1))
                    mm.then_inc(s["fold"], 1)
                pe.wait_ge(s["folded"], 4)

                def body(t, i):
                    if has(t, BLOCKS):
                        pe.wait_ge(f.s["yT"], t + 1)
                        need(pe, s["sc_out"], t - 1)
                        need(pe, s["d_out"], t - 1)
                        for k in range(2):
                            mm = pe.matmul(SP_[i][:, 0:2 * RH], f.YT[:, i, k * P:(k + 1) * P], WX[:, k, RELS * FEAT:],
                                           start=(k == 0), stop=(k == 1))
                        mm.then_inc(s["sc_mm"], 1)
                        for g in range(4):
                            need(pe, s["h_out"], t * 4 + (g - 3))
                            for k in range(2):
                                mm = pe.matmul(HP[g][:, :], f.YT[:, i, k * P:(k + 1) * P], WX[:, k, g * 512:(g + 1) * 512],
                                               start=(k == 0), stop=(k == 1))
                            mm.then_inc(s["mm"], 1)
                    front_turn(pe, m, f, t + 2, i)

                pipeline(pe, body, LEAD, 1, BLOCKS)


def feed_forward_top2(nc, m, d):
    PAIRS = EXPERTS // 2
    CH = 2 * EXPERTS
    ROUTE, MIX, SUMS = 16, EXPERTS + 1, 3
    with ExitStack() as ctx:
        s = sems(nc, m, "moe", "w summed x3 based logits route powed c_turned cT bias_out hidden gelu experts mixed stored")
        x_in = [new_sem(nc, m, f"moe_x_in{i}") for i in range(2)]
        sb = lambda nm, sh, dt: ctx.enter_context(nc.sbuf_tensor(f"moe_{nm}", sh, dt))
        f = norm_front(nc, m, ctx, "moe", BLOCKS, banks=1)
        Wr = sb("Wr", [P, 2, EXPERTS], F32)
        W1 = sb("W1", [P, 2, EXPERTS * FEAT], F32)
        b1 = sb("b1", [P, CH], F32)
        W2 = sb("W2", [P, 2, EXPERTS * FEAT], F32)
        b2 = sb("b2", [EXPERTS, FEAT], F32)
        X = sb("X", [P, 2, FEAT], F32)
        HT = sb("HT", [P, CH, P], F32)
        r = sb("r", [P, HEADS], F32)
        L = sb("L", [P, EXPERTS], F32)
        best = sb("best", [P, 8], F32)
        idx = sb("idx", [P, 8], U32)
        idx_f = sb("idx_f", [P, 8], F32)
        ex = sb("ex", [P, EXPERTS], F32)
        p = sb("p", [P, 4], F32)
        C = sb("C", [P, 2, EXPERTS], F32)
        C2 = sb("C2", [P, EXPERTS], F32)
        CT = sb("CT", [EXPERTS, P], F32)
        SMALL = ctx.enter_context(nc.psum_tensor("moe_SMALL", [P, 512], F32))
        bias_out, logits, c_turned = SMALL[:, 0:FEAT], SMALL[:, FEAT:FEAT + EXPERTS], SMALL[0:EXPERTS, 384:384 + P]
        HB = [ctx.enter_context(nc.psum_tensor(f"moe_HB{i}", [P, 512], F32)) for i in range(2)]
        YE = [ctx.enter_context(nc.psum_tensor(f"moe_YE{i}", [P, 512], F32)) for i in range(PAIRS)]
        node = lambda t, a=0, b=FEAT: m.node[:, bass.ds(t * NUMC + a, b - a)]
        LOADS = 8
        LEAD = 7
        with nc.Block() as block:

            @block.sync
            def _(sp):
                for k in range(2):
                    sp.dma_start(Wr[:, k, :], d["router"][k * P:(k + 1) * P, :]).then_inc(s["w"], 16)
                    sp.dma_start(W1[:, k, :], d["m1"][k * P:(k + 1) * P, :]).then_inc(s["w"], 16)
                    sp.dma_start(W2[:, k, :], d["m2"][k * P:(k + 1) * P, :]).then_inc(s["w"], 16)
                sp.dma_start(b1[:, :], d["mb1"][:, :]).then_inc(s["w"], 16)
                sp.dma_start(b2[:, :], d["mb2"][:, :]).then_inc(s["w"], 16)

                def body(t, i):
                    n, j = t + 7, (i + 1) % 2
                    if has(n, BLOCKS):
                        need(sp, s["x3"], n - 1)
                        hold(sp, m)
                        sp.dma_start(X[:, j, :], d["x2"][bass.ds(n * P, P), :]).then_inc(x_in[j], 16)
                    n = t - 1
                    if has(n, BLOCKS):
                        sp.wait_ge(s["mixed"], t * MIX)
                        hold(sp, m)
                        sp.dma_start(d["out"][bass.ds(n * P, P), :], node(n)).then_inc(s["stored"], 16)

                pipeline(sp, body, LEAD, 1, BLOCKS)
                sp.wait_ge(s["stored"], 16 * BLOCKS)

            @block.gpsimd
            def _(pool):
                def body(t, i):
                    n = t + 1
                    if has(n, BLOCKS):
                        pool.wait_ge(s["route"], n * ROUTE + 3)
                        pool.tensor_tensor(ex[:, :], m.e_const[:, :], L[:, :], ALU.pow).then_inc(s["powed"], 1)
                    front_scale(pool, m, f, t + 4, i)

                pipeline(pool, body, LEAD, 1, BLOCKS)

            @block.scalar
            def _(act):
                act.wait_ge(s["w"], 16 * LOADS)

                def body(t, i):
                    if has(t, BLOCKS):
                        for c in range(CH):
                            g = c // 4
                            if c % 4 == 0:
                                act.wait_ge(s["hidden"], t * PAIRS + (g + 1))
                                need(act, s["experts"], t * PAIRS + (g + 1 - PAIRS))
                            act.activation(HT[:, c, :], HB[g % 2][:, (c % 4) * P:(c % 4 + 1) * P], ACT.Gelu,
                                           bias=b1[:, c:c + 1]).then_inc(s["gelu"], 1)

                pipeline(act, body, LEAD, 1, BLOCKS)

            @block.tensor
            def _(pe):
                pe.wait_ge(s["w"], 16 * LOADS)

                def hidden(t, i, g):
                    if has(t, BLOCKS):
                        if g == 0:
                            pe.wait_ge(f.s["yT"], t + 1)
                        need(pe, s["gelu"], t * CH + (4 * g - 4))
                        for c in range(4 * g, 4 * g + 4):
                            for k in range(2):
                                mm = pe.matmul(HB[g % 2][:, (c % 4) * P:(c % 4 + 1) * P], W1[:, k, c * P:(c + 1) * P],
                                               f.YT[:, i, k * P:(k + 1) * P], start=(k == 0), stop=(k == 1))
                        mm.then_inc(s["hidden"], 1)

                def expert_pair(t, g):
                    if has(t, BLOCKS):
                        pe.wait_ge(s["gelu"], t * CH + (4 * g + 4))
                        need(pe, s["mixed"], t * MIX + (2 * g + 2 - MIX))
                        for e in (2 * g, 2 * g + 1):
                            for k in range(2):
                                mm = pe.matmul(YE[g][:, (e % 2) * FEAT:(e % 2 + 1) * FEAT], HT[:, 2 * e + k, :],
                                               W2[:, k, e * FEAT:(e + 1) * FEAT], start=(k == 0), stop=(k == 1))
                        mm.then_inc(s["experts"], 1)

                def body(t, i):
                    hidden(t, i, 0)
                    expert_pair(t - 1, PAIRS - 1)
                    front_turn(pe, m, f, t + 2, i)
                    hidden(t, i, 1)
                    if has(t, BLOCKS):
                        pe.wait_ge(s["route"], t * ROUTE + ROUTE)
                        need(pe, s["mixed"], t * MIX)
                        pe.transpose(c_turned, C[:, i, :], m.ident[:, :]).then_inc(s["c_turned"], 1)
                    expert_pair(t, 0)
                    n, j = t + 1, (i + 1) % 2
                    if has(n, BLOCKS):
                        pe.wait_ge(f.s["yT"], n + 1)
                        need(pe, s["cT"], n)
                        for k in range(2):
                            mm = pe.matmul(logits, f.YT[:, j, k * P:(k + 1) * P], Wr[:, k, :], start=(k == 0), stop=(k == 1))
                        mm.then_inc(s["logits"], 1)
                    hidden(t, i, 2)
                    expert_pair(t, 1)
                    if has(t, BLOCKS):
                        pe.wait_ge(s["cT"], t + 1)
                        if has(t + 1, BLOCKS):
                            pe.wait_ge(s["route"], (t + 1) * ROUTE + 1)
                        pe.matmul(bias_out, CT[:, :], b2[:, :], start=True, stop=True).then_inc(s["bias_out"], 1)
                    hidden(t, i, 3)
                    expert_pair(t, 2)

                pipeline(pe, body, LEAD, 1, BLOCKS)

            @block.vector
            def _(dve):
                dve.wait_ge(s["w"], 16 * LOADS)

                def mix_pair(t, i, g):
                    if has(t, BLOCKS):
                        link = LoopLink(dve, s["mixed"], t, MIX)
                        link.n = 2 * g
                        dve.wait_ge(s["experts"], t * PAIRS + (g + 1))
                        for e in (2 * g, 2 * g + 1):
                            link(dve.scalar_tensor_tensor(node(t), YE[g][:, (e % 2) * FEAT:(e % 2 + 1) * FEAT],
                                                          C[:, i, e:e + 1], node(t), ALU.mult, ALU.add))

                def route(n, j):
                    link = LoopLink(dve, s["route"], n, ROUTE)
                    dve.wait_ge(s["logits"], n + 1)
                    link(dve.tensor_copy(L[:, :], logits))
                    link(dve.tensor_reduce(p[:, 0:1], L[:, :], AX.X, ALU.max))
                    link(dve.tensor_scalar(L[:, :], L[:, :], p[:, 0:1], None, ALU.subtract))
                    dve.wait_ge(s["powed"], n + 1)
                    link(dve.tensor_reduce(p[:, 1:2], ex[:, :], AX.X, ALU.add))
                    link(dve.reciprocal(p[:, 1:2], p[:, 1:2]))
                    link(dve.tensor_scalar(ex[:, :], ex[:, :], p[:, 1:2], None, ALU.mult))
                    top_experts(dve, m, ex[:, :], best[:, :], idx[:, :], idx_f[:, :], link)
                    link(dve.tensor_tensor(p[:, 2:3], best[:, 0:1], best[:, 1:2], ALU.add))
                    link(dve.tensor_scalar(p[:, 2:3], p[:, 2:3], 1e-12, None, ALU.max))
                    link(dve.reciprocal(p[:, 3:4], p[:, 2:3]))
                    link(dve.tensor_scalar(C[:, j, :], m.iota_f[:, 0:EXPERTS], idx_f[:, 0:1], best[:, 0:1], ALU.is_equal, ALU.mult))
                    link(dve.tensor_scalar(C2[:, :], m.iota_f[:, 0:EXPERTS], idx_f[:, 1:2], best[:, 1:2], ALU.is_equal, ALU.mult))
                    link(dve.tensor_tensor(C[:, j, :], C[:, j, :], C2[:, :], ALU.add))
                    link(dve.tensor_scalar(C[:, j, :], C[:, j, :], p[:, 3:4], None, ALU.mult))
                    assert link.n == ROUTE

                def body(t, i):
                    j = (i + 1) % 2
                    n = t - 1
                    mix_pair(n, j, PAIRS - 1)
                    if has(n, BLOCKS):
                        dve.wait_ge(s["bias_out"], t)
                        link = LoopLink(dve, s["mixed"], n, MIX)
                        link.n = EXPERTS
                        link(dve.tensor_tensor(node(n), node(n), bias_out, ALU.add))
                    n = t + 3
                    if has(n, BLOCKS):
                        front_norm(dve, f, node(n), n, j)
                        dve.wait_ge(f.s["normed"], n + 1)
                        dve.tensor_tensor(node(n), node(n), f.Y[:, j, :], ALU.add).then_inc(s["based"], 1)
                    mix_pair(t, i, 0)
                    if has(t, BLOCKS):
                        dve.wait_ge(s["c_turned"], t + 1)
                        dve.tensor_copy(CT[:, :], c_turned).then_inc(s["cT"], 1)
                    if has(t + 1, BLOCKS):
                        route(t + 1, j)
                    mix_pair(t, i, 1)
                    n = t + 5
                    if has(n, BLOCKS):
                        link = LoopLink(dve, s["summed"], n, SUMS)
                        link(dve.tensor_scalar(r[:, :], node(n, FEAT, NUMC), 1e-12, None, ALU.add))
                        link(dve.reciprocal(r[:, :], r[:, :]))
                        heads = node(n).rearrange("p (h c) -> p h c", c=DH)
                        link(dve.tensor_tensor(heads, heads, r[:, :].unsqueeze(2).to_broadcast([P, HEADS, DH]), ALU.mult))
                        slot_wait(dve, x_in[j], n, 16)
                        dve.tensor_tensor(node(n), node(n), X[:, j, :], ALU.add).then_inc(s["x3"], 1)
                    n = t + 4
                    if has(n, BLOCKS):
                        dve.wait_ge(s["x3"], n + 1)
                        hold(dve, m)
                        front_stats(dve, m, f, node(n), n, i)
                    front_copy(dve, dve.tensor_copy, f, t + 2, i, s["hidden"], PAIRS)
                    mix_pair(t, i, 2)

                pipeline(dve, body, LEAD, 1, BLOCKS)


def program(nc, d):
    with ExitStack() as ctx:
        m = Shared()
        shared(nc, ctx, m)
        constants(nc, m)
        end_phase(nc, m)
        merge_path(nc, m, d)
        end_phase(nc, m)
        segment_starts(nc, m, d)
        end_phase(nc, m)
        m.node = ctx.enter_context(nc.sbuf_tensor("node", [P, BLOCKS * NUMC], F32))
        with ExitStack() as layer:
            S = layer.enter_context(nc.sbuf_tensor("S0", [P, SPAD * HEADS], F32))
            edge_bias(nc, m, d, S)
            end_phase(nc, m)
            project_attention(nc, m, d)
            end_phase(nc, m)
            scores_attention(nc, m, d, S)
            end_phase(nc, m)
            segment_softmax(nc, m, S, -1e38, "seg0")
            end_phase(nc, m)
            aggregate(nc, m, S, d["v_tab"], m.idx_src, "attn")
            end_phase(nc, m)
        with ExitStack() as routes:
            sb = lambda nm, sh, dt: routes.enter_context(nc.sbuf_tensor(nm, sh, dt))
            m.logits = sb("logits", [P, BLOCKS * EXPERTS], F32)
            m.prob = sb("prob", [P, BLOCKS], F32)
            m.slot = sb("slot", [P, BLOCKS], I32)
            m.tile_expert = sb("tile_expert", [1, SORTED], I32)
            attend_and_route(nc, m, d)
            end_phase(nc, m)
            sort_by_expert(nc, m, d)
            end_phase(nc, m)
            scatter_rows(nc, m, d)
            end_phase(nc, m)
            expert_of_sorted(nc, m, d)
            end_phase(nc, m)
            project_relations(nc, m, d)
            end_phase(nc, m)
        with ExitStack() as layer:
            S = layer.enter_context(nc.sbuf_tensor("S1", [P, SPAD * HEADS], F32))
            scores_relational(nc, m, d, S)
            end_phase(nc, m)
            segment_softmax(nc, m, S, 0.0, "seg1")
            end_phase(nc, m)
            aggregate(nc, m, S, d["h_tab"], m.idx_rel, "relagg")
            end_phase(nc, m)
        feed_forward_top2(nc, m, d)


def by_partition(w):
    return w.reshape(-1, P, w.shape[-1]).transpose(1, 0, 2).reshape(P, -1)


LAYOUT = {
    "wqkv": lambda g: stacked([g["L0_gnn_Wq"].T, g["L0_gnn_Wk"].T, g["L0_gnn_Wv"].T]),
    "wo": lambda g: g["L0_gnn_Wo"].T,
    "w1": lambda g: g["L0_ffn_W1"],
    "b1": lambda g: g["L0_ffn_b1"].reshape(HID // P, P).T,
    "wg": lambda g: by_partition(g["L0_ffn_Wg"]),
    "bg": lambda g: g["L0_ffn_bg"].reshape(1, -1),
    "wd": lambda g: g["L0_ffn_Wd"].transpose(1, 0, 2).reshape(HID, EXPERTS * FEAT),
    "bd": lambda g: g["L0_ffn_bd"].reshape(1, -1),
    "wr_t": lambda g: g["L1_gnn_W"].transpose(2, 0, 1).reshape(FEAT, RELS * FEAT),
    "wr_n": lambda g: g["L1_gnn_W"].transpose(1, 0, 2).reshape(FEAT, RELS * FEAT),
    "att": lambda g: stacked([g["L1_gnn_attn_src"].reshape(2, P).T, g["L1_gnn_attn_dst"].reshape(2, P).T]),
    "router": lambda g: g["L1_ffn_router_w"].T,
    "m1": lambda g: g["L1_ffn_w1"].transpose(1, 0, 2).reshape(FEAT, EXPERTS * FEAT),
    "mb1": lambda g: g["L1_ffn_b1"].reshape(EXPERTS * 2, P).T,
    "m2": lambda g: g["L1_ffn_w2"].transpose(1, 0, 2).reshape(FEAT, EXPERTS * FEAT),
    "mb2": lambda g: g["L1_ffn_b2"],
}


def stacked(parts):
    import numpy as _np
    return _np.concatenate(parts, axis=1)


SCRATCH = {
    "jf": ((SGROUPS, P), F32),
    "ji": ((SGROUPS, P), I32),
    "jp": ((SGROUPS, P // 4), I32),
    "dst_steps": ((1, (CHUNKS + 1) * CLEN), I32),
    "k_tab": ((NPAD, FEAT), F32),
    "v_tab": ((NPAD, FEAT), F32),
    "x2": ((NPAD, FEAT), F32),
    "y_tab": ((NPAD, FEAT), F32),
    "y_sorted": ((SORTED * P, FEAT), F32),
    "r_tab": ((SORTED * P, FEAT), F32),
    "h_tab": ((NPAD * RELS, FEAT), F32),
    "s_tab": ((NPAD * RELS, HEADS), F32),
}
OUTS = {"out": ((NPAD, FEAT), F32)}


def kernel(**inputs):
    import numpy as _np
    import concourse.bacc as _bacc
    from concourse import mybir as _mybir
    from concourse.bass_utils import run_bass_kernel_spmd as _run

    def rows(a, n, fill=0):
        out = _np.full((n,) + a.shape[1:], fill, a.dtype)
        out[:a.shape[0]] = a
        return out

    g = {k: _np.asarray(v) for k, v in inputs.items()}
    arrays = {
        "x": rows(g["x"], NPAD),
        "src": rows(g["src"], TROWS * P).reshape(TROWS, P),
        "dst": rows(g["dst"], TROWS * P, PAD_NODE).reshape(TROWS, P),
        "typ": rows(g["edge_type_8"], TROWS * P).reshape(TROWS, P),
        "attr": rows(g["edge_attr_8"], TROWS * P).reshape(TROWS, P * HEADS),
    }
    for k, v in LAYOUT.items():
        arrays[k] = _np.ascontiguousarray(v(g))
    nc = _bacc.Bacc("TRN2", target_bir_lowering=False, num_devices=1)
    dram = {k: nc.dram_tensor(f"in_{k}", a.shape, _mybir.dt.from_np(a.dtype), kind="ExternalInput").ap()
            for k, a in arrays.items()}
    for k, (shape, dt) in SCRATCH.items():
        dram[k] = nc.dram_tensor(k, shape, dt, kind="Internal").ap()
    for k, (shape, dt) in OUTS.items():
        dram[k] = nc.dram_tensor(k, shape, dt, kind="ExternalOutput").ap()
    program(nc, dram)
    r = _run(nc, [{f"in_{k}": a for k, a in arrays.items()}], core_ids=[0])
    return r.results[0]["out"][:N]
```
